# Optimizing a Trainium2 kernel written in Bass

```python
import numpy as np
import jax
import jax.numpy as jnp

def _softmax(x, axis=-1):
    return jax.nn.softmax(x, axis=axis)

def _gelu(x):
    return jax.nn.gelu(x, approximate=True)

def _silu(x):
    return jax.nn.silu(x)

def _sigmoid(x):
    return jax.nn.sigmoid(x)

def _layernorm(x, axis=-1, eps=1e-05):
    m = jnp.mean(x, axis=axis, keepdims=True)
    v = jnp.var(x, axis=axis, keepdims=True)
    return (x - m) / jnp.sqrt(v + eps)

def _scatter_add(tgt, idx, src, axis=0):
    return tgt.at[idx].add(src)

def _segment_sum(src, seg, n):
    return jax.ops.segment_sum(src, seg, n)
kernel_name = 'mk_gps_d1_gnn_r8_c8af1e'

def setup_inputs(seed: int=0):
    np.random.seed(seed)
    _w = jnp.asarray

    def _rec_inputs():
        import jax
        import jax.numpy as jnp
        _gk = jax.random.key(seed)
        x = -0.000125 + 0.9999 * jax.random.normal(jax.random.fold_in(_gk, 1), (8192, 512), jnp.float32)
        src = jax.random.randint(jax.random.fold_in(_gk, 2), (131072,), 0, 8192, jnp.int32)
        dst = jnp.minimum((8192 * jax.random.uniform(jax.random.fold_in(_gk, 3), (131072,)) ** 2.0).astype(jnp.int32), 65535)
        _o = jnp.argsort(dst, stable=True)
        src = src[_o]
        dst = dst[_o]
        edge_weight = jax.random.uniform(jax.random.fold_in(_gk, 12), (131072,), jnp.float32, 0.0, 0.999998)
        return (x, src, dst, edge_weight)
    x, src, dst, edge_weight = _rec_inputs()

    def _L0_gnn_setup():
        import jax, jax.numpy as jnp
        import numpy as np
        N_NODES = 8192
        N_EDGES = 65536
        FEAT_DIM = 512
        EMBED_DIM = 512
        key = jax.random.key(seed)
        k1, k2, k3, k4, k5 = jax.random.split(key, 5)
        x = jax.random.normal(k1, (N_NODES, FEAT_DIM), dtype=jnp.float32)
        limit = float(np.sqrt(6.0 / (EMBED_DIM + FEAT_DIM)))
        weight = jax.random.uniform(k2, (EMBED_DIM, FEAT_DIM), dtype=jnp.float32, minval=-limit, maxval=limit)
        row = jax.random.randint(k3, (N_EDGES,), 0, N_NODES, dtype=jnp.int64)
        col = jax.random.randint(k4, (N_EDGES,), 0, N_NODES, dtype=jnp.int64)
        vals = jax.random.uniform(k5, (N_EDGES,), dtype=jnp.float32)
        return {'x': x, 'weight': weight, 'row': row, 'col': col, 'vals': vals}
    _L0_gnn_all = _L0_gnn_setup()
    _L0_gnn_in = {k: v for k, v in _L0_gnn_all.items() if k in ('weight',)}
    del _L0_gnn_all

    def _L0_mix_setup():
        import jax, jax.numpy as jnp
        import numpy as np
        import math
        B, N, DIM = (4, 512, 512)
        HEADS, DH, NBF = (8, 64, 256)
        MLP_H = DIM * 2

        def layernorm(x, g, b, eps=1e-05):
            mu = jnp.mean(x, axis=-1, keepdims=True)
            var = jnp.mean(jnp.square(x - mu), axis=-1, keepdims=True)
            return (x - mu) * jax.lax.rsqrt(var + eps) * g + b

        def softmax_kernel(x, pmat):
            xp = jnp.einsum('bhnd,df->bhnf', x, pmat)
            xp = xp - jnp.max(xp, axis=-1, keepdims=True)
            return jnp.exp(xp) / math.sqrt(pmat.shape[-1])
        key = jax.random.key(seed)
        ks = jax.random.split(key, 8)
        s = lambda d: 1.0 / math.sqrt(d)
        return {'x': jax.random.normal(ks[0], (B, N, DIM), jnp.float32), 'Wqkv': jax.random.normal(ks[1], (DIM, 3 * HEADS * DH), jnp.float32) * s(DIM), 'bqkv': jnp.zeros((3 * HEADS * DH,), jnp.float32), 'Pmat': jax.random.normal(ks[2], (DH, NBF), jnp.float32), 'Wproj': jax.random.normal(ks[3], (HEADS * DH, DIM), jnp.float32) * s(HEADS * DH), 'bproj': jnp.zeros((DIM,), jnp.float32), 'W1': jax.random.normal(ks[4], (DIM, MLP_H), jnp.float32) * s(DIM), 'b1': jnp.zeros((MLP_H,), jnp.float32), 'W2': jax.random.normal(ks[5], (MLP_H, DIM), jnp.float32) * s(MLP_H), 'b2': jnp.zeros((DIM,), jnp.float32), 'g1': jnp.ones((DIM,), jnp.float32), 'be1': jnp.zeros((DIM,), jnp.float32), 'g2': jnp.ones((DIM,), jnp.float32), 'be2': jnp.zeros((DIM,), jnp.float32)}
    _L0_mix_all = _L0_mix_setup()
    _L0_mix_in = {k: v for k, v in _L0_mix_all.items() if k in ('Wqkv', 'bqkv', 'Pmat', 'Wproj', 'bproj', 'W1', 'b1', 'W2', 'b2', 'g1', 'be1', 'g2', 'be2')}
    del _L0_mix_all

    def _L0_ffn_setup():
        import jax, jax.numpy as jnp
        import numpy as np
        T = 512
        B = 64
        C = 1024

        def _triu_apply(x, W, b):
            Wm = jnp.tril(W)
            return jnp.einsum('bct,st->bcs', x, Wm) + b
        key = jax.random.key(seed)
        ks = jax.random.split(key, 5)
        x = jax.random.normal(ks[0], (B, C, T), dtype=jnp.float32)
        scale = 1.0 / jnp.sqrt(jnp.arange(1, T + 1, dtype=jnp.float32))[:, None]
        W1 = jax.random.uniform(ks[1], (T, T), jnp.float32, -1.0, 1.0) * scale
        b1 = jax.random.uniform(ks[2], (T,), jnp.float32, -1.0, 1.0) * scale[:, 0]
        W2 = jax.random.uniform(ks[3], (T, T), jnp.float32, -1.0, 1.0) * scale
        b2 = jax.random.uniform(ks[4], (T,), jnp.float32, -1.0, 1.0) * scale[:, 0]
        return {'x': x, 'W1': W1, 'b1': b1, 'W2': W2, 'b2': b2}
    _L0_ffn_all = _L0_ffn_setup()
    _L0_ffn_in = {k: v for k, v in _L0_ffn_all.items() if k in ('W1', 'b1', 'W2', 'b2')}
    del _L0_ffn_all
    return {'x': x, 'src': src, 'dst': dst, 'edge_weight': edge_weight, 'L0_gnn_weight': _L0_gnn_in['weight'], 'L0_mix_Wqkv': _L0_mix_in['Wqkv'], 'L0_mix_bqkv': _L0_mix_in['bqkv'], 'L0_mix_Pmat': _L0_mix_in['Pmat'], 'L0_mix_Wproj': _L0_mix_in['Wproj'], 'L0_mix_bproj': _L0_mix_in['bproj'], 'L0_mix_W1': _L0_mix_in['W1'], 'L0_mix_b1': _L0_mix_in['b1'], 'L0_mix_W2': _L0_mix_in['W2'], 'L0_mix_b2': _L0_mix_in['b2'], 'L0_mix_g1': _L0_mix_in['g1'], 'L0_mix_be1': _L0_mix_in['be1'], 'L0_mix_g2': _L0_mix_in['g2'], 'L0_mix_be2': _L0_mix_in['be2'], 'L0_ffn_W1': _L0_ffn_in['W1'], 'L0_ffn_b1': _L0_ffn_in['b1'], 'L0_ffn_W2': _L0_ffn_in['W2'], 'L0_ffn_b2': _L0_ffn_in['b2']}

def reference(x, src, dst, edge_weight, L0_gnn_weight, L0_mix_Wqkv, L0_mix_bqkv, L0_mix_Pmat, L0_mix_Wproj, L0_mix_bproj, L0_mix_W1, L0_mix_b1, L0_mix_W2, L0_mix_b2, L0_mix_g1, L0_mix_be1, L0_mix_g2, L0_mix_be2, L0_ffn_W1, L0_ffn_b1, L0_ffn_W2, L0_ffn_b2):
    import jax
    import jax.numpy as jnp

    def _L0_gnn_ref(x, weight, row, col, vals):
        import jax, jax.numpy as jnp
        import numpy as np
        N_NODES = 8192
        N_EDGES = 65536
        FEAT_DIM = 512
        EMBED_DIM = 512
        h = jnp.einsum('nf,ef->ne', x, weight)
        msgs = vals[:, None] * h[col]
        out = jax.ops.segment_sum(msgs, row, num_segments=N_NODES)
        return out

    def _L0_mix_ref(x, Wqkv, bqkv, Pmat, Wproj, bproj, W1, b1, W2, b2, g1, be1, g2, be2):
        import jax, jax.numpy as jnp
        import numpy as np
        import math
        B, N, DIM = (4, 512, 512)
        HEADS, DH, NBF = (8, 64, 256)
        MLP_H = DIM * 2

        def layernorm(x, g, b, eps=1e-05):
            mu = jnp.mean(x, axis=-1, keepdims=True)
            var = jnp.mean(jnp.square(x - mu), axis=-1, keepdims=True)
            return (x - mu) * jax.lax.rsqrt(var + eps) * g + b

        def softmax_kernel(x, pmat):
            xp = jnp.einsum('bhnd,df->bhnf', x, pmat)
            xp = xp - jnp.max(xp, axis=-1, keepdims=True)
            return jnp.exp(xp) / math.sqrt(pmat.shape[-1])
        b, n, d = x.shape
        h = layernorm(x, g1, be1)
        qkv = h @ Wqkv + bqkv
        q, k, v = jnp.split(qkv, 3, axis=-1)
        to_heads = lambda t: t.reshape(b, n, HEADS, DH).transpose(0, 2, 1, 3)
        q, k, v = (to_heads(q), to_heads(k), to_heads(v))
        q_prime = softmax_kernel(q, Pmat)
        k_prime = softmax_kernel(k, Pmat)
        kv = jnp.einsum('bhnf,bhne->bhfe', k_prime, v)
        k_sum = jnp.sum(k_prime, axis=2) + 1e-06
        z = 1.0 / jnp.einsum('bhnf,bhf->bhn', q_prime, k_sum)[..., None]
        attn = jnp.einsum('bhnf,bhfe->bhne', q_prime, kv) * z
        attn = attn.transpose(0, 2, 1, 3).reshape(b, n, HEADS * DH)
        x = x + attn @ Wproj + bproj
        h2 = layernorm(x, g2, be2)
        mlp = jax.nn.gelu(h2 @ W1 + b1, approximate=False) @ W2 + b2
        return x + mlp

    def _L0_ffn_ref(x, W1, b1, W2, b2):
        import jax, jax.numpy as jnp
        import numpy as np
        T = 512
        B = 64
        C = 1024

        def _triu_apply(x, W, b):
            Wm = jnp.tril(W)
            return jnp.einsum('bct,st->bcs', x, Wm) + b
        h = _triu_apply(x, W1, b1)
        h = jax.nn.gelu(h, approximate=False)
        return _triu_apply(h, W2, b2)
    xn = _layernorm(x, axis=-1)
    x = x + _L0_gnn_ref(xn, L0_gnn_weight, src, dst, edge_weight) + _L0_mix_ref(xn[None], L0_mix_Wqkv, L0_mix_bqkv, L0_mix_Pmat, L0_mix_Wproj, L0_mix_bproj, L0_mix_W1, L0_mix_b1, L0_mix_W2, L0_mix_b2, L0_mix_g1, L0_mix_be1, L0_mix_g2, L0_mix_be2)[0]
    x = x + _L0_ffn_ref(_layernorm(x, axis=-1)[None], L0_ffn_W1, L0_ffn_b1, L0_ffn_W2, L0_ffn_b2)[0]
    return x

_drawn_inputs = setup_inputs


def setup_inputs(seed=0):
    import zlib

    import numpy as np

    out = dict(_drawn_inputs(seed))
    spreads = {'L0_mix_bqkv': (0.0, 0.1),
     'L0_mix_bproj': (0.0, 0.1),
     'L0_mix_b1': (0.0, 0.384),
     'L0_mix_b2': (0.0, 0.273),
     'L0_mix_g1': (1.0, 0.2),
     'L0_mix_be1': (0.0, 0.1),
     'L0_mix_g2': (1.0, 0.2),
     'L0_mix_be2': (0.0, 0.379)}
    factors = {'L0_ffn_b1': 4.113, 'L0_ffn_b2': 2.779}
    for name, (base, spread) in spreads.items():
        noise = np.random.default_rng([zlib.crc32(name.encode()), seed]).standard_normal(out[name].shape)
        drawn = base * np.exp(spread * noise) if base else spread * noise
        out[name] = jnp.asarray(drawn.astype(out[name].dtype))
    for name, factor in factors.items():
        out[name] = (out[name] * factor).astype(out[name].dtype)
    return out
```

```python
import concourse.bass as bass
from concourse import mybir
from contextlib import ExitStack

F32 = mybir.dt.float32
F16 = mybir.dt.float16
I32 = mybir.dt.int32
ALU = mybir.AluOpType
ACT = mybir.ActivationFunctionType
X = mybir.AxisListType.X

P = 128
N, D, E = 8192, 512, 131072
KB = D // P
HEADS, DH, NF = 8, 64, 256
PAIRS = HEADS // 2
HID = 1024
JB = HID // P
EPS = 1e-5
KSUM_EPS = 1e-6
NT = 4
CT = NT * P
CHUNKS = N // CT
VW = DH + 1

BLOCKS = N // P
COLS = E // P
SORT_COLS = 8
CCOLS = COLS // CHUNKS
SORT_STEPS = CCOLS // SORT_COLS
SUP = 2
SUP_EDGES = SUP * P
SUPERS = E // SUP_EDGES + BLOCKS
TILES = SUPERS * SUP
B1 = 4
SEG = SUPERS // (CHUNKS - B1)
GT = 4
GS = 3
GROUPS = SEG * SUP // GT
GSUP = GT // SUP
AR = 4
MMB = 4
assert SUPERS % (CHUNKS - B1) == 0 and GROUPS % GS == 0 and SEG % AR == 0 and GT % SUP == 0


def order_of(uses):
    return {u: k for k, u in enumerate(uses)}


MM_A = order_of([("q", j) for j in range(4)] + [("k", j) for j in range(4)] + [("v", t) for t in range(NT)]
                + [("xp", h, t) for h in range(PAIRS) for t in range(NT)])
B_STEPS = NT * PAIRS + 4


def b_uses():
    mm, tr = [], []
    for n in range(B_STEPS):
        if n < NT * PAIRS:
            mm.append(("xp", n))
        if 1 <= n <= NT * PAIRS:
            tr.append(("q", n - 1))
        if n >= 6 and (n - 6) % 4 == 0:
            tr.append(("att", (n - 6) // 4))
        if n >= 7 and (n - 7) % 4 == 0:
            mm.append(("proj", (n - 7) // 4))
    tr += [("h", k) for k in range(KB)]
    mm += [("up", j) for j in range(JB)] + [("down", t) for t in range(NT)]
    return order_of(mm), order_of(tr)


MM_B, TR_B = b_uses()
MM_C = order_of([("gnn", t) for t in range(NT)] + [("f1", j) for j in range(KB)] + [("f2", t) for t in range(NT)])
assert not len(MM_A) % MMB and not len(MM_B) % MMB and not len(MM_C) % MMB
MM_B0 = CHUNKS * len(MM_A)
MM_C0 = MM_B0 + CHUNKS * len(MM_B)
TR_B0 = CHUNKS * KB
TR_C = order_of([("agg", k) for k in range(KB)] + [("z3", k) for k in range(KB)])
TR_C0 = TR_B0 + CHUNKS * len(TR_B)


def seg_plan(with_seg):
    plan = [2] * (NT * PAIRS) + [1] * (B_STEPS - NT * PAIRS) + [1] * (KB + JB)
    assert sum(plan) == SEG
    return plan if with_seg else [0] * len(plan)


def build(nc, x, src, dst, ew, wgT, wqkv, bqkv, pmat, wproj, bproj, w1, b1, w2, b2, g1, be1, g2, be2,
          f1T, fb1, f2T, fb2, bqkv_c, out):
    xn_d = nc.dram_tensor("xn_d", (N, D), F32).ap()
    y_d = nc.dram_tensor("y_d", (N, D), F32).ap()
    agg_d = nc.dram_tensor("agg_d", (BLOCKS * P, D), F32).ap()
    qT_d = nc.dram_tensor("qT_d", (P, CHUNKS * KB * CT), F32).ap()
    slots_d = nc.dram_tensor("slots_d", (P * TILES, 3), F32).ap()
    first_d = nc.dram_tensor("first_d", (2, COLS * BLOCKS), F16).ap()

    rows = lambda a: a.rearrange("(c t p) d -> p c t d", p=P, t=NT)
    x_v, xn_v, y_v, out_v, agg_v = rows(x), rows(xn_d), rows(y_d), rows(out), rows(agg_d)
    qT_v = qT_d.rearrange("p (c k n) -> p c k n", c=CHUNKS, k=KB)
    row1 = lambda a: a.rearrange("(a n) -> a n", a=1)

    with ExitStack() as ctx:
        def sb(name, shape, dt=F32):
            return ctx.enter_context(nc.sbuf_tensor(name, shape, dt))

        def sem(name):
            return ctx.enter_context(nc.semaphore(name))

        ident = sb("ident", [P, P])
        lane_ids = sb("lane_ids", [P, P])
        slots = sb("slots", [P, TILES + 4, 3])
        keep = sb("keep", [P, SUPERS])
        block_of = sb("block_of", [1, SUPERS + 1], I32)
        pbd = sb("pbd", [P, 2 * NF])
        kv = sb("kv", [P, HEADS, 2, VW])
        bq = sb("bq", [P, 4]); bk = sb("bk", [P, 4]); b1c = sb("b1c", [P, JB]); fb1c = sb("fb1c", [P, KB])
        g1c = sb("g1c", [P, KB]); be1c = sb("be1c", [P, KB]); g2c = sb("g2c", [P, KB]); be2c = sb("be2c", [P, KB])
        brow = sb("brow", [P, 2, D])
        wproj_s = sb("wproj_s", [P, KB, D])
        w1_s = sb("w1_s", [P, KB, HID])
        w2_s = sb("w2_s", [P, JB, D])
        stats = sb("stats", [P, NT, 6]); mv = sb("mv", [P, NT, 2]); rstd = sb("rstd", [P, NT])
        vpe = sb("vpe", [P, NT]); guess = sb("guess", [P, NT], I32); half_vy = sb("half_vy", [P, NT])
        edge = sb("edge", [P, 4 * COLS])
        rec = edge[:, 0:3 * COLS].rearrange("p (c f) -> p c f", f=3)
        addr = edge[:, 3 * COLS:4 * COLS].bitcast(I32)
        f1_s = edge[:, 0:KB * D].rearrange("p (k n) -> p k n", k=KB)
        f2_s = edge[:, KB * D:2 * KB * D].rearrange("p (k n) -> p k n", k=KB)
        stage_rec = sb("stage_rec", [P, CCOLS, 3]); stage_addr = sb("stage_addr", [P, CCOLS], I32)
        stage_dst = sb("stage_dst", [P, SEG * SUP], I32)
        below = sb("below", [P, P], F16)
        hilo = sb("hilo", [2, P], F16)
        ones16 = sb("ones16", [P, P], F16)
        block_ids = sb("block_ids", [P, BLOCKS], F16)
        ARENA = 29300
        arena = sb("arena", [P, ARENA])
        at = [0]

        def lay(*shape, dt=F32):
            n = 1
            for s in shape:
                n *= s
            words = n if dt != F16 else n // 2
            a = arena[:, at[0]:at[0] + words]
            at[0] += words
            assert at[0] <= ARENA, at[0]
            if dt != F32:
                a = a.bitcast(dt)
            names = "abcd"[:len(shape)]
            if len(shape) > 1:
                a = a.rearrange(f"p ({' '.join(names)}) -> p {' '.join(names)}", **dict(zip(names, shape)))
            return a

        wqkv_s = lay(KB, 3 * D)
        xa = lay(NT, D); xn = lay(NT, D); z = lay(NT, D)
        hT = lay(KB, CT); qT = lay(4, CT); kT = lay(4, CT); v = lay(NT, HEADS, VW)
        kp = lay(2, NT, 2 * NF)
        SETUP_END = at[0]
        first = lay(CCOLS * BLOCKS, dt=F16)
        bucket = lay(COLS, dt=F16)
        onehot = lay(2, 2 * SORT_COLS, BLOCKS, dt=F16)
        picked = lay(SORT_COLS, BLOCKS)
        pos = lay(CCOLS); posi = lay(CCOLS, dt=I32); posl = lay(CCOLS, dt=I32)
        post = lay(CCOLS, dt=I32)
        nmax = sb("nmax", [P, NT * PAIRS, 2])
        at[0] = KB * 3 * D
        srci = lay(COLS, dt=I32); dsti = lay(COLS, dt=I32); ewf = lay(COLS)
        shifted = lay(COLS, dt=I32); lanei = lay(COLS, dt=I32)
        count = lay(D); pairsum = lay(D); runs = lay(2, D); firstf = lay(D)
        firstT = lay(D, dt=I32); hi_i = lay(D, dt=I32); lo_i = lay(D, dt=I32); hl = lay(2, D, dt=F16)
        samepair = lay(P); oddpair = lay(P); upto = lay(P)
        sup_i = lay(SUPERS, dt=I32); sup_f = lay(SUPERS); passed = lay(SUPERS, dt=F16); blk_f = lay(SUPERS)
        lane_i = lay(P, dt=I32); blkid_i = lay(BLOCKS, dt=I32)
        tot = lay(2); toti = lay(2, dt=I32); supn = lay(2); ends = lay(2)
        assert at[0] <= SETUP_END
        at[0] = 0
        qTb = lay(4, CT); xnb = lay(NT, D)
        qp = lay(2, 2 * NF); qpT = lay(2, 4, P)
        att = lay(2, D); attT = lay(2, KB, P)
        x1 = lay(NT, D); z2 = lay(NT, D); h2T = lay(KB, CT); gT = lay(JB, CT)
        oh = lay(2, SUP, P)
        acc = lay(AR, D)
        ring = lay(GS, GT, D)
        rden = sb("rden", [P, NT * PAIRS, 2])
        at[0] = 0
        aggb = lay(2, NT, D); yb = lay(2, NT, D); xb = lay(2, NT, D)
        aggT = lay(KB, CT); x2 = lay(NT, D); z3 = lay(NT, D); z3T = lay(KB, CT); fT = lay(KB, CT)
        outb = lay(NT, D); wg_s = lay(KB, D)

        ps = ctx.enter_context(nc.psum_tensor("ps", [P, 8, 512], F32))
        mm_bank = lambda u: ps[:, u % MMB, :]
        TR0, KV_BANK, RANK_BANK, ATT_BANK, SEG0 = 4, 6, 7, 5, 6
        att_reg = lambda n: ps[:, ATT_BANK, (n % 2) * 2 * VW:(n % 2 + 1) * 2 * VW].rearrange("p (h e) -> p h e", e=VW)

        loaded_edges = sem("loaded_edges"); loaded_w = sem("loaded_w"); loaded_wb = sem("loaded_wb")
        consts_made = sem("consts_made"); zeroed = sem("zeroed"); recs_made = sem("recs_made")
        counted = sem("counted"); onehot_made = sem("onehot_made")
        pe_setup = sem("pe_setup"); dve_done = sem("dve_done"); first_stored = sem("first_stored")
        setup_done = sem("setup_done")
        x_loaded = sem("x_loaded"); xn_made = sem("xn_made"); xn_stored = sem("xn_stored")
        z_made = sem("z_made"); first_loaded = sem("first_loaded")
        q_made = sem("q_made"); q_stored = sem("q_stored"); k_made = sem("k_made"); v_made = sem("v_made")
        hT_made = sem("hT_made")
        mm_full = sem("mm_full"); tr_full = sem("tr_full")
        max_made = sem("max_made"); exp_made = sem("exp_made")
        kv_full = sem("kv_full"); kv_free = sem("kv_free")
        rank_full = sem("rank_full"); rank_free = sem("rank_free")
        addr_made = sem("addr_made"); staged = sem("staged"); scattered = sem("scattered")
        phase_done = sem("phase_done"); slots_loaded = sem("slots_loaded"); idle = sem("idle")
        qb_loaded = sem("qb_loaded"); xnb_loaded = sem("xnb_loaded")
        qpT_made = sem("qpT_made"); att_full = sem("att_full")
        att_made = sem("att_made"); attT_made = sem("attT_made"); z2_made = sem("z2_made"); h2T_made = sem("h2T_made")
        gT_made = sem("gT_made"); y_made = sem("y_made"); y_stored = sem("y_stored")
        dst_staged = sem("dst_staged"); gathered = [sem(f"gathered{s}") for s in range(GS)]
        oh_made = sem("oh_made"); seg_full = sem("seg_full"); acc_made = sem("acc_made"); acc_saved = sem("acc_saved")
        agg_stored = sem("agg_stored"); ffn_loaded = sem("ffn_loaded")
        c_loaded = [sem(f"c_loaded{s}") for s in range(2)]; x2_made = sem("x2_made")
        aggT_made = sem("aggT_made"); z3_made = sem("z3_made"); z3T_made = sem("z3T_made"); fT_made = sem("fT_made")
        out_made = sem("out_made"); out_stored = sem("out_stored"); tril_made = sem("tril_made")
        brow_loaded = sem("brow_loaded"); x1_made = sem("x1_made"); slots_cleared = sem("slots_cleared")
        setup_left = sem("setup_left"); dve_setup = sem("dve_setup"); out_free = sem("out_free")

        SEG_CREDIT = GS * GSUP
        ACC_CREDIT = 2
        SAVED_CREDIT = AR
        X1_CREDIT = 1
        Y_CREDIT = NT

        def hold(eng, s, value):
            eng.wait_ge(s, value)
            eng.sem_inc(idle, 1)

        class Chain:
            def __init__(self):
                self.base, self.n, self.i, self.per = 0, 0, None, 0
            def enter(self, i, per, first=0):
                self.base += self.n
                self.i, self.per, self.first, self.n = i, per, first, 0
            def leave(self, times):
                assert self.n == self.per, (self.n, self.per)
                self.base += times * self.per
                self.i, self.n = None, 0
            def step(self, ins):
                ins.then_inc(dve_done, 1)
                self.n += 1
                return ins
            def value(self):
                if self.i is None:
                    return self.base + self.n
                return (self.i - self.first) * self.per + (self.base + self.n)

        block = ctx.enter_context(nc.Block())

        @block.sync
        def _(sp):
            cols = lambda a: a.rearrange("(p c) -> p c", p=P)
            sp.dma_start(srci, cols(src)).then_inc(loaded_edges, 16)
            sp.dma_start(dsti, cols(dst)).then_inc(loaded_edges, 16)
            sp.dma_start(ewf, cols(ew)).then_inc(loaded_edges, 16)
            wide = lambda w: w.rearrange("(k p) n -> p k n", p=P)
            sp.dma_start(wqkv_s, wide(wqkv)).then_inc(loaded_w, 16)
            sp.wait_ge(consts_made, 8)
            sp.dma_start(pbd[0:DH, 0:NF], pmat).then_inc(loaded_w, 16)
            sp.dma_start(pbd[DH:P, NF:2 * NF], pmat).then_inc(loaded_w, 16)
            sp.dma_start(brow[:, 0, :], bqkv[2 * D:3 * D].partition_broadcast(P)).then_inc(loaded_w, 16)
            for to, of in ((bq, bqkv_c[:, 0:4]), (bk, bqkv_c[:, 4:8]), (g1c, g1), (be1c, be1), (g2c, g2), (be2c, be2),
                           (b1c, b1), (fb1c, fb1)):
                sp.dma_start(to[:, :], of).then_inc(loaded_w, 16)
            sp.wait_ge(slots_cleared, 1)
            sp.dma_start(slots_d.rearrange("(p t) f -> p t f", p=P), slots[:, 0:TILES, :]).then_inc(zeroed, 16)
            sp.dma_start(wproj_s[:, :, :], wide(wproj)).then_inc(loaded_wb, 16)
            sp.dma_start(w1_s[:, :, :], wide(w1)).then_inc(loaded_wb, 16)
            sp.dma_start(w2_s[:, :, :], wide(w2)).then_inc(loaded_wb, 16)
            sp.sem_inc(acc_saved, SAVED_CREDIT)
            sp.wait_ge(first_stored, 1)
            for h in range(2):
                sp.dma_start(first_d[h, :].rearrange("(k p n) -> p k n", p=P, n=P),
                             hl[:, h, :].rearrange("p (k n) -> p k n", n=P)).then_inc(setup_done, 16)
            sp.wait_ge(setup_done, 32)
            sp.wait_ge(setup_left, 1)
            sp.dma_start(xa, x_v[:, 0, :, :]).then_inc(x_loaded, 16)
            sp.dma_start(first[0:2, :], first_d[:, 0:CCOLS * BLOCKS]).then_inc(first_loaded, 16)
            sp.wait_ge(xn_made, 1)
            sp.dma_start(xn_v[:, 0, :, :], xn).then_inc(xn_stored, 16)

            def a_chunk(i, last=False):
                if not last:
                    sp.wait_ge(xn_made, i + 1)
                    sp.dma_start(xa, x_v[:, i + 1, :, :]).then_inc(x_loaded, 16)
                sp.wait_ge(q_made, 4 * i + 4)
                sp.dma_start(qT_v[:, i, :, :], qT).then_inc(q_stored, 16)
                if not last:
                    sp.wait_ge(xn_made, i + 2)
                    sp.dma_start(xn_v[:, i + 1, :, :], xn).then_inc(xn_stored, 16)
                    sp.wait_ge(rank_full, SORT_STEPS * i + SORT_STEPS)
                    sp.dma_start(first[0:2, :], first_d[:, bass.ds((i + 1) * (CCOLS * BLOCKS), CCOLS * BLOCKS)])\
                        .then_inc(first_loaded, 16)
            with sp.Fori(0, CHUNKS - 1) as i:
                a_chunk(i)
            a_chunk(CHUNKS - 1, last=True)
            sp.wait_ge(q_stored, 16 * CHUNKS)
            sp.wait_ge(xn_stored, 16 * CHUNKS)
            sp.sem_inc(phase_done, 1)
            sp.wait_ge(phase_done, 4)
            sp.dma_start(brow[:, 0, :], bproj.partition_broadcast(P)).then_inc(brow_loaded, 16)
            sp.dma_start(brow[:, 1, :], b2.partition_broadcast(P)).then_inc(brow_loaded, 16)

            def b_loads(i):
                sp.wait_ge(mm_full, MM_B0 + len(MM_B) * i)
                sp.dma_start(qTb, qT_v[:, i, :, :]).then_inc(qb_loaded, 16)
                sp.wait_ge(x1_made, i * NT + X1_CREDIT)
                sp.dma_start(xnb, xn_v[:, i, :, :]).then_inc(xnb_loaded, 16)

            def b_store(i):
                sp.wait_ge(y_made, i * NT + (Y_CREDIT + NT))
                sp.dma_start(y_v[:, i, :, :], x1).then_inc(y_stored, 16)

            with sp.Fori(0, B1) as i:
                b_loads(i)
                b_store(i)
            sp.wait_ge(scattered, 16 * COLS)
            sp.dma_start(slots[:, 0:TILES, :], slots_d.rearrange("(p t) f -> p t f", p=P)).then_inc(slots_loaded, 16)
            sp.dma_start(f1_s, wide(f1T)).then_inc(ffn_loaded, 16)
            sp.dma_start(f2_s, wide(f2T)).then_inc(ffn_loaded, 16)
            with sp.Fori(B1, CHUNKS) as i:
                b_loads(i)
                with sp.Fori(0, SEG // AR) as r:
                    for a in range(AR):
                        s = (i - B1) * SEG + (r * AR + a)
                        sp.wait_ge(acc_made, s + (ACC_CREDIT + 1))
                        here = sp.value_load(block_of[0:1, bass.ds(s, 1)], min_val=0, max_val=BLOCKS - 1)
                        nxt = sp.value_load(block_of[0:1, bass.ds(s + 1, 1)], min_val=0, max_val=BLOCKS)
                        with sp.If(here < nxt):
                            sp.dma_start(agg_d[bass.ds(here * P, P), :], acc[:, a, :]).then_inc(agg_stored, 16)
                            hold(sp, agg_stored, (here + 1) * 16)
                        sp.sem_inc(acc_saved, 1)
                b_store(i)
            sp.wait_ge(y_stored, 16 * CHUNKS)
            sp.wait_ge(agg_stored, 16 * BLOCKS)
            sp.sem_inc(phase_done, 1)
            sp.wait_ge(phase_done, 8)
            sp.dma_start(brow[:, 0, :], fb2.partition_broadcast(P)).then_inc(brow_loaded, 16)
            sp.dma_start(wg_s, wide(wgT)).then_inc(loaded_wb, 16)

            def c_load(i, b):
                sp.dma_start(aggb[:, b, :, :], agg_v[:, i, :, :]).then_inc(c_loaded[b], 16)
                sp.dma_start(yb[:, b, :, :], y_v[:, i, :, :]).then_inc(c_loaded[b], 16)
                sp.dma_start(xb[:, b, :, :], x_v[:, i, :, :]).then_inc(c_loaded[b], 16)

            def c_store(i):
                sp.wait_ge(out_made, i * NT + (Y_CREDIT + NT))
                sp.dma_start(out_v[:, i, :, :], outb).then_inc(out_stored, 16)
                sp.wait_ge(out_stored, i * 16 + 16)
                sp.sem_inc(out_free, 1)
            sp.sem_inc(out_free, 1)
            c_load(0, 0)
            c_load(1, 1)
            with sp.Fori(0, CHUNKS // 2 - 1) as r:
                for b in range(2):
                    i = 2 * r + b
                    sp.wait_ge(x2_made, i * NT + NT)
                    c_load(i + 2, b)
                    c_store(i)
            c_store(CHUNKS - 2)
            c_store(CHUNKS - 1)
            sp.wait_ge(out_stored, 16 * CHUNKS)

        @block.gpsimd
        def _(pool):
            g = nc.gpsimd
            g.memset(ident[:, :], 0.0).then_inc(consts_made, 1)
            g.memset(samepair, 0.0).then_inc(consts_made, 1)
            g.memset(oddpair, 0.0).then_inc(consts_made, 1)
            g.memset(upto[0:BLOCKS, :], 1.0).then_inc(consts_made, 1)
            g.memset(below[:, :], 1.0).then_inc(consts_made, 1)
            g.memset(ones16[:, :], 1.0).then_inc(consts_made, 1)
            g.memset(hilo[:, :], 1.0).then_inc(consts_made, 1)
            g.memset(pbd[:, :], 0.0).then_inc(consts_made, 1)
            pool.wait_ge(consts_made, 8)

            def diag(m, base, n=P):
                return g.affine_select(out=m, in_=m, compare_op=ALU.not_equal, fill=1.0, base=base,
                                       pattern=[[-1, n]], channel_multiplier=1).then_inc(consts_made, 1)
            diag(ident[:, :], 0)
            diag(samepair, 0)
            diag(oddpair, BLOCKS)
            g.memset(hilo[0:1, :], float(P)).then_inc(consts_made, 1)
            g.affine_select(out=below[:, :], in_=below[:, :], compare_op=ALU.is_gt, fill=0.0, base=0,
                            pattern=[[1, P]], channel_multiplier=-1).then_inc(consts_made, 1)
            g.affine_select(out=upto[0:BLOCKS, :].rearrange("p (a b) -> p a b", a=2),
                            in_=upto[0:BLOCKS, :].rearrange("p (a b) -> p a b", a=2), compare_op=ALU.is_ge,
                            fill=0.0, base=0, pattern=[[0, 2], [1, BLOCKS]], channel_multiplier=-1)\
                .then_inc(consts_made, 1)
            pool.wait_ge(consts_made, 14)
            diag(samepair, BLOCKS)
            pool.wait_ge(consts_made, 15)
            diag(samepair, -BLOCKS)
            g.iota(lane_i, pattern=[[1, P]], base=0, channel_multiplier=0).then_inc(consts_made, 1)
            g.iota(blkid_i, pattern=[[1, BLOCKS]], base=0, channel_multiplier=0).then_inc(consts_made, 1)
            g.iota(sup_i, pattern=[[1, SUPERS]], base=0, channel_multiplier=0).then_inc(consts_made, 1)
            pool.wait_ge(loaded_edges, 48)
            g.tensor_copy(rec[:, :, 1], ewf).then_inc(recs_made, 1)
            g.tensor_copy(rec[:, :, 2].bitcast(I32), dsti).then_inc(recs_made, 1)
            pool.wait_ge(recs_made, 3)
            pool.wait_ge(zeroed, 16)
            with pool.Fori(0, CHUNKS) as i:
                hold(pool, addr_made, i + 1)
                g.tensor_copy(stage_rec[:, :, :], rec[:, bass.ds(i * CCOLS, CCOLS), :]).then_inc(staged, 1)
                g.tensor_copy(stage_addr[:, :], addr[:, bass.ds(i * CCOLS, CCOLS)]).then_inc(staged, 1)
                hold(pool, staged, 2 * i + 2)
                for c in range(CCOLS):
                    pool.indirect_dma_start(
                        out=slots_d, out_offset=bass.IndirectOffsetOnAxis(ap=stage_addr[:, c:c + 1], axis=0),
                        in_=stage_rec[:, c, :], in_offset=None).then_inc(scattered, 16)
                hold(pool, scattered, (i + 1) * (16 * CCOLS))
            pool.wait_ge(phase_done, 4)
            pool.wait_ge(slots_loaded, 16)
            with pool.Fori(0, CHUNKS - B1) as i:
                g.tensor_copy(stage_dst[:, :], slots[:, bass.ds(i * (SEG * SUP), SEG * SUP), 2].bitcast(I32))\
                    .then_inc(dst_staged, 1)
                hold(pool, dst_staged, i + 1)
                for gr in range(GROUPS):
                    hold(pool, seg_full, i * SEG + (GSUP * gr + GSUP))
                    for t in range(GT):
                        c = gr * GT + t
                        pool.indirect_dma_start(
                            out=ring[:, gr % GS, t, :], out_offset=None, in_=xn_d,
                            in_offset=bass.IndirectOffsetOnAxis(ap=stage_dst[:, c:c + 1], axis=0))\
                            .then_inc(gathered[gr % GS], 16)
                for s in range(GS):
                    hold(pool, gathered[s], (i + 1) * (16 * GT * GROUPS // GS))
            pool.wait_ge(ffn_loaded, 32)
            for m in (f1_s, f2_s):
                for k in range(KB):
                    tri = m[:, k, k * P:(k + 1) * P]
                    g.affine_select(out=tri, in_=tri, compare_op=ALU.is_ge, fill=0.0, base=0, pattern=[[1, P]],
                                    channel_multiplier=-1).then_inc(tril_made, 1)

        @block.scalar
        def _(act):
            a = nc.scalar
            act.wait_ge(loaded_w, 16 * 12)

            def hT_copy(i):
                for k in range(KB):
                    act.wait_ge(tr_full, i * KB + (k + 1))
                    a.activation(hT[:, k, :], ps[:, TR0 + k % 2, :], ACT.Identity, bias=be1c[:, k:k + 1],
                                 scale=g1c[:, k:k + 1]).then_inc(hT_made, 1)
            hT_copy(0)

            def a_chunk(i, last=False):
                if not (isinstance(i, int) and i == 0):
                    hold(act, q_stored, i * 16)
                for j in range(4):
                    act.wait_ge(mm_full, i * len(MM_A) + (MM_A["q", j] + 1))
                    a.activation(qT[:, j, :], mm_bank(MM_A["q", j]), ACT.Identity, bias=bq[:, j:j + 1])\
                        .then_inc(q_made, 1)
                for j in range(4):
                    act.wait_ge(mm_full, i * len(MM_A) + (MM_A["k", j] + 1))
                    a.activation(kT[:, j, :], mm_bank(MM_A["k", j]), ACT.Identity, bias=bk[:, j:j + 1])\
                        .then_inc(k_made, 1)
                if not last:
                    hT_copy(i + 1)
                for h in range(PAIRS):
                    for t in range(NT):
                        u = MM_A["xp", h, t]
                        act.wait_ge(max_made, i * (PAIRS * NT) + (h * NT + t + 1))
                        for e in range(2):
                            ins = a.activation(kp[:, h % 2, t, e * NF:(e + 1) * NF],
                                               mm_bank(u)[:, e * NF:(e + 1) * NF], ACT.Exp,
                                               bias=nmax[:, h * NT + t, e:e + 1])
                        ins.then_inc(exp_made, 1)
            a_chunk(0)
            with act.Fori(1, CHUNKS - 1) as i:
                a_chunk(i)
            a_chunk(CHUNKS - 1, last=True)
            act.sem_inc(phase_done, 1)
            act.wait_ge(phase_done, 4)

            def b_chunk(i):
                def tr_copy(to, ordinal, made, **kw):
                    act.wait_ge(tr_full, i * len(TR_B) + (TR_B0 + ordinal + 1))
                    a.activation(to, ps[:, TR0, :], ACT.Identity, **kw).then_inc(made, 1)
                for n in range(B_STEPS):
                    if n < NT * PAIRS:
                        act.wait_ge(max_made, i * (NT * PAIRS) + (CHUNKS * NT * PAIRS + n + 1))
                        for e in range(2):
                            ins = a.activation(qp[:, n % 2, e * NF:(e + 1) * NF],
                                               mm_bank(MM_B["xp", n])[:, e * NF:(e + 1) * NF], ACT.Exp,
                                               bias=nmax[:, n, e:e + 1])
                        ins.then_inc(exp_made, 1)
                    if 1 <= n <= NT * PAIRS:
                        m = n - 1
                        if m >= 2:
                            hold(act, att_full, i * (NT * PAIRS) + (m - 1))
                        tr_copy(qpT[:, m % 2, :, :], TR_B["q", m], qpT_made)
                    if n >= 6 and (n - 6) % 4 == 0:
                        t = (n - 6) // 4
                        if t >= 2:
                            hold(act, mm_full, i * len(MM_B) + (MM_B0 + MM_B["proj", t - 2] + 1))
                        tr_copy(attT[:, t % 2, :, :], TR_B["att", t], attT_made)
                for k in range(KB):
                    tr_copy(h2T[:, k, :], TR_B["h", k], h2T_made,
                            bias=be2c[:, k:k + 1], scale=g2c[:, k:k + 1])
                for j in range(JB):
                    u = MM_B["up", j]
                    act.wait_ge(mm_full, i * len(MM_B) + (MM_B0 + u + 1))
                    a.activation(gT[:, j, :], mm_bank(u), ACT.Gelu, bias=b1c[:, j:j + 1]).then_inc(gT_made, 1)
            with act.Fori(0, CHUNKS) as i:
                b_chunk(i)
            act.sem_inc(phase_done, 1)
            act.wait_ge(phase_done, 8)

            with act.Fori(0, CHUNKS) as i:
                for part, to, made in (("agg", aggT, aggT_made), ("z3", z3T, z3T_made)):
                    for k in range(KB):
                        act.wait_ge(tr_full, i * len(TR_C) + (TR_C0 + TR_C[part, k] + 1))
                        a.activation(to[:, k, :], ps[:, TR0 + k % 2, :], ACT.Copy).then_inc(made, 1)
                for j in range(KB):
                    u = MM_C["f1", j]
                    act.wait_ge(mm_full, i * len(MM_C) + (MM_C0 + u + 1))
                    a.activation(fT[:, j, :], mm_bank(u), ACT.Gelu, bias=fb1c[:, j:j + 1]).then_inc(fT_made, 1)

        @block.vector
        def _(dve):
            vec = nc.vector
            ch = Chain()

            def link(ins):
                ch.step(ins)
                hold(dve, dve_done, ch.value())

            dve.sem_inc(kv_free, 1)
            dve.sem_inc(rank_free, 1)
            dve.sem_inc(acc_made, ACC_CREDIT)
            dve.sem_inc(x1_made, X1_CREDIT)
            dve.sem_inc(y_made, Y_CREDIT)
            dve.sem_inc(out_made, Y_CREDIT)
            vec.memset(slots[:, :, :], 0.0)
            vec.memset(kv[:, :, :, :], 0.0)
            vec.memset(keep[:, 0:1], 0.0)
            vec.memset(block_of[0:1, SUPERS:SUPERS + 1], BLOCKS)
            link(vec.memset(tot, 0.0))
            dve.sem_inc(slots_cleared, 1)
            dve.wait_ge(consts_made, 19)
            vec.tensor_copy(lane_ids[:, :], lane_i)
            vec.tensor_copy(block_ids[:, :], blkid_i)
            vec.tensor_copy(sup_f, sup_i)
            dve.wait_ge(loaded_edges, 48)
            vec.tensor_scalar(shifted, srci, 7, None, ALU.logical_shift_right)
            link(vec.tensor_scalar(lanei, srci, P - 1, None, ALU.bitwise_and))
            link(vec.tensor_copy(bucket, shifted))
            vec.tensor_copy(rec[:, :, 0], lanei).then_inc(recs_made, 1)

            ROOT = 3 + 3 * 3

            def make_onehot(to, col, ncols):
                return vec.tensor_tensor(
                    to, bucket[:, bass.ds(col, ncols)].unsqueeze(2).broadcast_to([P, ncols, BLOCKS]),
                    block_ids[:, :].unsqueeze(1).broadcast_to([P, ncols, BLOCKS]), ALU.is_equal)

            W = 2 * SORT_COLS
            make_onehot(onehot[:, 0, :, :], 0, W).then_inc(onehot_made, 1)
            make_onehot(onehot[:, 1, :, :], W, W).then_inc(onehot_made, 1)
            with dve.Fori(1, COLS // (2 * W)) as r:
                for b in range(2):
                    dve.wait_ge(counted, r * 2 + (b - 1))
                    make_onehot(onehot[:, b, :, :], (2 * r + b) * W, W).then_inc(onehot_made, 1)
            dve.wait_ge(counted, COLS // W)
            vec.tensor_copy(count, ps[:, RANK_BANK, :]).then_inc(dve_setup, 1)
            dve.wait_ge(pe_setup, 1)
            vec.memset(runs[:, 0, 0:1], 0.0)
            vec.tensor_copy(runs[:, 0, 1:D], ps[:, 6, 0:D - 1])
            link(vec.tensor_copy(pairsum, ps[:, 6, :]))
            k, d = 0, 1
            while d < D:
                vec.tensor_copy(runs[:, 1 - k, 0:d], runs[:, k, 0:d])
                link(vec.tensor_tensor(runs[:, 1 - k, d:D], runs[:, k, d:D], runs[:, k, 0:D - d], ALU.add))
                k, d = 1 - k, 2 * d
            link(vec.tensor_tensor(tot[:, 0:1], runs[:, k, D - 1:D], pairsum[:, D - 1:D], ALU.add))
            link(vec.tensor_scalar(toti[:, 0:1], tot[:, 0:1], float(SUP_EDGES - 1), None, ALU.add))
            link(vec.tensor_scalar(toti[:, 1:2], toti[:, 0:1], 8, None, ALU.logical_shift_right))
            link(vec.tensor_scalar(supn[:, 0:1], toti[:, 1:2], 1.0, None, ALU.max))
            dve.sem_inc(dve_setup, 1)
            dve.wait_ge(pe_setup, 2)
            link(vec.tensor_copy(ends[:, 0:1], ps[:, 4, 0:1]))
            link(vec.tensor_tensor(ends[:, 1:2], ends[:, 0:1], supn[:, 0:1], ALU.subtract))
            link(vec.tensor_scalar(ends[:, 1:2], ends[:, 1:2], float(SUP_EDGES), None, ALU.mult))
            vec.tensor_scalar(passed[0:BLOCKS, :], sup_f[0:BLOCKS, :], ends[0:BLOCKS, 0:1], None, ALU.is_ge)
            link(vec.scalar_tensor_tensor(firstf, runs[:, k, :], ends[:, 1:2], ps[:, 5, :], ALU.add, ALU.add))
            dve.sem_inc(dve_setup, 1)
            dve.wait_ge(pe_setup, 3)
            half = SUPERS // 2
            for h in range(2):
                vec.tensor_scalar(blk_f[:, h * half:(h + 1) * half], ps[:, 2 + h, 0:half], float(BLOCKS - 1), None,
                                  ALU.min)
            link(vec.tensor_copy(firstT, ps[:, 0, :]))
            vec.tensor_tensor(keep[:, 1:SUPERS], blk_f[:, 1:SUPERS], blk_f[:, 0:SUPERS - 1], ALU.is_equal)
            vec.tensor_copy(block_of[0:1, 0:SUPERS], blk_f[0:1, :])
            vec.tensor_scalar(hi_i, firstT, 7, None, ALU.logical_shift_right)
            link(vec.tensor_scalar(lo_i, firstT, P - 1, None, ALU.bitwise_and))
            vec.tensor_copy(hl[:, 0, :], hi_i)
            link(vec.tensor_copy(hl[:, 1, :], lo_i))
            dve.sem_inc(first_stored, 1)
            dve.wait_ge(recs_made, 3)
            dve.wait_ge(setup_done, 32)
            dve.sem_inc(setup_left, 1)
            link(vec.memset(v, 1.0))

            def inverse_root():
                link(vec.tensor_scalar(vpe[:, :], mv[:, :, 1], EPS, None, ALU.add))
                link(vec.tensor_scalar(guess[:, :], vpe[:, :].bitcast(I32), 1, None, ALU.logical_shift_right))
                link(vec.tensor_scalar(rstd[:, :].bitcast(I32), guess[:, :], -1.0, float(0x5F3759DF),
                                       ALU.mult, ALU.add))
                for _ in range(3):
                    link(vec.scalar_tensor_tensor(half_vy[:, :], rstd[:, :], -0.5, rstd[:, :], ALU.mult, ALU.mult))
                    link(vec.tensor_tensor(half_vy[:, :], half_vy[:, :], vpe[:, :], ALU.mult))
                    link(vec.scalar_tensor_tensor(rstd[:, :], half_vy[:, :], 1.5, rstd[:, :], ALU.add, ALU.mult))

            def normalise(to, of):
                for t in range(NT):
                    last = vec.bn_stats(stats[:, t, :], of[:, t, :])
                link(last)
                for t in range(NT):
                    last = vec.bn_aggr(mv[:, t, :], stats[:, t, :])
                link(last)
                inverse_root()
                for t in range(NT):
                    last = vec.tensor_scalar(to[:, t, :], of[:, t, :], mv[:, t, 0:1], rstd[:, t:t + 1],
                                             ALU.subtract, ALU.mult)
                return last

            def norms(i):
                hold(dve, x_loaded, (i + 1) * 16)
                if not (isinstance(i, int) and i == 0):
                    hold(dve, xn_stored, i * 16)
                    hold(dve, tr_full, i * KB)
                normalise(xn, xa).then_inc(xn_made, 1)
                hold(dve, xn_made, i + 1)
                normalise(z, xn).then_inc(z_made, 1)
                hold(dve, z_made, i + 1)

            def rank_onehot(i, r):
                make_onehot(onehot[:, r % 2, 0:SORT_COLS, :], i * CCOLS + r * SORT_COLS, SORT_COLS)\
                    .then_inc(onehot_made, 1)

            def rank(i, r):
                hold(dve, rank_full, i * SORT_STEPS + (r + 1))
                hold(dve, dve_done, ch.value())
                vec.tensor_tensor(picked, ps[:, RANK_BANK, :].rearrange("p (c b) -> p c b", b=BLOCKS),
                                  onehot[:, r % 2, 0:SORT_COLS, :], ALU.mult).then_inc(rank_free, 1)
                hold(dve, rank_free, i * SORT_STEPS + (r + 2))
                ch.step(vec.tensor_reduce(pos[:, r * SORT_COLS:(r + 1) * SORT_COLS], picked, X, ALU.add))

            norms(0)

            def a_chunk(i, last=False):
                hold(dve, dve_done, ch.value())
                rank_onehot(i, 0)
                rank_onehot(i, 1)
                if not last:
                    norms(i + 1)
                for r in range(SORT_STEPS):
                    rank(i, r)
                    if r + 2 < SORT_STEPS:
                        rank_onehot(i, r + 2)
                    if r == SORT_STEPS // 2 - 1:
                        for t in range(NT):
                            u = MM_A["v", t]
                            dve.wait_ge(mm_full, i * len(MM_A) + (u + 1))
                            vec.tensor_tensor(v[:, t, :, 0:DH],
                                              mm_bank(u).rearrange("p (h e) -> p h e", e=DH),
                                              brow[:, 0, :].rearrange("p (h e) -> p h e", e=DH), ALU.add)\
                                .then_inc(v_made, 1)
                    if r >= SORT_STEPS // 2 - 1 and r < SORT_STEPS - 1:
                        h = r - (SORT_STEPS // 2 - 1)
                        for t in range(NT):
                            u = MM_A["xp", h, t]
                            dve.wait_ge(mm_full, i * len(MM_A) + (u + 1))
                            vec.tensor_reduce(nmax[:, h * NT + t, :],
                                              mm_bank(u).rearrange("p (e f) -> p e f", e=2), X, ALU.max, negate=True)\
                                .then_inc(max_made, 1)
                        if h >= 1:
                            kv_add(i, h - 1)
                hold(dve, dve_done, ch.value())
                link(vec.tensor_copy(posi, pos))
                vec.tensor_scalar(posl, posi, P - 1, None, ALU.bitwise_and)
                link(vec.tensor_scalar(post, posi, 7, None, ALU.logical_shift_right))
                vec.scalar_tensor_tensor(addr[:, bass.ds(i * CCOLS, CCOLS)], posl, float(TILES), post,
                                         ALU.mult, ALU.add).then_inc(addr_made, 1)
                kv_add(i, PAIRS - 1)

            def kv_add(i, h):
                hold(dve, kv_full, i * PAIRS + (h + 1))
                to = kv[:, 2 * h:2 * h + 2, :, :].rearrange("p h c e -> p (h c e)")
                vec.tensor_tensor(to, to, ps[:, KV_BANK, 0:4 * VW], ALU.add).then_inc(kv_free, 1)

            A_LINKS = 2 * (2 + ROOT) + SORT_STEPS + 2
            ch.enter(0, A_LINKS)
            a_chunk(0)
            ch.leave(1)
            with dve.Fori(1, CHUNKS - 1) as i:
                ch.enter(i, A_LINKS, 1)
                a_chunk(i)
            ch.leave(CHUNKS - 2)
            a_chunk(CHUNKS - 1, last=True)
            hold(dve, kv_free, 1 + PAIRS * CHUNKS)
            link(vec.tensor_scalar(kv[:, :, :, :], kv[:, :, :, :], 1.0 / float(NF) ** 0.5, None, ALU.mult))
            link(vec.tensor_scalar(kv[:, :, :, DH:VW], kv[:, :, :, DH:VW], KSUM_EPS, None, ALU.add))
            dve.wait_ge(addr_made, CHUNKS)
            dve.sem_inc(phase_done, 1)
            dve.wait_ge(phase_done, 4)
            link(vec.memset(acc[:, AR - 1, :], 0.0))
            dve.wait_ge(brow_loaded, 32)

            def make_oh(s, b):
                for t in range(SUP):
                    c = s * SUP + t
                    last = vec.tensor_scalar(oh[:, b, t, :], lane_ids[:, :], slots[:, bass.ds(c, 1), 0],
                                             slots[:, bass.ds(c, 1), 1], ALU.is_equal, ALU.mult)
                last.then_inc(oh_made, 1)

            def seg(i, k):
                s = (i - B1) * SEG + k
                hold(dve, seg_full, s + (SEG_CREDIT + 1))
                hold(dve, acc_saved, s + 1)
                hold(dve, acc_made, s + ACC_CREDIT)
                vec.scalar_tensor_tensor(acc[:, k % AR, :], acc[:, (k - 1) % AR, :], keep[:, bass.ds(s, 1)],
                                         ps[:, SEG0 + k % 2, :], ALU.mult, ALU.add).then_inc(acc_made, 1)
                make_oh(s + 2, k % 2)

            def b_chunk(i, with_seg, first_chunk):
                todo = seg_plan(with_seg)
                done = [0]

                def fill(n):
                    for _ in range(n):
                        seg(i, done[0])
                        done[0] += 1
                hold(dve, xnb_loaded, (i + 1) * 16)
                for t in range(NT):
                    last = vec.tensor_tensor(xnb[:, t, :], xnb[:, t, :], brow[:, 0, :], ALU.add)
                link(last)
                for n in range(B_STEPS):
                    if n < NT * PAIRS:
                        dve.wait_ge(mm_full, i * len(MM_B) + (MM_B0 + MM_B["xp", n] + 1))
                        vec.tensor_reduce(nmax[:, n, :], mm_bank(MM_B["xp", n]).rearrange("p (e f) -> p e f", e=2),
                                          X, ALU.max, negate=True).then_inc(max_made, 1)
                    if n >= 3 and n - 3 < NT * PAIRS:
                        m = n - 3
                        t, h = m // PAIRS, m % PAIRS
                        hold(dve, att_full, i * (NT * PAIRS) + (m + 1))
                        link(vec.reciprocal(rden[:, m, :], att_reg(m)[:, :, DH]))
                        vec.tensor_tensor(att[:, t % 2, h * P:(h + 1) * P].rearrange("p (h e) -> p h e", e=DH),
                                          att_reg(m)[:, :, 0:DH], rden[:, m, :].unsqueeze(2).broadcast_to([P, 2, DH]),
                                          ALU.mult).then_inc(att_made, 1)
                    if n >= 7 and (n - 7) % 4 == 0:
                        t = (n - 7) // 4
                        u = MM_B["proj", t]
                        dve.wait_ge(mm_full, i * len(MM_B) + (MM_B0 + u + 1))
                        if t == 0 and not first_chunk:
                            hold(dve, y_stored, i * 16)
                        vec.tensor_tensor(x1[:, t, :], mm_bank(u), xnb[:, t, :], ALU.add).then_inc(x1_made, 1)
                        hold(dve, x1_made, i * NT + (X1_CREDIT + t + 1))
                        link(vec.bn_stats(stats[:, t, :], x1[:, t, :]))
                        link(vec.bn_aggr(mv[:, t, :], stats[:, t, :]))
                        if t == NT - 1:
                            inverse_root()
                            for k in range(NT):
                                vec.tensor_scalar(z2[:, k, :], x1[:, k, :], mv[:, k, 0:1], rstd[:, k:k + 1],
                                                  ALU.subtract, ALU.mult).then_inc(z2_made, 1)
                            hold(dve, z2_made, i * NT + NT)
                            for k in range(NT):
                                ch.step(vec.tensor_tensor(x1[:, k, :], x1[:, k, :], brow[:, 1, :], ALU.add))
                    fill(todo[n])
                for k in range(KB + JB):
                    fill(todo[B_STEPS + k])
                hold(dve, dve_done, ch.value())
                for t in range(NT):
                    u = MM_B["down", t]
                    dve.wait_ge(mm_full, i * len(MM_B) + (MM_B0 + u + 1))
                    vec.tensor_tensor(x1[:, t, :], x1[:, t, :], mm_bank(u), ALU.add).then_inc(y_made, 1)

            B_LINKS = 1 + NT * PAIRS + 3 * NT + ROOT
            ch.enter(0, B_LINKS)
            b_chunk(0, False, True)
            ch.leave(1)
            with dve.Fori(1, B1) as i:
                ch.enter(i, B_LINKS, 1)
                b_chunk(i, False, False)
            ch.leave(B1 - 1)
            dve.wait_ge(slots_loaded, 16)
            make_oh(0, 0)
            make_oh(1, 1)
            with dve.Fori(B1, CHUNKS) as i:
                ch.enter(i, B_LINKS, B1)
                b_chunk(i, True, False)
            ch.leave(CHUNKS - B1)
            dve.wait_ge(oh_made, SUPERS + 2)
            dve.sem_inc(phase_done, 1)
            dve.wait_ge(phase_done, 8)
            dve.wait_ge(brow_loaded, 48)

            def c_chunk(i, b, free):
                hold(dve, c_loaded[b], free * 48 + 48)
                for t in range(NT):
                    last = vec.tensor_tensor(yb[:, b, t, :], yb[:, b, t, :], xb[:, b, t, :], ALU.add)
                link(last)
                for t in range(NT):
                    u = MM_C["gnn", t]
                    dve.wait_ge(mm_full, i * len(MM_C) + (MM_C0 + u + 1))
                    vec.tensor_tensor(x2[:, t, :], mm_bank(u), yb[:, b, t, :], ALU.add).then_inc(x2_made, 1)
                hold(dve, x2_made, i * NT + NT)
                normalise(z3, x2).then_inc(z3_made, 1)
                hold(dve, z3_made, i + 1)
                for t in range(NT):
                    last = vec.tensor_tensor(x2[:, t, :], x2[:, t, :], brow[:, 0, :], ALU.add)
                link(last)
                hold(dve, out_free, i + 1)
                for t in range(NT):
                    u = MM_C["f2", t]
                    dve.wait_ge(mm_full, i * len(MM_C) + (MM_C0 + u + 1))
                    vec.tensor_tensor(outb[:, t, :], x2[:, t, :], mm_bank(u), ALU.add).then_inc(out_made, 1)

            C_LINKS = 1 + 2 + ROOT + 1
            with dve.Fori(0, CHUNKS // 2) as r:
                ch.enter(r, 2 * C_LINKS)
                for b in range(2):
                    c_chunk(2 * r + b, b, r)
            ch.leave(CHUNKS // 2)

        @block.tensor
        def _(pe):
            mm, tr = nc.tensor.matmul, nc.tensor.transpose

            def take_mm(phase, use, i):
                order = {"A": MM_A, "B": MM_B, "C": MM_C}[phase]
                u = order[use]
                last = list(order)[(u - MMB) % len(order)]
                j = i if u >= MMB else i - 1
                if isinstance(j, int) and j < 0:
                    return mm_bank(u)
                name, k = last[0], last[-1]
                if name == "xp" and phase == "A":
                    k = last[1] * NT + last[2]
                taken = {"q": (q_made, 4, 0), "k": (k_made, 4, 0), "v": (v_made, NT, 0),
                         "xp": (exp_made, NT * PAIRS, CHUNKS * NT * PAIRS * (phase == "B")),
                         "proj": (x1_made, NT, X1_CREDIT), "up": (gT_made, JB, 0), "down": (y_made, NT, Y_CREDIT),
                         "gnn": (x2_made, NT, 0), "f1": (fT_made, KB, 0), "f2": (out_made, NT, Y_CREDIT)}
                s, per, credit = taken[name]
                if u >= MMB:
                    pe.wait_ge(s, j * per + (credit + k + 1))
                else:
                    pe.wait_ge(s, i * per + (credit - per + k + 1))
                return mm_bank(u)

            pe.wait_ge(consts_made, 19)
            with pe.Fori(0, COLS // (4 * SORT_COLS)) as r:
                for b in range(2):
                    pe.wait_ge(onehot_made, 2 * r + (b + 1))
                    for k in range(SORT_COLS):
                        last = mm(ps[:, RANK_BANK, bass.ds(r * (2 * SORT_COLS) + (b * SORT_COLS + k), 1)],
                                  onehot[:, b, 2 * k:2 * k + 2, :].rearrange("p c b -> p (c b)"), ones16[:, 0:1],
                                  start=True, stop=True)
                    last.then_inc(counted, 1)
            pe.wait_ge(dve_setup, 1)
            mm(ps[:, 6, :], samepair, count, start=True, stop=True)
            mm(ps[:, 5, :], oddpair, count, start=True, stop=True).then_inc(pe_setup, 1)
            pe.wait_ge(dve_setup, 2)
            mm(ps[:, 4, 0:1], upto[0:BLOCKS, :], supn[0:BLOCKS, 0:1], start=True, stop=True).then_inc(pe_setup, 1)
            pe.wait_ge(dve_setup, 3)
            half = SUPERS // 2
            for h in range(2):
                mm(ps[:, 2 + h, 0:half], ones16[0:BLOCKS, :], passed[0:BLOCKS, h * half:(h + 1) * half],
                   start=True, stop=True)
            for k in range(KB):
                last = tr(ps[:, 0, k * P:(k + 1) * P], firstf[:, k * P:(k + 1) * P], ident[:, :])
            last.then_inc(pe_setup, 1)
            pe.wait_ge(setup_left, 1)
            pe.sem_inc(seg_full, SEG_CREDIT)
            pe.wait_ge(loaded_w, 16 * 12)

            def hT_transposes(i):
                pe.wait_ge(z_made, i + 1)
                for k in range(KB):
                    if not (isinstance(i, int) and i == 0 and k < 2):
                        pe.wait_ge(hT_made, i * KB + (k - 1))
                    for t in range(NT):
                        last = tr(ps[:, TR0 + k % 2, t * P:(t + 1) * P], z[:, t, k * P:(k + 1) * P], ident[:, :])
                    last.then_inc(tr_full, 1)

            def rank(i, r):
                pe.wait_ge(onehot_made, i * SORT_STEPS + (COLS // (2 * SORT_COLS) + r + 1))
                pe.wait_ge(rank_free, i * SORT_STEPS + (r + 1))
                pe.wait_ge(first_loaded, i * 16 + 16)
                w = SORT_COLS * BLOCKS
                mm(ps[:, RANK_BANK, :], below[:, :],
                   onehot[:, r % 2, 0:SORT_COLS, :].rearrange("p c b -> p (c b)"), start=True, stop=False)
                mm(ps[:, RANK_BANK, :], hilo[0:2, :], first[0:2, r * w:(r + 1) * w],
                   start=False, stop=True).then_inc(rank_full, 1)

            def kv_product(i, h):
                pe.wait_ge(exp_made, i * (NT * PAIRS) + (h * NT + NT))
                pe.wait_ge(v_made, i * NT + NT)
                pe.wait_ge(kv_free, i * PAIRS + (h + 1))
                for e in range(2):
                    for c in range(2):
                        r = e * 2 + c
                        for t in range(NT):
                            last = mm(ps[:, KV_BANK, r * VW:(r + 1) * VW], kp[:, h % 2, t, r * P:(r + 1) * P],
                                      v[:, t, 2 * h + e, :], start=(t == 0), stop=(t == NT - 1))
                last.then_inc(kv_full, 1)

            def a_chunk(i, last=False):
                pe.wait_ge(hT_made, i * KB + KB)
                for part, off in (("q", 0), ("k", D)):
                    for j in range(4):
                        bank = take_mm("A", (part, j), i)
                        for k in range(KB):
                            ins = mm(bank, wqkv_s[:, k, off + j * P:off + (j + 1) * P], hT[:, k, :],
                                     start=(k == 0), stop=(k == KB - 1))
                        ins.then_inc(mm_full, 1)
                        if j % 2:
                            rank(i, 2 * (part == "k") + j // 2)
                for t in range(NT):
                    bank = take_mm("A", ("v", t), i)
                    for k in range(KB):
                        ins = mm(bank, hT[:, k, t * P:(t + 1) * P], wqkv_s[:, k, 2 * D:3 * D],
                                 start=(k == 0), stop=(k == KB - 1))
                    ins.then_inc(mm_full, 1)
                if not last:
                    hT_transposes(i + 1)
                pe.wait_ge(k_made, i * 4 + 4)
                for h in range(PAIRS):
                    for t in range(NT):
                        bank = take_mm("A", ("xp", h, t), i)
                        mm(bank, kT[:, h, t * P:(t + 1) * P], pbd[:, :], start=True, stop=True).then_inc(mm_full, 1)
                    if h >= 1:
                        kv_product(i, h - 1)
                    rank(i, 4 + h)
                kv_product(i, PAIRS - 1)

            hT_transposes(0)
            a_chunk(0)
            with pe.Fori(1, CHUNKS - 1) as i:
                a_chunk(i)
            a_chunk(CHUNKS - 1, last=True)
            pe.sem_inc(phase_done, 1)
            pe.wait_ge(phase_done, 4)
            pe.wait_ge(loaded_wb, 48)

            def seg(i, k):
                s = (i - B1) * SEG + k
                gr = k // GSUP
                if k % GSUP == 0:
                    pe.wait_ge(gathered[gr % GS], (i - B1) * (16 * GT * GROUPS // GS) + (gr // GS + 1) * 16 * GT)
                pe.wait_ge(oh_made, s + 1)
                pe.wait_ge(acc_made, s + 1)
                for t in range(SUP):
                    ins = mm(ps[:, SEG0 + k % 2, :], oh[:, k % 2, t, :], ring[:, gr % GS, (k % GSUP) * SUP + t, :],
                             start=(t == 0), stop=(t == SUP - 1))
                ins.then_inc(seg_full, 1)

            def b_chunk(i, with_seg):
                todo = seg_plan(with_seg)
                done = [0]

                def fill(n):
                    for _ in range(n):
                        seg(i, done[0])
                        done[0] += 1

                def take_tr(made, value):
                    pe.wait_ge(made, value)
                    return ps[:, TR0, :]
                pe.wait_ge(qb_loaded, i * 16 + 16)
                for n in range(B_STEPS):
                    if n < NT * PAIRS:
                        t, h = n // PAIRS, n % PAIRS
                        bank = take_mm("B", ("xp", n), i)
                        mm(bank, qTb[:, h, t * P:(t + 1) * P], pbd[:, :], start=True, stop=True).then_inc(mm_full, 1)
                    fill(min(1, todo[n]))
                    if 1 <= n <= NT * PAIRS:
                        m = n - 1
                        pe.wait_ge(exp_made, i * (NT * PAIRS) + (CHUNKS * NT * PAIRS + m + 1))
                        if m >= 1:
                            pe.wait_ge(qpT_made, i * (NT * PAIRS) + m)
                        if n >= 7 and (n - 7) % 4 == 0:
                            pe.wait_ge(attT_made, i * NT + ((n - 7) // 4 + 1))
                        for r in range(4):
                            ins = tr(ps[:, TR0, r * P:(r + 1) * P], qp[:, m % 2, r * P:(r + 1) * P], ident[:, :])
                        ins.then_inc(tr_full, 1)
                    fill(max(0, todo[n] - 1))
                    if 2 <= n < NT * PAIRS + 2:
                        m = n - 2
                        pe.wait_ge(qpT_made, i * (NT * PAIRS) + (m + 1))
                        if m >= 1:
                            pe.wait_ge(att_made, i * (NT * PAIRS) + m)
                        h = m % PAIRS
                        for e in range(2):
                            for c in range(2):
                                ins = mm(att_reg(m)[:, e, :], qpT[:, m % 2, e * 2 + c, :], kv[:, 2 * h + e, c, :],
                                         start=(c == 0), stop=(c == 1))
                        ins.then_inc(att_full, 1)
                    if n >= 6 and (n - 6) % 4 == 0:
                        t = (n - 6) // 4
                        pe.wait_ge(att_made, i * (NT * PAIRS) + (t * PAIRS + PAIRS))
                        pe.wait_ge(qpT_made, i * (NT * PAIRS) + min(n, NT * PAIRS))
                        for k in range(KB):
                            ins = tr(ps[:, TR0, k * P:(k + 1) * P], att[:, t % 2, k * P:(k + 1) * P], ident[:, :])
                        ins.then_inc(tr_full, 1)
                    if n >= 7 and (n - 7) % 4 == 0:
                        t = (n - 7) // 4
                        pe.wait_ge(attT_made, i * NT + (t + 1))
                        bank = take_mm("B", ("proj", t), i)
                        for k in range(KB):
                            ins = mm(bank, attT[:, t % 2, k, :], wproj_s[:, k, :], start=(k == 0), stop=(k == KB - 1))
                        ins.then_inc(mm_full, 1)
                pe.wait_ge(z2_made, i * NT + NT)
                for k in range(KB):
                    if k >= 1:
                        pe.wait_ge(h2T_made, i * KB + k)
                    for t in range(NT):
                        ins = tr(ps[:, TR0, t * P:(t + 1) * P], z2[:, t, k * P:(k + 1) * P], ident[:, :])
                    ins.then_inc(tr_full, 1)
                    fill(todo[B_STEPS + k])
                pe.wait_ge(h2T_made, i * KB + KB)
                for j in range(JB):
                    bank = take_mm("B", ("up", j), i)
                    for k in range(KB):
                        ins = mm(bank, w1_s[:, k, j * P:(j + 1) * P], h2T[:, k, :], start=(k == 0), stop=(k == KB - 1))
                    ins.then_inc(mm_full, 1)
                    fill(todo[B_STEPS + KB + j])
                pe.wait_ge(gT_made, i * JB + JB)
                for t in range(NT):
                    bank = take_mm("B", ("down", t), i)
                    for j in range(JB):
                        ins = mm(bank, gT[:, j, t * P:(t + 1) * P], w2_s[:, j, :], start=(j == 0), stop=(j == JB - 1))
                    ins.then_inc(mm_full, 1)

            with pe.Fori(0, B1) as i:
                b_chunk(i, False)
            with pe.Fori(B1, CHUNKS) as i:
                b_chunk(i, True)
            pe.sem_inc(phase_done, 1)
            pe.wait_ge(phase_done, 8)
            pe.wait_ge(loaded_wb, 64)
            pe.wait_ge(tril_made, 2 * KB)

            def c_chunk(i, b, r):
                def transposes(part, of, made):
                    for k in range(KB):
                        if k >= 2:
                            pe.wait_ge(made, i * KB + (k - 1))
                        elif part == "z3":
                            pe.wait_ge(aggT_made, i * KB + (k + 3))
                        for t in range(NT):
                            ins = tr(ps[:, TR0 + k % 2, t * P:(t + 1) * P], of[:, t, k * P:(k + 1) * P], ident[:, :])
                        ins.then_inc(tr_full, 1)
                pe.wait_ge(c_loaded[b], r * 48 + 48)
                transposes("agg", aggb[:, b, :, :], aggT_made)
                pe.wait_ge(aggT_made, i * KB + KB)
                for t in range(NT):
                    bank = take_mm("C", ("gnn", t), i)
                    for k in range(KB):
                        ins = mm(bank, aggT[:, k, t * P:(t + 1) * P], wg_s[:, k, :], start=(k == 0), stop=(k == KB - 1))
                    ins.then_inc(mm_full, 1)
                pe.wait_ge(z3_made, i + 1)
                transposes("z3", z3, z3T_made)
                pe.wait_ge(z3T_made, i * KB + KB)
                for j in range(KB):
                    bank = take_mm("C", ("f1", j), i)
                    for k in range(j + 1):
                        ins = mm(bank, f1_s[:, k, j * P:(j + 1) * P], z3T[:, k, :], start=(k == 0), stop=(k == j))
                    ins.then_inc(mm_full, 1)
                pe.wait_ge(fT_made, i * KB + KB)
                for t in range(NT):
                    bank = take_mm("C", ("f2", t), i)
                    for k in range(KB):
                        ins = mm(bank[:, k * P:D], fT[:, k, t * P:(t + 1) * P], f2_s[:, k, k * P:D],
                                 start=(k == 0), stop=(k == KB - 1))
                    ins.then_inc(mm_full, 1)

            with pe.Fori(0, CHUNKS // 2) as r:
                for b in range(2):
                    c_chunk(2 * r + b, b, r)


def kernel(x, src, dst, edge_weight, L0_gnn_weight, L0_mix_Wqkv, L0_mix_bqkv, L0_mix_Pmat, L0_mix_Wproj, L0_mix_bproj,
           L0_mix_W1, L0_mix_b1, L0_mix_W2, L0_mix_b2, L0_mix_g1, L0_mix_be1, L0_mix_g2, L0_mix_be2,
           L0_ffn_W1, L0_ffn_b1, L0_ffn_W2, L0_ffn_b2):
    import numpy as np
    import concourse.bacc as bacc
    from concourse.bass_utils import run_bass_kernel_spmd

    def cols(a):
        return np.asarray(a).reshape(-1, P).T
    given = {"x": x, "src": src, "dst": dst, "ew": edge_weight, "wgT": np.asarray(L0_gnn_weight).T,
             "wqkv": L0_mix_Wqkv, "bqkv": L0_mix_bqkv, "pmat": L0_mix_Pmat, "wproj": L0_mix_Wproj,
             "bproj": L0_mix_bproj, "w1": L0_mix_W1, "b1": cols(L0_mix_b1), "w2": L0_mix_W2, "b2": L0_mix_b2,
             "g1": cols(L0_mix_g1), "be1": cols(L0_mix_be1), "g2": cols(L0_mix_g2), "be2": cols(L0_mix_be2),
             "f1T": np.asarray(L0_ffn_W1).T, "fb1": cols(L0_ffn_b1), "f2T": np.asarray(L0_ffn_W2).T, "fb2": L0_ffn_b2,
             "bqkv_c": cols(L0_mix_bqkv)}
    nc = bacc.Bacc("TRN2", target_bir_lowering=False, num_devices=1)
    arrays, aps = {}, {}
    for name, a in given.items():
        a = np.ascontiguousarray(a)
        arrays["in_" + name] = a
        aps[name] = nc.dram_tensor("in_" + name, a.shape, mybir.dt.from_np(a.dtype), kind="ExternalInput").ap()
    out = nc.dram_tensor("out", (N, D), F32, kind="ExternalOutput").ap()
    build(nc, *aps.values(), out)
    r = run_bass_kernel_spmd(nc, [arrays], core_ids=[0])
    return r.results[0]["out"]
```

```python
import concourse.bass as bass
from concourse import mybir
from contextlib import ExitStack

F32 = mybir.dt.float32
F16 = mybir.dt.float16
I32 = mybir.dt.int32
ALU = mybir.AluOpType
ACT = mybir.ActivationFunctionType
X = mybir.AxisListType.X

P = 128
N, D, E = 8192, 512, 131072
KB = D // P
HEADS, DH, NF = 8, 64, 256
PAIRS = HEADS // 2
HID = 1024
JB = HID // P
EPS = 1e-5
KSUM_EPS = 1e-6
NT = 4
CT = NT * P
CHUNKS = N // CT
VW = DH + 1
WS = 256.0
FS = 2.0 ** 15
PARTS = ((0, 0), (0, 1), (1, 0))
MS = NT * PAIRS

BLOCKS = N // P
COLS = E // P
HALF = COLS // 2
SORT_COLS = 8
CCOLS = COLS // CHUNKS
SORT_STEPS = CCOLS // SORT_COLS
SUP = 2
SUP_EDGES = SUP * P
SUPERS = E // SUP_EDGES + BLOCKS
TILES = SUPERS * SUP
B1 = 4
SEG = SUPERS // (CHUNKS - B1)
GT = 4
GS = 3
GROUPS = SEG * SUP // GT
GSUP = GT // SUP
AR = 4
MMB = 4
PBD_CLEARED, EARLY_CONSTS, ALL_CONSTS = 1, 15, 26
assert SUPERS % (CHUNKS - B1) == 0 and GROUPS % GS == 0 and SEG % AR == 0 and GT % SUP == 0


def order_of(uses):
    return {u: k for k, u in enumerate(uses)}


def some(name, n=4):
    return [(name, k) for k in range(n)]


def a_orders(last):
    z, x = ([], []) if last else (some("z"), some("x"))
    mm = some("q") + some("k") + some("v")
    hi = some("q") + some("k") + some("v") + z
    lo = list(hi)
    for h in range(PAIRS):
        mm += [("e", 4 * h + t) for t in range(NT)] + [("g", h)]
        hi += [("e", 4 * h + t) for t in range(NT)] + [("g", h)]
        lo += [("e", m - 1) for m in range(4 * h, 4 * h + NT) if m] + [("g", h)]
    lo += [("e", MS - 1)] + x
    hi += x
    return order_of(mm), order_of(hi), order_of(lo), order_of(some("q") + some("k") + z + some("e", MS))


A_BODY, A_LAST = a_orders(False), a_orders(True)
MM_A = A_BODY[0]
HL_A0 = 2 * KB
HL_A = len(A_BODY[1])
HL_B0 = HL_A0 + (CHUNKS - 1) * HL_A + len(A_LAST[1])
TR_A = 2 * KB
B_STEPS = MS + 5


def b_orders(first):
    mm, tr = [], []
    for n in range(B_STEPS):
        if n < MS:
            mm.append(("e", n))
        if not first and 1 <= n <= NT:
            mm.append(("down", n - 1))
        if 1 <= n <= MS:
            tr.append(("q", n - 1))
        if n >= 6 and (n - 6) % 4 == 0 and (n - 6) // 4 < NT:
            tr.append(("att", (n - 6) // 4))
        if n >= 7 and (n - 7) % 4 == 0 and (n - 7) // 4 < NT:
            mm.append(("proj", (n - 7) // 4))
    return order_of(mm + some("up", JB)), order_of(tr + some("h"))


MM_B1, TR_B = b_orders(True)
MM_B, _ = b_orders(False)
HL_BT = order_of(some("att") + some("h") + some("up", JB))
HL_B = len(HL_BT)
MM_C = order_of(some("f1") + some("f2"))
HL_CT = order_of(some("z") + some("f"))
MM_B0 = CHUNKS * len(MM_A)
MM_BB = MM_B0 + len(MM_B1) - len(MM_B)
MM_D0 = MM_BB + CHUNKS * len(MM_B)
MM_C0 = MM_D0 + NT
HL_C0 = HL_B0 + CHUNKS * HL_B
TR_B0 = CHUNKS * TR_A
TR_C0 = TR_B0 + CHUNKS * len(TR_B)
for o in (MM_A, MM_B, MM_B1, MM_C, A_BODY[3], A_LAST[3]):
    assert not len(o) % MMB


def seg_plan(with_seg):
    plan = [2] * MS + [1] * (B_STEPS - MS) + [0] * KB + [1] * JB
    plan[B_STEPS - 1] += SEG - sum(plan)
    assert sum(plan) == SEG and min(plan) >= 0
    return plan if with_seg else [0] * len(plan)


def build(nc, x, src, dst, ew, wgT, wqkv, bqkv, pmat, wproj, bproj, w1, b1, w2, b2, g1, be1, g2, be2,
          f1T, fb1, f2T, fb2, bqkv_c, out):
    xn_d = nc.dram_tensor("xn_d", (N, D), F32).ap()
    h_d = nc.dram_tensor("h_d", (N, 2 * D), F16).ap()
    y_d = nc.dram_tensor("y_d", (N, D), F32).ap()
    agg_d = nc.dram_tensor("agg_d", (BLOCKS * P, D), F32).ap()
    qT_d = nc.dram_tensor("qT_d", (P, CHUNKS * 2 * KB * CT), F16).ap()
    slots_d = nc.dram_tensor("slots_d", (P * TILES, 3), F32).ap()
    first_d = nc.dram_tensor("first_d", (2, COLS * BLOCKS), F16).ap()

    rows = lambda a: a.rearrange("(c t p) d -> p c t d", p=P, t=NT)
    x_v, xn_v, y_v, out_v, agg_v, h_v = rows(x), rows(xn_d), rows(y_d), rows(out), rows(agg_d), rows(h_d)
    qT_v = qT_d.rearrange("p (c k) -> p c k", c=CHUNKS)

    with ExitStack() as ctx:
        def sb(name, shape, dt=F32):
            return ctx.enter_context(nc.sbuf_tensor(name, shape, dt))

        def sem(name):
            return ctx.enter_context(nc.semaphore(name))

        def layer(area, size):
            at = [0]

            def lay(*shape, dt=F32):
                n = 1
                for s in shape:
                    n *= s
                words = n if dt != F16 else n // 2
                a = area[:, at[0]:at[0] + words]
                at[0] += words
                assert at[0] <= size, at[0]
                if dt != F32:
                    a = a.bitcast(dt)
                names = "abcde"[:len(shape)]
                if len(shape) > 1:
                    a = a.rearrange(f"p ({' '.join(names)}) -> p {' '.join(names)}", **dict(zip(names, shape)))
                return a
            return at, lay

        ident = sb("ident", [P, P])
        lane_ids = sb("lane_ids", [P, P])
        slots = sb("slots", [P, TILES + 4, 3])
        slots16 = slots[:, :, :].rearrange("p t f -> p (t f)").bitcast(F16).rearrange("p (t f) -> p t f", f=6)
        keep = sb("keep", [P, SUPERS])
        block_of = sb("block_of", [1, SUPERS + 1], I32)
        pbd = sb("pbd", [P, 2, 2 * NF], F16)
        kv = sb("kv", [P, HEADS, 2, VW])
        bq = sb("bq", [P, 4]); bk = sb("bk", [P, 4]); b1c = sb("b1c", [P, JB]); fb1c = sb("fb1c", [P, KB])
        g1c = sb("g1c", [P, KB]); be1c = sb("be1c", [P, KB]); g2c = sb("g2c", [P, KB]); be2c = sb("be2c", [P, KB])
        brow = sb("brow", [P, 2, D])
        bv2 = sb("bv2", [2, D], F16)
        minus = sb("minus", [2, P], F16)
        wproj_s = sb("wproj_s", [P, 2, KB, D], F16)
        w1_s = sb("w1_s", [P, 2, KB, HID], F16)
        w2_s = sb("w2_s", [P, 2, JB, D], F16)
        stats = sb("stats", [P, NT, 6]); mv = sb("mv", [P, NT, 2]); rstd = sb("rstd", [P, NT])
        vpe = sb("vpe", [P, NT]); guess = sb("guess", [P, NT], I32); half_vy = sb("half_vy", [P, NT])
        nmax = sb("nmax", [P, MS, 2]); rden = sb("rden", [P, MS, 2])
        edge = sb("edge", [P, 4 * COLS])
        rec = edge[:, 0:3 * COLS].rearrange("p (c f) -> p c f", f=3)
        rec16 = edge[:, 0:3 * COLS].bitcast(F16).rearrange("p (c f) -> p c f", f=6)
        addr = edge[:, 3 * COLS:4 * COLS].bitcast(I32)
        dsti = addr
        f1_raw = edge[:, 0:KB * D].rearrange("p (k n) -> p k n", k=KB)
        f2_raw = edge[:, KB * D:2 * KB * D].rearrange("p (k n) -> p k n", k=KB)
        stage_rec = sb("stage_rec", [P, CCOLS, 3]); stage_addr = sb("stage_addr", [P, CCOLS], I32)
        stage_dst = sb("stage_dst", [P, SEG * SUP], I32)
        below = sb("below", [P, P], F16)
        hilo = sb("hilo", [P, P], F16)
        ones16 = sb("ones16", [P, P], F16)
        pick = sb("pick", [P, 2 * P], F16)
        block_ids = sb("block_ids", [P, BLOCKS], F16)

        _, lay = layer(slots[:, :, :].rearrange("p t f -> p (t f)"), 3 * (TILES + 4))
        xT = lay(2, KB, CT, dt=F16)
        bucket = lay(COLS, dt=F16)
        onehot = lay(2, SORT_COLS, BLOCKS, dt=F16)
        pos = lay(CCOLS); posi = lay(CCOLS, dt=I32); posl = lay(CCOLS, dt=I32); post = lay(CCOLS, dt=I32)
        ARENA = 30080
        arena = sb("arena", [P, ARENA])
        at, lay = layer(arena, ARENA)
        wqkv_s = lay(2, KB, 3 * D, dt=F16); wg_s = lay(2, KB, D, dt=F16)
        WEIGHTS_END = at[0]
        xz = lay(NT, D); xn = lay(NT, D)
        hT = lay(2, KB, CT, dt=F16); qT = lay(2, 4, CT, dt=F16); kT = lay(2, 4, CT, dt=F16)
        v = lay(2, NT, HEADS, VW, dt=F16)
        kp = lay(2, 2, NT, 2 * NF, dt=F16)
        tmp = lay(MMB, CT)
        hb = lay(2 * NT, D, dt=F16).rearrange("p (t h) n -> p t h n", h=2)
        picked = lay(SORT_COLS, BLOCKS)
        first = lay(2 * SORT_COLS * BLOCKS, dt=F16)
        at[0] = WEIGHTS_END
        raw = lay(JB * D + KB * HID + KB * D)
        bv_raw = lay(D); bv_h = lay(D, dt=F16)
        srci = lay(COLS, dt=I32); ewf = lay(COLS); lanei = lay(COLS, dt=I32)
        ohb = lay(2, COLS, dt=F16)
        count = lay(HALF); runs = lay(2, HALF); firstf = lay(HALF)
        firstT = lay(HALF, dt=I32); hi_i = lay(HALF, dt=I32); lo_i = lay(HALF, dt=I32); hl = lay(2, HALF, dt=F16)
        samehalf = lay(P); otherhalf = lay(P); upto = lay(P)
        sup_i = lay(SUPERS, dt=I32); sup_f = lay(SUPERS); passed = lay(SUPERS, dt=F16)
        blk_f = lay(SUPERS)
        lane_i = lay(P, dt=I32); blkid_i = lay(BLOCKS, dt=I32); blkid_f = lay(BLOCKS); row_f = lay(2)
        tot = lay(2); toti = lay(2, dt=I32); supn = lay(2); ends = lay(2)
        at[0] = 0
        qTb = lay(2, 4, CT, dt=F16); xnb = lay(NT, D)
        qp = lay(2, 2 * NF); qpT = lay(2, 4, P)
        att = lay(2, D); attT = lay(2, 2, KB, P, dt=F16)
        x1 = lay(NT, D); z2 = lay(NT, D)
        h2T = lay(2, KB, CT, dt=F16); gT = lay(2, JB, CT, dt=F16); tmp_b = lay(MMB, CT)
        oh = lay(2 * SUP, 2, P, dt=F16)
        acc = lay(AR, D)
        ring = lay(GS, GT, 2 * D, dt=F16)
        at[0] = 0
        aggb = lay(2, NT, D); yb = lay(2, NT, D); xb = lay(2, NT, D)
        x2 = lay(NT, D); x2b = lay(NT, D); z3 = lay(NT, D)
        z3T = lay(2, KB, CT, dt=F16); fT = lay(2, KB, CT, dt=F16); tmp_c = lay(MMB, CT)
        outb = lay(NT, D)
        f1_s = wproj_s
        f2_s = w1_s[:, :, :, :].rearrange("p h k n -> p (h k n)")[:, 0:2 * KB * D]\
            .rearrange("p (h k n) -> p h k n", h=2, k=KB)

        ps = ctx.enter_context(nc.psum_tensor("ps", [P, 8, 512], F32))
        mm_bank = lambda u: ps[:, u % MMB, :]
        TR0, KV_BANK, RANK_BANK, ATT_BANK, SEG0 = 4, 6, 7, 5, 6
        att_out = ps[:, ATT_BANK, 0:2 * VW].rearrange("p (h e) -> p h e", e=VW)

        names = """loaded_edges loaded_w loaded_w2 consts_made zeroed slots_cleared recs_loaded lanes_made recs_made weights_high weights_low
            counted onehot_made pe_setup dve_setup dve_done first_split first_stored setup_left
            x_loaded xn_made xn_stored z_made first_loaded q_stored h_stored mm_full tr_full hi_made lo_made
            tmp_made max_made exp_made kv_full kv_free rank_full rank_free addr_made staged scattered phase_done
            slots_loaded idle qb_loaded xnb_loaded xb_made qpT_made att_full att_made x1_made z2_made y_made y_stored
            brow_loaded dst_staged oh_made seg_full acc_made acc_saved agg_stored ffn_loaded tril_made ffn_high
            ffn_low x2_made x2b_made yx_made z3_made out_made out_stored out_free""".split()
        S = {n: sem(n) for n in names}
        (loaded_edges, loaded_w, loaded_w2, consts_made, zeroed, slots_cleared, recs_loaded, lanes_made, recs_made, weights_high, weights_low,
         counted, onehot_made, pe_setup, dve_setup, dve_done, first_split, first_stored, setup_left,
         x_loaded, xn_made, xn_stored, z_made, first_loaded, q_stored, h_stored, mm_full, tr_full, hi_made, lo_made,
         tmp_made, max_made, exp_made, kv_full, kv_free, rank_full, rank_free, addr_made, staged, scattered, phase_done,
         slots_loaded, idle, qb_loaded, xnb_loaded, xb_made, qpT_made, att_full, att_made, x1_made, z2_made, y_made,
         y_stored, brow_loaded, dst_staged, oh_made, seg_full, acc_made, acc_saved, agg_stored, ffn_loaded, tril_made,
         ffn_high, ffn_low, x2_made, x2b_made, yx_made, z3_made, out_made, out_stored, out_free) = S.values()
        gathered = [sem(f"gathered{s}") for s in range(GS)]
        c_loaded = [sem(f"c_loaded{s}") for s in range(2)]

        SEG_CREDIT = GS * GSUP
        ACC_CREDIT = 2
        SAVED_CREDIT = AR
        OUT_CREDIT = NT
        LOADS_W = 4 + 8

        def hold(eng, s, value):
            eng.wait_ge(s, value)
            eng.sem_inc(idle, 1)

        def a_val(table, i, key, last=False):
            return i * HL_A + (HL_A0 + (A_LAST if last else A_BODY)[table][key] + 1)

        def zx_low(i, key, table=2):
            if isinstance(i, int) and i == 0:
                return order_of(some("z") + some("x"))[key] + 1
            return i * HL_A + (HL_A0 - HL_A + A_BODY[table][key] + 1)

        def b_val(i, key):
            return i * HL_B + (HL_B0 + HL_BT[key] + 1)

        def c_val(i, key):
            return i * len(HL_CT) + (HL_C0 + HL_CT[key] + 1)

        def mm_a(i, key):
            return i * len(MM_A) + (MM_A[key] + 1)

        def mm_b(i, key):
            first = isinstance(i, int) and i == 0
            return MM_B0 + MM_B1[key] + 1 if first else i * len(MM_B) + (MM_BB + MM_B[key] + 1)

        def mm_down(i, t):
            if isinstance(i, int) and i == CHUNKS - 1:
                return MM_D0 + t + 1
            return (i + 1) * len(MM_B) + (MM_BB + MM_B["down", t] + 1)

        def bank_b(i, key):
            first = isinstance(i, int) and i == 0
            return mm_bank((MM_B1 if first else MM_B)[key])

        class Chain:
            def __init__(self):
                self.base, self.n, self.i, self.per, self.first = 0, 0, None, 0, 0

            def enter(self, i, per, first=0):
                self.base += self.n
                self.i, self.per, self.first, self.n = i, per, first, 0

            def leave(self, times):
                assert self.n == self.per, (self.n, self.per)
                self.base += times * self.per
                self.i, self.n = None, 0

            def step(self, ins):
                ins.then_inc(dve_done, 1)
                self.n += 1
                return ins

            def value(self):
                if self.i is None:
                    return self.base + self.n
                return (self.i - self.first) * self.per + (self.base + self.n)

        block = ctx.enter_context(nc.Block())

        @block.sync
        def _(sp):
            cols = lambda a: a.rearrange("(p c) -> p c", p=P)
            wide = lambda w: w.rearrange("(k p) n -> p k n", p=P)

            def raw_at(start, k, n):
                return raw[:, start:start + k * n].rearrange("p (k n) -> p k n", n=n)
            sp.sem_inc(acc_saved, SAVED_CREDIT)
            sp.dma_start(srci, cols(src)).then_inc(loaded_edges, 16)
            sp.dma_start(raw_at(0, KB, 3 * D), wide(wqkv)).then_inc(loaded_w, 16)
            sp.wait_ge(slots_cleared, 1)
            sp.dma_start(slots_d.rearrange("(p t) f -> p t f", p=P), slots[:, 0:TILES, :]).then_inc(zeroed, 16)
            sp.dma_start(ewf, cols(ew)).then_inc(recs_loaded, 16)
            sp.dma_start(dsti, cols(dst)).then_inc(recs_loaded, 16)
            sp.dma_start(raw_at(KB * 3 * D, KB, D), wide(wgT)).then_inc(loaded_w, 16)
            p0 = KB * 4 * D
            sp.wait_ge(consts_made, PBD_CLEARED)
            sp.dma_start(raw[0:DH, p0:p0 + NF], pmat).then_inc(loaded_w, 16)
            sp.dma_start(raw[DH:P, p0 + NF:p0 + 2 * NF], pmat).then_inc(loaded_w, 16)
            for to, of in ((bq, bqkv_c[:, 0:4]), (bk, bqkv_c[:, 4:8]), (g1c, g1), (be1c, be1), (g2c, g2), (be2c, be2),
                           (b1c, b1), (fb1c, fb1)):
                sp.dma_start(to[:, :], of).then_inc(loaded_w, 16)
            sp.dma_start(bv_raw[0:2, :], bqkv[2 * D:3 * D].partition_broadcast(2)).then_inc(loaded_w2, 16)
            sp.dma_start(brow[:, 0, :], bproj.partition_broadcast(P)).then_inc(brow_loaded, 16)
            sp.dma_start(brow[:, 1, :], b2.partition_broadcast(P)).then_inc(brow_loaded, 16)
            sp.wait_ge(weights_high, 3)
            sp.wait_ge(weights_low, 3)
            sp.dma_start(raw_at(0, KB, HID), wide(w1)).then_inc(loaded_w2, 16)
            sp.dma_start(raw_at(KB * HID, JB, D), wide(w2)).then_inc(loaded_w2, 16)
            sp.dma_start(raw_at(KB * HID + JB * D, KB, D), wide(wproj)).then_inc(loaded_w2, 16)
            sp.wait_ge(first_split, 1)
            for part in range(2):
                for h in range(2):
                    sp.dma_start(first_d[part, :].rearrange("(h k p b) -> h p k b", h=2, p=P, b=BLOCKS)[h],
                                 hl[:, part, :].rearrange("p (k h b) -> p k h b", h=2, b=BLOCKS)[:, :, h, :])\
                        .then_inc(first_stored, 16)
            sp.wait_ge(first_stored, 64)
            sp.wait_ge(setup_left, 2)
            sp.dma_start(xz, x_v[:, 0, :, :]).then_inc(x_loaded, 16)

            def load_first(i):
                for g in range(4):
                    w = 2 * SORT_COLS * BLOCKS
                    sp.dma_start(first[32 * g:32 * g + 2, :], first_d[:, bass.ds(i * (CCOLS * BLOCKS) + g * w, w)])\
                        .then_inc(first_loaded, 16)
            load_first(0)
            sp.wait_ge(xn_made, 1)
            sp.dma_start(xn_v[:, 0, :, :], xn).then_inc(xn_stored, 16)
            sp.wait_ge(tr_full, KB)
            sp.dma_start(xz, x_v[:, 1, :, :]).then_inc(x_loaded, 16)

            def a_chunk(i, load=True, last=False):
                if not last:
                    sp.wait_ge(xn_made, i + 2)
                    sp.dma_start(xn_v[:, i + 1, :, :], xn).then_inc(xn_stored, 16)
                sp.wait_ge(lo_made, a_val(2, i, ("q", 3), last))
                sp.dma_start(qT_v[:, i, :], qT.rearrange("p h k n -> p (h k n)")).then_inc(q_stored, 16)
                if load:
                    sp.wait_ge(tr_full, (i + 1) * TR_A + KB)
                    sp.dma_start(xz, x_v[:, i + 2, :, :]).then_inc(x_loaded, 16)
                sp.wait_ge(lo_made, a_val(2, i, ("g", 3), last))
                sp.dma_start(h_v[:, i, :, :], hb.rearrange("p t h n -> p t (h n)")).then_inc(h_stored, 16)
                if not last:
                    sp.wait_ge(rank_full, i * SORT_STEPS + SORT_STEPS)
                    load_first(i + 1)
            with sp.Fori(0, CHUNKS - 2) as i:
                a_chunk(i)
            a_chunk(CHUNKS - 2, load=False)
            a_chunk(CHUNKS - 1, load=False, last=True)
            for s in (q_stored, xn_stored, h_stored):
                sp.wait_ge(s, 16 * CHUNKS)
            sp.sem_inc(phase_done, 1)
            sp.wait_ge(phase_done, 4)
            sp.dma_start(qTb.rearrange("p h k n -> p (h k n)"), qT_v[:, 0, :]).then_inc(qb_loaded, 16)
            sp.dma_start(xnb, xn_v[:, 0, :, :]).then_inc(xnb_loaded, 16)

            def load_q(i):
                sp.wait_ge(exp_made, (i + 1) * MS + CHUNKS * MS)
                sp.dma_start(qTb.rearrange("p h k n -> p (h k n)"), qT_v[:, (i + 1) % CHUNKS, :]).then_inc(qb_loaded, 16)

            def load_xn(i):
                sp.wait_ge(x1_made, i * NT + NT)
                sp.dma_start(xnb, xn_v[:, (i + 1) % CHUNKS, :, :]).then_inc(xnb_loaded, 16)

            def store_y(i):
                sp.wait_ge(y_made, i * NT + NT)
                sp.dma_start(y_v[:, i, :, :], x1).then_inc(y_stored, 16)
            load_q(0)
            load_xn(0)
            with sp.Fori(1, B1) as i:
                store_y(i - 1)
                load_q(i)
                load_xn(i)
            sp.wait_ge(scattered, 16 * COLS)
            sp.dma_start(slots[:, 0:TILES, :], slots_d.rearrange("(p t) f -> p t f", p=P)).then_inc(slots_loaded, 16)
            sp.dma_start(f1_raw, wide(f1T)).then_inc(ffn_loaded, 16)
            sp.dma_start(f2_raw, wide(f2T)).then_inc(ffn_loaded, 16)

            def flush(i, start, stop):
                with sp.Fori(start // AR, stop // AR) as r:
                    for a in range(AR):
                        s = (i - B1) * SEG + (r * AR + a)
                        sp.wait_ge(acc_made, s + (ACC_CREDIT + 1))
                        here = sp.value_load(block_of[0:1, bass.ds(s, 1)], min_val=0, max_val=BLOCKS - 1)
                        nxt = sp.value_load(block_of[0:1, bass.ds(s + 1, 1)], min_val=0, max_val=BLOCKS)
                        with sp.If(here < nxt):
                            sp.dma_start(agg_d[bass.ds(here * P, P), :], acc[:, a, :]).then_inc(agg_stored, 16)
                            hold(sp, agg_stored, (here + 1) * 16)
                        sp.sem_inc(acc_saved, 1)
            with sp.Fori(B1, CHUNKS) as i:
                flush(i, 0, 2 * AR)
                store_y(i - 1)
                flush(i, 2 * AR, 8 * AR)
                load_q(i)
                flush(i, 8 * AR, SEG)
                load_xn(i)
            store_y(CHUNKS - 1)
            sp.wait_ge(y_stored, 16 * CHUNKS)
            sp.wait_ge(agg_stored, 16 * BLOCKS)
            sp.wait_ge(qb_loaded, 16 * (CHUNKS + 1))
            sp.wait_ge(xnb_loaded, 16 * (CHUNKS + 1))
            sp.sem_inc(phase_done, 1)
            sp.wait_ge(phase_done, 9)
            sp.dma_start(brow[:, 0, :], fb2.partition_broadcast(P)).then_inc(brow_loaded, 16)

            def c_load(i, b):
                sp.dma_start(yb[:, b, :, :], y_v[:, i, :, :]).then_inc(c_loaded[b], 16)
                sp.dma_start(xb[:, b, :, :], x_v[:, i, :, :]).then_inc(c_loaded[b], 16)
                sp.dma_start(aggb[:, b, :, :], agg_v[:, i, :, :]).then_inc(c_loaded[b], 16)

            def c_store(i):
                sp.wait_ge(out_made, i * NT + (OUT_CREDIT + NT))
                sp.dma_start(out_v[:, i, :, :], outb).then_inc(out_stored, 16)
                sp.wait_ge(out_stored, i * 16 + 16)
                sp.sem_inc(out_free, 1)
            sp.sem_inc(out_free, 1)
            c_load(0, 0)
            c_load(1, 1)
            with sp.Fori(0, CHUNKS // 2 - 1) as r:
                for b in range(2):
                    i = 2 * r + b
                    sp.wait_ge(x2_made, i * NT + NT)
                    c_load(i + 2, b)
                    c_store(i)
            c_store(CHUNKS - 2)
            c_store(CHUNKS - 1)
            sp.wait_ge(out_stored, 16 * CHUNKS)

        @block.gpsimd
        def _(pool):
            g = nc.gpsimd
            made = [0]

            def const(ins):
                ins.then_inc(consts_made, 1)
                made[0] += 1
            const(g.memset(raw[:, KB * 4 * D:KB * 4 * D + 2 * NF], 0.0))
            assert made[0] == PBD_CLEARED
            const(g.memset(pick[:, :], 0.0))
            const(g.memset(ident[:, :], 0.0))
            const(g.memset(samehalf, 0.0))
            const(g.memset(otherhalf, 0.0))
            const(g.memset(upto[0:BLOCKS, :], 1.0))
            const(g.memset(below[:, :], 1.0))
            const(g.memset(ones16[:, :], 1.0))
            const(g.memset(hilo[:, :], 1.0))
            const(g.memset(minus[:, :], -1.0))
            const(g.iota(lane_i, pattern=[[1, P]], base=0, channel_multiplier=0))
            const(g.iota(blkid_i, pattern=[[1, BLOCKS]], base=0, channel_multiplier=0))
            const(g.iota(sup_i, pattern=[[1, SUPERS]], base=0, channel_multiplier=0))
            const(g.iota(toti[:, 0:1], pattern=[[1, 1]], base=0, channel_multiplier=1))
            pool.wait_ge(consts_made, made[0])
            const(g.memset(pick[:, P:P + 1], 1.0))
            assert made[0] == EARLY_CONSTS

            def diag(m, base):
                const(g.affine_select(out=m, in_=m, compare_op=ALU.not_equal, fill=1.0, base=base,
                                      pattern=[[-1, P]], channel_multiplier=1))
            diag(ident[:, :], 0)
            diag(samehalf, 0)
            diag(otherhalf, BLOCKS)
            for q in range(4):
                pool.wait_ge(consts_made, made[0])
                const(g.memset(hilo[32 * q:32 * q + 1, :], float(P)))
            pool.wait_ge(consts_made, made[0])
            const(g.affine_select(out=below[:, :], in_=below[:, :], compare_op=ALU.is_gt, fill=0.0, base=0,
                                  pattern=[[1, P]], channel_multiplier=-1))
            halves = upto[0:BLOCKS, :].rearrange("p (a b) -> p a b", a=2)
            const(g.affine_select(out=halves, in_=halves, compare_op=ALU.is_ge, fill=0.0, base=0,
                                  pattern=[[0, 2], [1, BLOCKS]], channel_multiplier=-1))
            pool.wait_ge(consts_made, made[0])
            diag(samehalf, BLOCKS)
            pool.wait_ge(consts_made, made[0])
            diag(samehalf, -BLOCKS)
            assert made[0] == ALL_CONSTS
            pool.wait_ge(recs_loaded, 32)
            g.tensor_copy(rec16[:, :, 2], ewf).then_inc(recs_made, 1)
            g.tensor_copy(rec[:, :, 2].bitcast(I32), dsti).then_inc(recs_made, 1)
            hold(pool, recs_made, 2)
            g.tensor_tensor(rec16[:, :, 3], ewf, rec16[:, :, 2], ALU.subtract).then_inc(recs_made, 1)
            pool.wait_ge(recs_made, 3)
            pool.wait_ge(lanes_made, 1)
            pool.sem_inc(setup_left, 1)
            with pool.Fori(0, CHUNKS) as i:
                hold(pool, addr_made, i + 1)
                g.tensor_copy(stage_rec[:, :, :], rec[:, bass.ds(i * CCOLS, CCOLS), :]).then_inc(staged, 1)
                g.tensor_copy(stage_addr[:, :], addr[:, bass.ds(i * CCOLS, CCOLS)]).then_inc(staged, 1)
                hold(pool, staged, 2 * i + 2)
                for c in range(CCOLS):
                    pool.indirect_dma_start(
                        out=slots_d, out_offset=bass.IndirectOffsetOnAxis(ap=stage_addr[:, c:c + 1], axis=0),
                        in_=stage_rec[:, c, :], in_offset=None).then_inc(scattered, 16)
                hold(pool, scattered, (i + 1) * (16 * CCOLS))
            pool.wait_ge(phase_done, 4)
            pool.wait_ge(slots_loaded, 16)
            with pool.Fori(0, CHUNKS - B1) as i:
                g.tensor_copy(stage_dst[:, :], slots[:, bass.ds(i * (SEG * SUP), SEG * SUP), 2].bitcast(I32))\
                    .then_inc(dst_staged, 1)
                hold(pool, dst_staged, i + 1)
                for gr in range(GROUPS):
                    hold(pool, seg_full, i * SEG + (GSUP * gr + GSUP))
                    for t in range(GT):
                        c = gr * GT + t
                        pool.indirect_dma_start(
                            out=ring[:, gr % GS, t, :], out_offset=None, in_=h_d,
                            in_offset=bass.IndirectOffsetOnAxis(ap=stage_dst[:, c:c + 1], axis=0))\
                            .then_inc(gathered[gr % GS], 16)
                for s in range(GS):
                    hold(pool, gathered[s], (i + 1) * (16 * GT * GROUPS // GS))
            pool.wait_ge(ffn_loaded, 32)
            for m in (f1_raw, f2_raw):
                for k in range(KB):
                    tri = m[:, k, k * P:(k + 1) * P]
                    g.affine_select(out=tri, in_=tri, compare_op=ALU.is_ge, fill=0.0, base=0, pattern=[[1, P]],
                                    channel_multiplier=-1).then_inc(tril_made, 1)
            pool.sem_inc(phase_done, 1)
            pool.wait_ge(phase_done, 9)
            pool.wait_ge(brow_loaded, 48)

            def add_x(i, b, r):
                hold(pool, c_loaded[b], r * 48 + 48)
                g.tensor_tensor(yb[:, b, :, :], yb[:, b, :, :], xb[:, b, :, :], ALU.add).then_inc(yx_made, 1)

            def add_bias(i):
                hold(pool, x2_made, i * NT + NT)
                hold(pool, out_made, i * NT + OUT_CREDIT)
                g.tensor_tensor(x2b, x2, brow[:, 0, :].unsqueeze(1).broadcast_to([P, NT, D]), ALU.add)\
                    .then_inc(x2b_made, 1)
            add_x(0, 0, 0)
            add_bias(0)
            add_x(1, 1, 0)
            with pool.Fori(0, CHUNKS // 2 - 1) as r:
                for b in range(2):
                    i = 2 * r + b
                    add_bias(i + 1)
                    add_x(i + 2, b, r + 1)
            add_bias(CHUNKS - 1)

        @block.scalar
        def _(act):
            a = nc.scalar

            def weights(to, of, s, scale=WS):
                a.activation(to, of, ACT.Copy, scale=scale).then_inc(s, 1)
            act.wait_ge(loaded_w, 16 * LOADS_W)
            c0, c1 = KB * 3 * D, KB * 4 * D
            flat = lambda w: w.rearrange("p k n -> p (k n)")
            weights(flat(wqkv_s[:, 0]), raw[:, 0:c0], weights_high)
            weights(flat(wg_s[:, 0]), raw[:, c0:c1], weights_high)
            weights(pbd[:, 0, :], raw[:, c1:c1 + 2 * NF], weights_high, 1.0)
            act.wait_ge(loaded_w2, 64)
            c0, c1 = KB * HID, KB * HID + JB * D
            weights(flat(w1_s[:, 0]), raw[:, 0:c0], weights_high)
            weights(flat(w2_s[:, 0]), raw[:, c0:c1], weights_high)
            weights(flat(wproj_s[:, 0]), raw[:, c1:c1 + KB * D], weights_high)
            act.wait_ge(setup_left, 2)

            def both(t_slot, high, of, func, **kw):
                a.activation(t_slot, of, func, **kw).then_inc(tmp_made, 1)
                a.activation(high, of, func, **kw).then_inc(hi_made, 1)

            def z_high(i, k):
                act.wait_ge(tr_full, i * TR_A + (k + 1))
                both(tmp[:, k, :], hT[:, 0, k, :], ps[:, TR0 + k % 2, :], ACT.Identity, bias=be1c[:, k:k + 1],
                     scale=g1c[:, k:k + 1])

            def x_high(i, k):
                act.wait_ge(tr_full, i * TR_A + (KB + k + 1))
                a.activation(xT[:, 0, k, :], ps[:, TR0 + k % 2, :], ACT.Copy).then_inc(hi_made, 1)
            for k in range(KB):
                z_high(0, k)
            for k in range(KB):
                x_high(0, k)

            def a_chunk(i, last=False):
                mm, hi, lo, tm = A_LAST if last else A_BODY
                tmps = list(tm)

                def slot(key):
                    u = tm[key]
                    if u >= MMB:
                        hold(act, lo_made, a_val(2, i, tmps[u - MMB], last))
                    elif isinstance(i, int) and i == 0:
                        act.wait_ge(lo_made, u + 1)
                    else:
                        hold(act, lo_made, a_val(2, i - 1, ("e", MS - MMB + u)))
                    return tmp[:, u % MMB, :]
                later = not (isinstance(i, int) and i == 0)
                if later:
                    hold(act, q_stored, i * 16)
                for part, to, bias in (("q", qT, bq), ("k", kT, bk)):
                    for j in range(4):
                        s = slot((part, j))
                        act.wait_ge(mm_full, mm_a(i, (part, j)))
                        both(s, to[:, 0, j, :], mm_bank(MM_A[part, j]), ACT.Identity, bias=bias[:, j:j + 1],
                             scale=1.0 / WS)
                for t in range(NT):
                    act.wait_ge(mm_full, mm_a(i, ("v", t)))
                    a.activation(v[:, 0, t, :, 0:DH], mm_bank(MM_A["v", t]).rearrange("p (h e) -> p h e", e=DH),
                                 ACT.Copy, scale=1.0 / WS).then_inc(hi_made, 1)
                if not last:
                    for k in range(KB):
                        act.wait_ge(tr_full, (i + 1) * TR_A + (k + 1))
                        s = slot(("z", k))
                        both(s, hT[:, 0, k, :], ps[:, TR0 + k % 2, :], ACT.Identity, bias=be1c[:, k:k + 1],
                             scale=g1c[:, k:k + 1])
                for h in range(PAIRS):
                    for t in range(NT):
                        m = NT * h + t
                        s = slot(("e", m))
                        hold(act, max_made, i * MS + (m + 1))
                        for e in range(2):
                            ins = a.activation(s[:, e * NF:(e + 1) * NF],
                                               mm_bank(MM_A["e", m])[:, e * NF:(e + 1) * NF], ACT.Exp,
                                               bias=nmax[:, m, e:e + 1])
                        ins.then_inc(exp_made, 1)
                        act.wait_ge(exp_made, i * MS + (m + 1))
                        a.activation(kp[:, h % 2, 0, t, :], s, ACT.Copy, scale=FS).then_inc(hi_made, 1)
                    if h == 0 and later:
                        hold(act, h_stored, i * 16)
                    act.wait_ge(mm_full, mm_a(i, ("g", h)))
                    a.activation(hb[:, h, 0, :], mm_bank(MM_A["g", h]), ACT.Copy, scale=1.0 / WS).then_inc(hi_made, 1)
                if not last:
                    for k in range(KB):
                        x_high(i + 1, k)
            a_chunk(0)
            with act.Fori(1, CHUNKS - 1) as i:
                a_chunk(i)
            a_chunk(CHUNKS - 1, last=True)
            act.sem_inc(phase_done, 1)
            act.wait_ge(phase_done, 4)

            def b_chunk(i):
                first = isinstance(i, int) and i == 0
                for n in range(B_STEPS):
                    if n < MS:
                        act.wait_ge(max_made, i * MS + (CHUNKS * MS + n + 1))
                        for e in range(2):
                            ins = a.activation(qp[:, n % 2, e * NF:(e + 1) * NF],
                                               bank_b(i, ("e", n))[:, e * NF:(e + 1) * NF], ACT.Exp,
                                               bias=nmax[:, n, e:e + 1])
                        ins.then_inc(exp_made, 1)
                    if 1 <= n <= MS:
                        m = n - 1
                        if m >= 2:
                            hold(act, att_full, i * MS + (m - 1))
                        act.wait_ge(tr_full, i * len(TR_B) + (TR_B0 + TR_B["q", m] + 1))
                        a.activation(qpT[:, m % 2, :, :], ps[:, TR0, :], ACT.Copy).then_inc(qpT_made, 1)
                    if ("att", (n - 6) // 4) in TR_B and (n - 6) % 4 == 0:
                        t = (n - 6) // 4
                        if t >= 2:
                            hold(act, mm_full, mm_b(i, ("proj", t - 2)))
                        act.wait_ge(tr_full, i * len(TR_B) + (TR_B0 + TR_B["att", t] + 1))
                        a.activation(attT[:, t % 2, 0, :, :], ps[:, TR0, :], ACT.Copy).then_inc(hi_made, 1)

                def slot(u):
                    if u >= MMB:
                        key = ("h", u - MMB) if u < 2 * MMB else ("up", u - 2 * MMB)
                        hold(act, lo_made, b_val(i, key))
                    elif not first:
                        hold(act, lo_made, b_val(i - 1, ("up", JB - MMB + u)))
                    return tmp_b[:, u % MMB, :]
                for k in range(KB):
                    s = slot(k)
                    act.wait_ge(tr_full, i * len(TR_B) + (TR_B0 + TR_B["h", k] + 1))
                    both(s, h2T[:, 0, k, :], ps[:, TR0, :], ACT.Identity, bias=be2c[:, k:k + 1], scale=g2c[:, k:k + 1])
                for j in range(JB):
                    s = slot(KB + j)
                    act.wait_ge(mm_full, mm_b(i, ("up", j)))
                    both(s, gT[:, 0, j, :], bank_b(i, ("up", j)), ACT.Gelu, bias=b1c[:, j:j + 1], scale=1.0 / WS)
            b_chunk(0)
            with act.Fori(1, CHUNKS) as i:
                b_chunk(i)
            act.wait_ge(tril_made, 2 * KB)
            act.wait_ge(mm_full, MM_D0)
            weights(flat(f1_s[:, 0]), flat(f1_raw), ffn_high)
            weights(flat(f2_s[:, 0]), flat(f2_raw), ffn_high)
            act.sem_inc(phase_done, 1)
            act.wait_ge(phase_done, 9)

            with act.Fori(0, CHUNKS) as i:
                for k in range(KB):
                    act.wait_ge(tr_full, i * KB + (TR_C0 + k + 1))
                    a.activation(z3T[:, 0, k, :], ps[:, TR0 + k % 2, :], ACT.Copy).then_inc(hi_made, 1)
                for j in range(KB):
                    u = MM_C["f1", j]
                    act.wait_ge(mm_full, i * len(MM_C) + (MM_C0 + u + 1))
                    both(tmp_c[:, j, :], fT[:, 0, j, :], mm_bank(u), ACT.Gelu, bias=fb1c[:, j:j + 1], scale=1.0 / WS)

        @block.vector
        def _(dve):
            vec = nc.vector
            ch = Chain()

            def link(ins):
                ch.step(ins)
                hold(dve, dve_done, ch.value())

            def settle():
                hold(dve, dve_done, ch.value())

            dve.sem_inc(kv_free, 1)
            dve.sem_inc(rank_free, 1)
            dve.sem_inc(acc_made, ACC_CREDIT)
            dve.sem_inc(out_made, OUT_CREDIT)
            link(vec.memset(slots[:, :, :], 0.0))
            dve.sem_inc(slots_cleared, 1)
            vec.memset(kv[:, :, :, :], 0.0)
            vec.memset(keep[:, 0:1], 0.0)
            vec.memset(block_of[0:1, SUPERS:SUPERS + 1], BLOCKS)
            dve.wait_ge(consts_made, EARLY_CONSTS)
            vec.tensor_copy(lane_ids[:, :], lane_i)
            vec.tensor_copy(block_ids[:, :], blkid_i)
            vec.tensor_copy(blkid_f, blkid_i)
            vec.tensor_copy(row_f[:, 0:1], toti[:, 0:1])
            vec.tensor_copy(sup_f, sup_i)
            dve.wait_ge(loaded_edges, 16)
            link(vec.tensor_scalar(lanei, srci, P - 1, None, ALU.bitwise_and))
            link(vec.tensor_scalar(srci, srci, 7, None, ALU.logical_shift_right))
            dve.wait_ge(zeroed, 16)
            link(vec.tensor_copy(bucket, srci))
            vec.tensor_copy(rec[:, :, 0], lanei).then_inc(lanes_made, 1)

            def one_block(k, b):
                return vec.tensor_scalar(ohb[:, b, :], bucket, blkid_f[:, bass.ds(k, 1)], None, ALU.is_equal)\
                    .then_inc(onehot_made, 1)
            one_block(0, 0)
            one_block(1, 1)
            with dve.Fori(1, BLOCKS // 2) as r:
                for b in range(2):
                    hold(dve, counted, r * 2 + (b - 1))
                    one_block(2 * r + b, b)

            def low(to, of, high, s, scale=WS):
                vec.scalar_tensor_tensor(to, of, scale, high, ALU.mult, ALU.subtract).then_inc(s, 1)
            flat = lambda w: w.rearrange("p k n -> p (k n)")
            c0, c1 = KB * 3 * D, KB * 4 * D
            dve.wait_ge(weights_high, 3)
            low(flat(wqkv_s[:, 1]), raw[:, 0:c0], flat(wqkv_s[:, 0]), weights_low)
            low(flat(wg_s[:, 1]), raw[:, c0:c1], flat(wg_s[:, 0]), weights_low)
            low(pbd[:, 1, :], raw[:, c1:c1 + 2 * NF], pbd[:, 0, :], weights_low, 1.0)
            dve.wait_ge(counted, BLOCKS + 1)
            vec.memset(runs[:, 0, 0:1], 0.0)
            vec.tensor_copy(runs[:, 0, 1:HALF], ps[:, RANK_BANK, 0:HALF - 1])
            link(vec.tensor_copy(count, ps[:, RANK_BANK, :]))
            k, d = 0, 1
            while d < HALF:
                vec.tensor_copy(runs[:, 1 - k, 0:d], runs[:, k, 0:d])
                link(vec.tensor_tensor(runs[:, 1 - k, d:HALF], runs[:, k, d:HALF], runs[:, k, 0:HALF - d], ALU.add))
                k, d = 1 - k, 2 * d
            vec.tensor_tensor(tot[:, 0:1], runs[:, k, HALF - 1:HALF], count[:, HALF - 1:HALF], ALU.add)\
                .then_inc(dve_setup, 1)
            dve.wait_ge(pe_setup, 1)
            vec.tensor_copy(tot[:, 1:2], ps[:, 5, 0:1])
            link(vec.tensor_scalar(toti[:, 0:1], ps[:, 6, 0:1], float(SUP_EDGES - 1), None, ALU.add))
            link(vec.tensor_scalar(toti[:, 1:2], toti[:, 0:1], 8, None, ALU.logical_shift_right))
            vec.tensor_scalar(supn[:, 0:1], toti[:, 1:2], 1.0, None, ALU.max).then_inc(dve_setup, 1)
            dve.wait_ge(pe_setup, 2)
            link(vec.tensor_copy(ends[:, 0:1], ps[:, 4, 0:1]))
            link(vec.tensor_tensor(ends[:, 1:2], ends[:, 0:1], supn[:, 0:1], ALU.subtract))
            link(vec.scalar_tensor_tensor(ends[:, 1:2], ends[:, 1:2], float(SUP_EDGES), tot[:, 1:2],
                                          ALU.mult, ALU.add))
            vec.tensor_scalar(passed[0:BLOCKS, :], sup_f[0:BLOCKS, :], ends[0:BLOCKS, 0:1], None, ALU.is_ge)
            vec.tensor_scalar(firstf, runs[:, k, :], ends[:, 1:2], None, ALU.add).then_inc(dve_setup, 1)
            dve.wait_ge(pe_setup, 3)
            half = SUPERS // 2
            for h in range(2):
                vec.tensor_scalar(blk_f[:, h * half:(h + 1) * half], ps[:, 2 + h, 0:half], float(BLOCKS - 1), None,
                                  ALU.min)
            link(vec.tensor_copy(firstT, ps[:, 0, :]))
            vec.tensor_tensor(keep[:, 1:SUPERS], blk_f[:, 1:SUPERS], blk_f[:, 0:SUPERS - 1], ALU.is_equal)
            vec.tensor_copy(block_of[0:1, 0:SUPERS], blk_f[0:1, :])
            vec.tensor_scalar(hi_i, firstT, 7, None, ALU.logical_shift_right)
            link(vec.tensor_scalar(lo_i, firstT, P - 1, None, ALU.bitwise_and))
            vec.tensor_copy(hl[:, 0, :], hi_i)
            vec.tensor_copy(hl[:, 1, :], lo_i).then_inc(first_split, 1)
            dve.wait_ge(loaded_w2, 64)
            link(vec.tensor_scalar(bv_raw[0:2, :], bv_raw[0:2, :], WS, None, ALU.mult))
            link(vec.tensor_copy(bv_h[0:2, :], bv_raw[0:2, :]))
            link(vec.scalar_tensor_tensor(bv2[:, :], bv_h[0:2, :], row_f[0:2, 0:1], bv_raw[0:2, :],
                                          ALU.mult, ALU.subtract))
            dve.wait_ge(weights_high, 6)
            c0, c1 = KB * HID, KB * HID + JB * D
            low(flat(w1_s[:, 1]), raw[:, 0:c0], flat(w1_s[:, 0]), weights_low)
            low(flat(w2_s[:, 1]), raw[:, c0:c1], flat(w2_s[:, 0]), weights_low)
            low(flat(wproj_s[:, 1]), raw[:, c1:c1 + KB * D], flat(wproj_s[:, 0]), weights_low)
            dve.wait_ge(weights_low, 6)
            dve.wait_ge(first_stored, 64)
            dve.sem_inc(setup_left, 1)
            dve.wait_ge(setup_left, 2)
            vec.memset(v[:, 0, :, :, :], 1.0)
            link(vec.memset(v[:, 1, :, :, :], 0.0))

            def inverse_root():
                link(vec.tensor_scalar(vpe[:, :], mv[:, :, 1], EPS, None, ALU.add))
                link(vec.tensor_scalar(guess[:, :], vpe[:, :].bitcast(I32), 1, None, ALU.logical_shift_right))
                link(vec.tensor_scalar(rstd[:, :].bitcast(I32), guess[:, :], -1.0, float(0x5F3759DF),
                                       ALU.mult, ALU.add))
                for _ in range(3):
                    link(vec.scalar_tensor_tensor(half_vy[:, :], rstd[:, :], -0.5, rstd[:, :], ALU.mult, ALU.mult))
                    link(vec.tensor_tensor(half_vy[:, :], half_vy[:, :], vpe[:, :], ALU.mult))
                    link(vec.scalar_tensor_tensor(rstd[:, :], half_vy[:, :], 1.5, rstd[:, :], ALU.add, ALU.mult))

            def normalise(to, of):
                for t in range(NT):
                    last = vec.bn_stats(stats[:, t, :], of[:, t, :])
                link(last)
                for t in range(NT):
                    last = vec.bn_aggr(mv[:, t, :], stats[:, t, :])
                link(last)
                inverse_root()
                for t in range(NT):
                    last = vec.tensor_scalar(to[:, t, :], of[:, t, :], mv[:, t, 0:1], rstd[:, t:t + 1],
                                             ALU.subtract, ALU.mult)
                return last

            def norm_x(i):
                hold(dve, x_loaded, (i + 1) * 16)
                if not (isinstance(i, int) and i == 0):
                    hold(dve, xn_stored, i * 16)
                    hold(dve, tr_full, i * TR_A)
                normalise(xn, xz).then_inc(xn_made, 1)
                hold(dve, xn_made, i + 1)

            def norm_z(i):
                normalise(xz, xn).then_inc(z_made, 1)
                hold(dve, z_made, i + 1)

            def rank_onehot(i, r):
                vec.tensor_tensor(
                    onehot[:, r % 2, :, :],
                    bucket[:, bass.ds(i * CCOLS + r * SORT_COLS, SORT_COLS)].unsqueeze(2)
                    .broadcast_to([P, SORT_COLS, BLOCKS]),
                    block_ids[:, :].unsqueeze(1).broadcast_to([P, SORT_COLS, BLOCKS]), ALU.is_equal)\
                    .then_inc(onehot_made, 1)

            def rank(i, r):
                hold(dve, rank_full, i * SORT_STEPS + (r + 1))
                settle()
                vec.tensor_tensor(picked, ps[:, RANK_BANK, :].rearrange("p (c b) -> p c b", b=BLOCKS),
                                  onehot[:, r % 2, :, :], ALU.mult).then_inc(rank_free, 1)
                hold(dve, rank_free, i * SORT_STEPS + (r + 2))
                ch.step(vec.tensor_reduce(pos[:, r * SORT_COLS:(r + 1) * SORT_COLS], picked, X, ALU.add))
                if r + 2 < SORT_STEPS:
                    rank_onehot(i, r + 2)

            def z_low(i, k, slot, value):
                hold(dve, hi_made, value)
                vec.tensor_tensor(hT[:, 1, k, :], tmp[:, slot, :], hT[:, 0, k, :], ALU.subtract).then_inc(lo_made, 1)

            def x_low(i, k, value):
                hold(dve, hi_made, value)
                vec.tensor_tensor(xT[:, 1, k, :], ps[:, TR0 + k % 2, :], xT[:, 0, k, :], ALU.subtract)\
                    .then_inc(lo_made, 1)
            norm_x(0)
            norm_z(0)
            for k in range(KB):
                z_low(0, k, k, k + 1)
            for k in range(KB):
                x_low(0, k, KB + k + 1)

            def kv_add(i, h):
                hold(dve, kv_full, i * PAIRS + (h + 1))
                to = kv[:, 2 * h:2 * h + 2, :, :].rearrange("p h c e -> p (h c e)")
                vec.scalar_tensor_tensor(to, ps[:, KV_BANK, 0:4 * VW], 1.0 / (FS * float(NF) ** 0.5), to,
                                         ALU.mult, ALU.add).then_inc(kv_free, 1)

            def a_chunk(i, last=False):
                mm, hi, lo, tm = A_LAST if last else A_BODY
                high = lambda key: a_val(1, i, key, last)
                settle()
                rank_onehot(i, 0)
                rank_onehot(i, 1)
                if not last:
                    norm_x(i + 1)

                def qk_low(part, to, j):
                    hold(dve, hi_made, high((part, j)))
                    vec.tensor_tensor(to[:, 1, j, :], tmp[:, tm[part, j] % MMB, :], to[:, 0, j, :], ALU.subtract)\
                        .then_inc(lo_made, 1)
                for j in range(4):
                    qk_low("q", qT, j)
                    if j % 2:
                        rank(i, j // 2)
                if not last:
                    norm_z(i + 1)
                for j in range(4):
                    qk_low("k", kT, j)
                    if j % 2:
                        rank(i, 2 + j // 2)
                for t in range(NT):
                    hold(dve, hi_made, high(("v", t)))
                    vec.scalar_tensor_tensor(v[:, 1, t, :, 0:DH],
                                             mm_bank(MM_A["v", t]).rearrange("p (h e) -> p h e", e=DH), 1.0 / WS,
                                             v[:, 0, t, :, 0:DH], ALU.mult, ALU.subtract).then_inc(lo_made, 1)
                if not last:
                    for k in range(KB):
                        z_low(i + 1, k, tm["z", k] % MMB, high(("z", k)))

                def e_low(m):
                    hold(dve, hi_made, high(("e", m)))
                    vec.scalar_tensor_tensor(kp[:, m // NT % 2, 1, m % NT, :], tmp[:, tm["e", m] % MMB, :], FS,
                                             kp[:, m // NT % 2, 0, m % NT, :], ALU.mult, ALU.subtract)\
                        .then_inc(lo_made, 1)
                for h in range(PAIRS):
                    for t in range(NT):
                        m = NT * h + t
                        hold(dve, mm_full, mm_a(i, ("e", m)))
                        vec.tensor_reduce(nmax[:, m, :], mm_bank(MM_A["e", m]).rearrange("p (e f) -> p e f", e=2),
                                          X, ALU.max, negate=True).then_inc(max_made, 1)
                        if m:
                            e_low(m - 1)
                    hold(dve, hi_made, high(("g", h)))
                    vec.scalar_tensor_tensor(hb[:, h, 1, :], mm_bank(MM_A["g", h]), 1.0 / WS, hb[:, h, 0, :],
                                             ALU.mult, ALU.subtract).then_inc(lo_made, 1)
                    if h >= 1:
                        kv_add(i, h - 1)
                    rank(i, PAIRS + h)
                e_low(MS - 1)
                if not last:
                    for k in range(KB):
                        x_low(i + 1, k, high(("x", k)))
                settle()
                link(vec.tensor_copy(posi, pos))
                vec.tensor_scalar(posl, posi, P - 1, None, ALU.bitwise_and)
                link(vec.tensor_scalar(post, posi, 7, None, ALU.logical_shift_right))
                vec.scalar_tensor_tensor(addr[:, bass.ds(i * CCOLS, CCOLS)], posl, float(TILES), post,
                                         ALU.mult, ALU.add).then_inc(addr_made, 1)
                hold(dve, addr_made, i + 1)
                kv_add(i, PAIRS - 1)
                hold(dve, kv_free, i * PAIRS + (PAIRS + 1))

            ROOT = 3 + 3 * 3
            A_LINKS = 2 * (2 + ROOT) + SORT_STEPS + 2
            ch.enter(0, A_LINKS)
            a_chunk(0)
            ch.leave(1)
            with dve.Fori(1, CHUNKS - 1) as i:
                ch.enter(i, A_LINKS, 1)
                a_chunk(i)
            ch.leave(CHUNKS - 2)
            a_chunk(CHUNKS - 1, last=True)
            link(vec.tensor_scalar(kv[:, :, :, DH:VW], kv[:, :, :, DH:VW], KSUM_EPS, None, ALU.add))
            dve.sem_inc(phase_done, 1)
            dve.wait_ge(phase_done, 4)
            link(vec.memset(acc[:, AR - 1, :], 0.0))
            dve.wait_ge(brow_loaded, 32)

            def make_oh(s, b):
                for t in range(SUP):
                    c = s * SUP + t
                    w = slots16[:, bass.ds(c, 1), 2:4].rearrange("p a h -> p (a h)")
                    last = vec.scalar_tensor_tensor(
                        oh[:, b * SUP + t, :, :], lane_ids[:, :].unsqueeze(1).broadcast_to([P, 2, P]),
                        slots[:, bass.ds(c, 1), 0], w.unsqueeze(2).broadcast_to([P, 2, P]), ALU.is_equal, ALU.mult)
                last.then_inc(oh_made, 1)

            def seg(i, k):
                s = (i - B1) * SEG + k
                hold(dve, seg_full, s + (SEG_CREDIT + 1))
                hold(dve, acc_saved, s + 1)
                hold(dve, acc_made, s + ACC_CREDIT)
                vec.scalar_tensor_tensor(acc[:, k % AR, :], acc[:, (k - 1) % AR, :], keep[:, bass.ds(s, 1)],
                                         ps[:, SEG0 + k % 2, :], ALU.mult, ALU.add).then_inc(acc_made, 1)
                make_oh(s + 2, k % 2)

            def take_down(i, t):
                dve.wait_ge(mm_full, mm_down(i, t))
                bank = mm_bank(t) if isinstance(i, int) and i == CHUNKS - 1 else mm_bank(MM_B["down", t])
                vec.scalar_tensor_tensor(x1[:, t, :], bank, 1.0 / WS, x1[:, t, :], ALU.mult, ALU.add)\
                    .then_inc(y_made, 1)

            def b_chunk(i, with_seg):
                first = isinstance(i, int) and i == 0
                todo = seg_plan(with_seg)
                done = [0]

                def fill(n):
                    for _ in range(n):
                        seg(i, done[0])
                        done[0] += 1
                for n in range(B_STEPS):
                    if n < MS:
                        dve.wait_ge(mm_full, mm_b(i, ("e", n)))
                        vec.tensor_reduce(nmax[:, n, :], bank_b(i, ("e", n)).rearrange("p (e f) -> p e f", e=2),
                                          X, ALU.max, negate=True).then_inc(max_made, 1)
                    if not first and 2 <= n <= NT + 1:
                        take_down(i - 1, n - 2)
                    if 3 <= n < MS + 3:
                        m = n - 3
                        t, h = m // PAIRS, m % PAIRS
                        hold(dve, att_full, i * MS + (m + 1))
                        link(vec.reciprocal(rden[:, m, :], att_out[:, :, DH]))
                        vec.tensor_tensor(att[:, t % 2, h * P:(h + 1) * P].rearrange("p (h e) -> p h e", e=DH),
                                          att_out[:, :, 0:DH], rden[:, m, :].unsqueeze(2).broadcast_to([P, 2, DH]),
                                          ALU.mult).then_inc(att_made, 1)
                    if n == 6:
                        hold(dve, xnb_loaded, i * 16 + 16)
                        vec.tensor_tensor(xnb, xnb, brow[:, 0, :].unsqueeze(1).broadcast_to([P, NT, D]), ALU.add)\
                            .then_inc(xb_made, 1)
                    if n >= 8 and n % 4 == 0:
                        t = n // 4 - 2
                        u = ("proj", t)
                        if t == 0:
                            hold(dve, xb_made, i + 1)
                            if not first:
                                hold(dve, y_stored, i * 16)
                        dve.wait_ge(mm_full, mm_b(i, u))
                        vec.scalar_tensor_tensor(x1[:, t, :], bank_b(i, u), 1.0 / WS, xnb[:, t, :],
                                                 ALU.mult, ALU.add).then_inc(x1_made, 1)
                        hold(dve, x1_made, i * NT + (t + 1))
                        link(vec.bn_stats(stats[:, t, :], x1[:, t, :]))
                        link(vec.bn_aggr(mv[:, t, :], stats[:, t, :]))
                        if t == NT - 1:
                            inverse_root()
                            for k in range(NT):
                                vec.tensor_scalar(z2[:, k, :], x1[:, k, :], mv[:, k, 0:1], rstd[:, k:k + 1],
                                                  ALU.subtract, ALU.mult).then_inc(z2_made, 1)
                            hold(dve, z2_made, i * NT + NT)
                            link(vec.tensor_tensor(x1, x1, brow[:, 1, :].unsqueeze(1).broadcast_to([P, NT, D]),
                                                   ALU.add))
                    fill(todo[n])
                    if n >= 6 and (n - 6) % 4 == 0 and (n - 6) // 4 < NT:
                        t = (n - 6) // 4
                        hold(dve, hi_made, b_val(i, ("att", t)))
                        vec.tensor_tensor(attT[:, t % 2, 1, :, :].rearrange("p k n -> p (k n)"), ps[:, TR0, :],
                                          attT[:, t % 2, 0, :, :].rearrange("p k n -> p (k n)"), ALU.subtract)\
                            .then_inc(lo_made, 1)
                for part, to, count_, u0 in (("h", h2T, KB, 0), ("up", gT, JB, KB)):
                    for k in range(count_):
                        hold(dve, hi_made, b_val(i, (part, k)))
                        vec.tensor_tensor(to[:, 1, k, :], tmp_b[:, (u0 + k) % MMB, :], to[:, 0, k, :], ALU.subtract)\
                            .then_inc(lo_made, 1)
                        fill(todo[B_STEPS + u0 + k])

            B_LINKS = MS + 2 * NT + ROOT + 1
            ch.enter(0, B_LINKS)
            b_chunk(0, False)
            ch.leave(1)
            with dve.Fori(1, B1) as i:
                ch.enter(i, B_LINKS, 1)
                b_chunk(i, False)
            ch.leave(B1 - 1)
            dve.wait_ge(slots_loaded, 16)
            link(vec.memset(slots[:, TILES:TILES + 4, :], 0.0))
            make_oh(0, 0)
            make_oh(1, 1)
            with dve.Fori(B1, CHUNKS) as i:
                ch.enter(i, B_LINKS, B1)
                b_chunk(i, True)
            ch.leave(CHUNKS - B1)
            dve.wait_ge(ffn_high, 2)
            low(flat(f1_s[:, 1]), flat(f1_raw), flat(f1_s[:, 0]), ffn_low)
            low(flat(f2_s[:, 1]), flat(f2_raw), flat(f2_s[:, 0]), ffn_low)
            for t in range(NT):
                take_down(CHUNKS - 1, t)
            dve.wait_ge(ffn_low, 2)
            dve.wait_ge(oh_made, SUPERS + 2)
            dve.sem_inc(phase_done, 1)
            dve.wait_ge(phase_done, 9)

            def take_sum(i, b, first=False):
                hold(dve, yx_made, i + 1)
                if not first:
                    hold(dve, x2b_made, i)
                for t in range(NT):
                    last = vec.tensor_tensor(x2[:, t, :], aggb[:, b, t, :], yb[:, b, t, :], ALU.add)
                    last.then_inc(x2_made, 1)
                hold(dve, x2_made, i * NT + NT)
                if not first:
                    hold(dve, tr_full, i * KB + TR_C0)
                normalise(z3, x2).then_inc(z3_made, 1)
                hold(dve, z3_made, i + 1)

            def c_chunk(i, b, last=False):
                for k in range(KB):
                    hold(dve, hi_made, c_val(i, ("z", k)))
                    vec.tensor_tensor(z3T[:, 1, k, :], ps[:, TR0 + k % 2, :], z3T[:, 0, k, :], ALU.subtract)\
                        .then_inc(lo_made, 1)
                if not last:
                    take_sum(i + 1, b)
                for j in range(KB):
                    hold(dve, hi_made, c_val(i, ("f", j)))
                    vec.tensor_tensor(fT[:, 1, j, :], tmp_c[:, j, :], fT[:, 0, j, :], ALU.subtract)\
                        .then_inc(lo_made, 1)
                hold(dve, out_free, i + 1)
                hold(dve, x2b_made, i + 1)
                for t in range(NT):
                    u = MM_C["f2", t]
                    hold(dve, mm_full, i * len(MM_C) + (MM_C0 + u + 1))
                    vec.scalar_tensor_tensor(outb[:, t, :], mm_bank(u), 1.0 / WS, x2b[:, t, :],
                                             ALU.mult, ALU.add).then_inc(out_made, 1)

            C_LINKS = 2 + ROOT
            take_sum(0, 0, first=True)
            with dve.Fori(0, CHUNKS // 2 - 1) as r:
                ch.enter(r, 2 * C_LINKS)
                c_chunk(2 * r, 1)
                c_chunk(2 * r + 1, 0)
            ch.leave(CHUNKS // 2 - 1)
            c_chunk(CHUNKS - 2, 1)
            c_chunk(CHUNKS - 1, 0, last=True)

        @block.tensor
        def _(pe):
            mm, tr = nc.tensor.matmul, nc.tensor.transpose

            def mm3(bank, pairs, start=True):
                n = len(pairs) * len(PARTS)
                c = 0
                for lhs, rhs in pairs:
                    for p, q in PARTS:
                        ins = mm(bank, lhs[p], rhs[q], start=start and c == 0, stop=c == n - 1)
                        c += 1
                return ins

            pe.wait_ge(consts_made, EARLY_CONSTS)
            pe.wait_ge(onehot_made, 2)
            mm(ps[:, RANK_BANK, :], pick[:, 0:P], ohb[:, 0, 0:HALF], start=True, stop=False)
            with pe.Fori(0, BLOCKS // 2) as r:
                for b in range(2):
                    hold(pe, onehot_made, 2 * r + (b + 1))
                    for h in range(2):
                        last = mm(ps[:, RANK_BANK, :], pick[:, bass.ds((P - h * BLOCKS - b) - 2 * r, P)],
                                  ohb[:, b, h * HALF:(h + 1) * HALF], start=False, stop=False)
                    last.then_inc(counted, 1)
            mm(ps[:, RANK_BANK, :], pick[:, 0:P], ohb[:, 0, 0:HALF], start=False, stop=True).then_inc(counted, 1)
            pe.wait_ge(consts_made, ALL_CONSTS)
            pe.wait_ge(dve_setup, 1)
            mm(ps[:, 6, 0:1], samehalf, tot[:, 0:1], start=True, stop=True)
            mm(ps[:, 5, 0:1], otherhalf, tot[:, 0:1], start=True, stop=True).then_inc(pe_setup, 1)
            pe.wait_ge(dve_setup, 2)
            mm(ps[:, 4, 0:1], upto[0:BLOCKS, :], supn[0:BLOCKS, 0:1], start=True, stop=True).then_inc(pe_setup, 1)
            pe.wait_ge(dve_setup, 3)
            half = SUPERS // 2
            for h in range(2):
                mm(ps[:, 2 + h, 0:half], ones16[0:BLOCKS, :], passed[0:BLOCKS, h * half:(h + 1) * half],
                   start=True, stop=True)
            for k in range(KB):
                last = tr(ps[:, 0, k * P:(k + 1) * P], firstf[:, k * P:(k + 1) * P], ident[:, :])
            last.then_inc(pe_setup, 1)
            pe.wait_ge(setup_left, 2)
            pe.sem_inc(seg_full, SEG_CREDIT)

            def transposes(bank, of, k):
                for t in range(NT):
                    last = tr(bank[:, t * P:(t + 1) * P], of[:, t, k * P:(k + 1) * P], ident[:, :])
                last.then_inc(tr_full, 1)

            def z_transposes(i, first=False):
                pe.wait_ge(z_made, i + 1)
                for k in range(KB):
                    if k < 2 and not first:
                        pe.wait_ge(lo_made, zx_low(i - 1, ("x", k + 2)))
                    elif k >= 2:
                        pe.wait_ge(hi_made, zx_low(i, ("z", k - 2), 1))
                    transposes(ps[:, TR0 + k % 2, :], xz, k)

            def x_transposes(i):
                for k in range(KB):
                    if k < 2:
                        pe.wait_ge(hi_made, zx_low(i, ("z", k + 2), 1))
                    else:
                        pe.wait_ge(lo_made, zx_low(i, ("x", k - 2)))
                    transposes(ps[:, TR0 + k % 2, :], xn, k)

            def rank(i, r):
                pe.wait_ge(onehot_made, i * SORT_STEPS + (BLOCKS + r + 1))
                pe.wait_ge(rank_free, i * SORT_STEPS + (r + 1))
                if r == 0:
                    pe.wait_ge(first_loaded, i * 64 + 64)
                g, w = 32 * (r // 2), SORT_COLS * BLOCKS
                mm(ps[:, RANK_BANK, :], below[:, :], onehot[:, r % 2, :, :].rearrange("p c b -> p (c b)"),
                   start=True, stop=False)
                mm(ps[:, RANK_BANK, :], hilo[g:g + 2, :], first[g:g + 2, r % 2 * w:(r % 2 + 1) * w],
                   start=False, stop=True).then_inc(rank_full, 1)

            def kv_product(i, h, last):
                pe.wait_ge(lo_made, a_val(2, i, ("e", h * NT + NT - 1), last))
                pe.wait_ge(kv_free, i * PAIRS + (h + 1))
                for r in range(4):
                    e = r // 2
                    ins = mm3(ps[:, KV_BANK, r * VW:(r + 1) * VW],
                              [([kp[:, h % 2, p, t, r * P:(r + 1) * P] for p in range(2)],
                                [v[:, p, t, 2 * h + e, :] for p in range(2)]) for t in range(NT)])
                ins.then_inc(kv_full, 1)

            def a_bank(key, i, last):
                u = MM_A[key]
                j = i
                if u < MMB:
                    if isinstance(i, int) and i == 0:
                        return mm_bank(u)
                    j = i - 1
                name, k = list(MM_A)[(u - MMB) % len(MM_A)]
                late = last and u >= MMB
                if name in ("q", "k"):
                    pe.wait_ge(hi_made, a_val(1, j, (name, k), late))
                elif name in ("v", "g"):
                    pe.wait_ge(lo_made, a_val(2, j, (name, k), late))
                else:
                    pe.wait_ge(exp_made, j * MS + (k + 1))
                return mm_bank(u)

            def a_chunk(i, last=False):
                pe.wait_ge(lo_made, zx_low(i, ("z", KB - 1)))
                both = lambda w, *rest: [w[(slice(None), p) + rest] for p in range(2)]
                al = slice(None)
                for part, off in (("q", 0), ("k", D)):
                    for j in range(4):
                        bank = a_bank((part, j), i, last)
                        mm3(bank, [(both(wqkv_s, k, slice(off + j * P, off + (j + 1) * P)), both(hT, k, al))
                                   for k in range(KB)]).then_inc(mm_full, 1)
                        if j % 2:
                            rank(i, 2 * (part == "k") + j // 2)
                for t in range(NT):
                    bank = a_bank(("v", t), i, last)
                    mm(bank, minus[:, :], bv2[:, :], start=True, stop=False)
                    mm3(bank, [(both(hT, k, slice(t * P, (t + 1) * P)), both(wqkv_s, k, slice(2 * D, 3 * D)))
                               for k in range(KB)], start=False).then_inc(mm_full, 1)
                if not last:
                    z_transposes(i + 1)
                pe.wait_ge(lo_made, a_val(2, i, ("v", NT - 1), last))
                for h in range(PAIRS):
                    for t in range(NT):
                        bank = a_bank(("e", NT * h + t), i, last)
                        mm3(bank, [(both(kT, h, slice(t * P, (t + 1) * P)), both(pbd, al))]).then_inc(mm_full, 1)
                    if h == 0:
                        pe.wait_ge(lo_made, zx_low(i, ("x", KB - 1)))
                    bank = a_bank(("g", h), i, last)
                    mm3(bank, [(both(xT, k, slice(h * P, (h + 1) * P)), both(wg_s, k, al)) for k in range(KB)])\
                        .then_inc(mm_full, 1)
                    if h >= 1:
                        kv_product(i, h - 1, last)
                    rank(i, PAIRS + h)
                if not last:
                    x_transposes(i + 1)
                kv_product(i, PAIRS - 1, last)

            z_transposes(0, first=True)
            x_transposes(0)
            a_chunk(0)
            with pe.Fori(1, CHUNKS - 1) as i:
                a_chunk(i)
            a_chunk(CHUNKS - 1, last=True)
            pe.sem_inc(phase_done, 1)
            pe.wait_ge(phase_done, 4)

            both = lambda w, *rest: [w[(slice(None), p) + rest] for p in range(2)]
            al = slice(None)

            def seg(i, k):
                s = (i - B1) * SEG + k
                gr = k // GSUP
                if k % GSUP == 0:
                    pe.wait_ge(gathered[gr % GS], (i - B1) * (16 * GT * GROUPS // GS) + (gr // GS + 1) * 16 * GT)
                pe.wait_ge(oh_made, s + 1)
                pe.wait_ge(acc_made, s + 1)
                mm3(ps[:, SEG0 + k % 2, :],
                    [([oh[:, k % 2 * SUP + t, p, :] for p in range(2)],
                      [ring[:, gr % GS, k % GSUP * SUP + t, p * D:(p + 1) * D] for p in range(2)])
                     for t in range(SUP)]).then_inc(seg_full, 1)

            def down(i, t, bank):
                mm3(bank, [(both(gT, j, slice(t * P, (t + 1) * P)), both(w2_s, j, al)) for j in range(JB)])\
                    .then_inc(mm_full, 1)

            def b_chunk(i, with_seg):
                first = isinstance(i, int) and i == 0
                table = MM_B1 if first else MM_B
                todo = seg_plan(with_seg)
                done = [0]

                def fill(n):
                    for _ in range(n):
                        seg(i, done[0])
                        done[0] += 1

                def take(key):
                    u = table[key]
                    if u < MMB:
                        if not first:
                            pe.wait_ge(hi_made, b_val(i - 1, ("up", JB - MMB + u)))
                        return mm_bank(u)
                    name, k = list(table)[u - MMB]
                    if name == "e":
                        pe.wait_ge(exp_made, i * MS + (CHUNKS * MS + k + 1))
                    elif name == "down":
                        pe.wait_ge(y_made, i * NT + (k + 1 - NT))
                    elif name == "proj":
                        pe.wait_ge(x1_made, i * NT + (k + 1))
                    else:
                        pe.wait_ge(hi_made, b_val(i, ("up", k)))
                    return mm_bank(u)

                def take_tr(key):
                    u = TR_B[key]
                    if u == 0:
                        if not first:
                            pe.wait_ge(hi_made, b_val(i - 1, ("h", KB - 1)))
                    else:
                        name, k = list(TR_B)[u - 1]
                        if name == "q":
                            pe.wait_ge(qpT_made, i * MS + (k + 1))
                        elif name == "att":
                            pe.wait_ge(lo_made, b_val(i, ("att", k)))
                        else:
                            pe.wait_ge(hi_made, b_val(i, ("h", k)))
                    return ps[:, TR0, :]
                pe.wait_ge(qb_loaded, i * 16 + 16)
                for n in range(B_STEPS):
                    if n < MS:
                        t, h = n // PAIRS, n % PAIRS
                        bank = take(("e", n))
                        mm3(bank, [(both(qTb, h, slice(t * P, (t + 1) * P)), both(pbd, al))]).then_inc(mm_full, 1)
                    if not first and 1 <= n <= NT:
                        if n == 1:
                            pe.wait_ge(lo_made, b_val(i - 1, ("up", JB - 1)))
                        down(i - 1, n - 1, take(("down", n - 1)))
                    fill(min(1, todo[n]))
                    if 1 <= n <= MS:
                        m = n - 1
                        pe.wait_ge(exp_made, i * MS + (CHUNKS * MS + m + 1))
                        bank = take_tr(("q", m))
                        for r in range(4):
                            ins = tr(bank[:, r * P:(r + 1) * P], qp[:, m % 2, r * P:(r + 1) * P], ident[:, :])
                        ins.then_inc(tr_full, 1)
                    fill(max(0, todo[n] - 1))
                    if 2 <= n < MS + 2:
                        m = n - 2
                        pe.wait_ge(qpT_made, i * MS + (m + 1))
                        if m >= 1:
                            pe.wait_ge(att_made, i * MS + m)
                        h = m % PAIRS
                        for e in range(2):
                            for c in range(2):
                                ins = mm(att_out[:, e, :], qpT[:, m % 2, e * 2 + c, :], kv[:, 2 * h + e, c, :],
                                         start=(c == 0), stop=(c == 1))
                        ins.then_inc(att_full, 1)
                    if n >= 6 and (n - 6) % 4 == 0 and (n - 6) // 4 < NT:
                        t = (n - 6) // 4
                        pe.wait_ge(att_made, i * MS + (t * PAIRS + PAIRS))
                        bank = take_tr(("att", t))
                        for k in range(KB):
                            ins = tr(bank[:, k * P:(k + 1) * P], att[:, t % 2, k * P:(k + 1) * P], ident[:, :])
                        ins.then_inc(tr_full, 1)
                    if n >= 7 and (n - 7) % 4 == 0 and (n - 7) // 4 < NT:
                        t = (n - 7) // 4
                        pe.wait_ge(lo_made, b_val(i, ("att", t)))
                        mm3(take(("proj", t)),
                            [([attT[:, t % 2, p, k, :] for p in range(2)], both(wproj_s, k, al)) for k in range(KB)])\
                            .then_inc(mm_full, 1)
                pe.wait_ge(z2_made, i * NT + NT)
                for k in range(KB):
                    transposes(take_tr(("h", k)), z2, k)
                    fill(todo[B_STEPS + k])
                pe.wait_ge(lo_made, b_val(i, ("h", KB - 1)))
                for j in range(JB):
                    mm3(take(("up", j)), [(both(w1_s, k, slice(j * P, (j + 1) * P)), both(h2T, k, al))
                                          for k in range(KB)]).then_inc(mm_full, 1)
                    fill(todo[B_STEPS + KB + j])

            b_chunk(0, False)
            with pe.Fori(1, B1) as i:
                b_chunk(i, False)
            with pe.Fori(B1, CHUNKS) as i:
                b_chunk(i, True)
            pe.wait_ge(lo_made, b_val(CHUNKS - 1, ("up", JB - 1)))
            for t in range(NT):
                down(CHUNKS - 1, t, mm_bank(t))
            pe.sem_inc(phase_done, 1)
            pe.wait_ge(phase_done, 9)

            def c_chunk(i, first=False):
                pe.wait_ge(z3_made, i + 1)
                for k in range(KB):
                    if k >= 2:
                        pe.wait_ge(lo_made, c_val(i, ("z", k - 2)))
                    elif not first:
                        pe.wait_ge(lo_made, c_val(i - 1, ("z", k + 2)))
                    transposes(ps[:, TR0 + k % 2, :], z3, k)
                pe.wait_ge(lo_made, c_val(i, ("z", KB - 1)))
                for j in range(KB):
                    pe.wait_ge(out_made, i * NT + (OUT_CREDIT - NT + j + 1))
                    mm3(mm_bank(MM_C["f1", j]), [(both(f1_s, k, slice(j * P, (j + 1) * P)), both(z3T, k, al))
                                                 for k in range(j + 1)]).then_inc(mm_full, 1)
                pe.wait_ge(lo_made, c_val(i, ("f", KB - 1)))
                for t in range(NT):
                    bank = mm_bank(MM_C["f2", t])
                    for k in range(KB):
                        for c, (p, q) in enumerate(PARTS):
                            ins = mm(bank[:, k * P:D], fT[:, p, k, t * P:(t + 1) * P], f2_s[:, q, k, k * P:D],
                                     start=(k == 0 and c == 0), stop=(k == KB - 1 and c == len(PARTS) - 1))
                    ins.then_inc(mm_full, 1)

            c_chunk(0, first=True)
            with pe.Fori(1, CHUNKS) as i:
                c_chunk(i)


def kernel(x, src, dst, edge_weight, L0_gnn_weight, L0_mix_Wqkv, L0_mix_bqkv, L0_mix_Pmat, L0_mix_Wproj, L0_mix_bproj,
           L0_mix_W1, L0_mix_b1, L0_mix_W2, L0_mix_b2, L0_mix_g1, L0_mix_be1, L0_mix_g2, L0_mix_be2,
           L0_ffn_W1, L0_ffn_b1, L0_ffn_W2, L0_ffn_b2):
    import numpy as np
    import concourse.bacc as bacc
    from concourse.bass_utils import run_bass_kernel_spmd

    def cols(a):
        return np.asarray(a).reshape(-1, P).T
    given = {"x": x, "src": src, "dst": dst, "ew": edge_weight, "wgT": np.asarray(L0_gnn_weight).T,
             "wqkv": L0_mix_Wqkv, "bqkv": L0_mix_bqkv, "pmat": L0_mix_Pmat, "wproj": L0_mix_Wproj,
             "bproj": L0_mix_bproj, "w1": L0_mix_W1, "b1": cols(L0_mix_b1), "w2": L0_mix_W2, "b2": L0_mix_b2,
             "g1": cols(L0_mix_g1), "be1": cols(L0_mix_be1), "g2": cols(L0_mix_g2), "be2": cols(L0_mix_be2),
             "f1T": np.asarray(L0_ffn_W1).T, "fb1": cols(L0_ffn_b1), "f2T": np.asarray(L0_ffn_W2).T, "fb2": L0_ffn_b2,
             "bqkv_c": cols(L0_mix_bqkv)}
    nc = bacc.Bacc("TRN2", target_bir_lowering=False, num_devices=1)
    arrays, aps = {}, {}
    for name, a in given.items():
        a = np.ascontiguousarray(a)
        arrays["in_" + name] = a
        aps[name] = nc.dram_tensor("in_" + name, a.shape, mybir.dt.from_np(a.dtype), kind="ExternalInput").ap()
    out = nc.dram_tensor("out", (N, D), F32, kind="ExternalOutput").ap()
    build(nc, *aps.values(), out)
    r = run_bass_kernel_spmd(nc, [arrays], core_ids=[0])
    return r.results[0]["out"]
```

```python
import concourse.bass as bass
from concourse import mybir
from contextlib import ExitStack

F32 = mybir.dt.float32
F16 = mybir.dt.float16
I32 = mybir.dt.int32
ALU = mybir.AluOpType
ACT = mybir.ActivationFunctionType
X = mybir.AxisListType.X

P = 128
N, D, E = 8192, 512, 131072
KB = D // P
HEADS, DH, NF = 8, 64, 256
PAIRS = HEADS // 2
HID = 1024
JB = HID // P
EPS = 1e-5
KSUM_EPS = 1e-6
NT = 4
CT = NT * P
CHUNKS = N // CT
VW = DH + 1
WS = 256.0
FS = 2.0 ** 15
PARTS = ((0, 0), (0, 1), (1, 0))
MS = NT * PAIRS

BLOCKS = N // P
COLS = E // P
HALF = COLS // 2
SORT_COLS = 8
CCOLS = COLS // CHUNKS
SORT_STEPS = CCOLS // SORT_COLS
SUP = 2
SUP_EDGES = SUP * P
B1 = 1
GT = 2
GS = 5
AR = 4
SEG = -(-(E // SUP_EDGES + BLOCKS) // (CHUNKS - B1))
SEG += -SEG % AR
SUPERS = E // SUP_EDGES + BLOCKS
SEG_LAST = SUPERS - SEG * (CHUNKS - B1 - 1)
TILES = SUPERS * SUP
GROUPS = SEG * SUP // GT
GSUP = GT // SUP
MMB = 4
OHB = 4
PBD_CLEARED, EARLY_CONSTS, ALL_CONSTS = 1, 15, 26
assert GROUPS % GS == 0 and SEG % AR == 0 and SEG_LAST % AR == 0 and GT % SUP == 0


RANK_Q, RANK_K, RANK_V, RANK_E = 0, 1, (2, 3, 4), (5, 6, 7)


def order_of(uses):
    return {u: k for k, u in enumerate(uses)}


def some(name, n=4):
    return [(name, k) for k in range(n)]


def a_orders(last):
    z, x = ([], []) if last else (some("z"), some("x"))
    mm = some("q") + some("k") + some("v")
    hi = some("q") + some("k") + some("v") + z
    lo = list(hi)
    for h in range(PAIRS):
        mm += [("e", 4 * h + t) for t in range(NT)] + [("g", h)]
        hi += [("e", m - 1) for m in range(4 * h, 4 * h + NT) if m] + [("g", h)]
        for m in range(4 * h, 4 * h + NT):
            lo += ([("e", m - 2)] if m >= 2 else []) + ([("g", h - 1)] if h and m == 4 * h else [])
    lo += [("g", PAIRS - 1), ("e", MS - 2), ("e", MS - 1)] + x
    hi += [("e", MS - 1)] + x
    return order_of(mm), order_of(hi), order_of(lo), order_of(some("q") + some("k") + z + some("e", MS))


A_BODY, A_LAST = a_orders(False), a_orders(True)
MM_A = A_BODY[0]
HL_A0 = 2 * KB
HL_A = len(A_BODY[1])
HL_B0 = HL_A0 + (CHUNKS - 1) * HL_A + len(A_LAST[1])
TR_A = 2 * KB
B_STEPS = MS + 5
DOWN_AT = (1, 2, 3, B_STEPS - 1)


def b_orders(first):
    mm, tr = [], []
    for n in range(B_STEPS):
        if n < MS:
            mm.append(("e", n))
        if not first and n in DOWN_AT:
            mm.append(("down", DOWN_AT.index(n)))
        if 1 <= n <= MS:
            tr.append(("q", n - 1))
        if n >= 6 and (n - 6) % 4 == 0 and (n - 6) // 4 < NT:
            tr.append(("att", (n - 6) // 4))
        if n >= 7 and (n - 7) % 4 == 0 and (n - 7) // 4 < NT:
            mm.append(("proj", (n - 7) // 4))
    return order_of(mm + some("up", JB)), order_of(tr + some("h"))


MM_B1, TR_B = b_orders(True)
MM_B, _ = b_orders(False)
HL_BT = order_of(some("att") + some("h") + some("up", JB))
HL_B = len(HL_BT)
MM_C = order_of(some("f1") + some("f2"))
HL_CT = order_of(some("z") + some("f"))
MM_B0 = CHUNKS * len(MM_A)
MM_BB = MM_B0 + len(MM_B1) - len(MM_B)
MM_D0 = MM_BB + CHUNKS * len(MM_B)
MM_C0 = MM_D0 + NT
HL_C0 = HL_B0 + CHUNKS * HL_B
TR_B0 = CHUNKS * TR_A
TR_C0 = TR_B0 + CHUNKS * len(TR_B)
for o in (MM_A, MM_B, MM_B1, MM_C, A_BODY[3], A_LAST[3]):
    assert not len(o) % MMB


def seg_plan(count):
    plan = [2, 3, 3, 3, 2] + [1, 2, 1, 1] * 2 + [1] * 7 + [2] + [1] * KB + [0, 1] * (JB // 2)
    if count < SEG:
        plan = [0] * 6 + [1] * (B_STEPS - 7) + [2] + [0] * KB + [0] * JB
        if count == 0:
            plan = [0] * len(plan)
    plan[6] += count - sum(plan)
    assert sum(plan) == count and min(plan) >= 0
    return plan


def build(nc, x, src, dst, ew, wgT, wqkv, bqkv, pmat, wproj, bproj, w1, b1, w2, b2, g1, be1, g2, be2,
          f1T, fb1, f2T, fb2, bqkv_c, out):
    xn_d = nc.dram_tensor("xn_d", (N, D), F32).ap()
    h_d = nc.dram_tensor("h_d", (N, 2 * D), F16).ap()
    y_d = nc.dram_tensor("y_d", (N, D), F32).ap()
    agg_d = nc.dram_tensor("agg_d", (BLOCKS * P, D), F32).ap()
    qT_d = nc.dram_tensor("qT_d", (P, CHUNKS * 2 * KB * CT), F16).ap()
    slots_d = nc.dram_tensor("slots_d", (P * TILES, 3), F32).ap()
    first_d = nc.dram_tensor("first_d", (2, COLS * BLOCKS), F16).ap()

    rows = lambda a: a.rearrange("(c t p) d -> p c t d", p=P, t=NT)
    x_v, xn_v, y_v, out_v, agg_v, h_v = rows(x), rows(xn_d), rows(y_d), rows(out), rows(agg_d), rows(h_d)
    qT_v = qT_d.rearrange("p (c k) -> p c k", c=CHUNKS)

    with ExitStack() as ctx:
        def sb(name, shape, dt=F32):
            return ctx.enter_context(nc.sbuf_tensor(name, shape, dt))

        def sem(name):
            return ctx.enter_context(nc.semaphore(name))

        def layer(area, size):
            at = [0]

            def lay(*shape, dt=F32):
                n = 1
                for s in shape:
                    n *= s
                words = n if dt != F16 else n // 2
                a = area[:, at[0]:at[0] + words]
                at[0] += words
                assert at[0] <= size, at[0]
                if dt != F32:
                    a = a.bitcast(dt)
                names = "abcde"[:len(shape)]
                if len(shape) > 1:
                    a = a.rearrange(f"p ({' '.join(names)}) -> p {' '.join(names)}", **dict(zip(names, shape)))
                return a
            return at, lay

        ident = sb("ident", [P, P])
        lane_ids = sb("lane_ids", [P, P])
        slots = sb("slots", [P, TILES + 4, 3])
        slots16 = slots[:, :, :].rearrange("p t f -> p (t f)").bitcast(F16).rearrange("p (t f) -> p t f", f=6)
        keep = sb("keep", [P, SUPERS])
        block_of = sb("block_of", [1, SUPERS + 1], I32)
        pbd = sb("pbd", [P, 2, 2 * NF], F16)
        kv = sb("kv", [P, HEADS, 2, VW])
        bq = sb("bq", [P, 4]); bk = sb("bk", [P, 4]); b1c = sb("b1c", [P, JB]); fb1c = sb("fb1c", [P, KB])
        g1c = sb("g1c", [P, KB]); be1c = sb("be1c", [P, KB]); g2c = sb("g2c", [P, KB]); be2c = sb("be2c", [P, KB])
        brow = sb("brow", [P, 2, D])
        bv2 = sb("bv2", [2, D], F16)
        minus = sb("minus", [2, P], F16)
        wproj_s = sb("wproj_s", [P, 2, KB, D], F16)
        w1_s = sb("w1_s", [P, 2, KB, HID], F16)
        w2_s = sb("w2_s", [P, 2, JB, D], F16)
        stats = sb("stats", [P, NT, 6]); mv = sb("mv", [P, NT, 2]); rstd = sb("rstd", [P, NT]); shift = sb("shift", [P, NT])
        vpe = sb("vpe", [P, NT]); guess = sb("guess", [P, NT], I32); half_vy = sb("half_vy", [P, NT])
        nmax = sb("nmax", [P, MS, 2]); rden = sb("rden", [P, MS, 2])
        edge = sb("edge", [P, 4 * COLS])
        rec = edge[:, 0:3 * COLS].rearrange("p (c f) -> p c f", f=3)
        rec16 = edge[:, 0:3 * COLS].bitcast(F16).rearrange("p (c f) -> p c f", f=6)
        addr = edge[:, 3 * COLS:4 * COLS].bitcast(I32)
        dsti = addr
        f1_raw = edge[:, 0:KB * D].rearrange("p (k n) -> p k n", k=KB)
        f2_raw = edge[:, KB * D:2 * KB * D].rearrange("p (k n) -> p k n", k=KB)
        stage_rec = sb("stage_rec", [P, CCOLS, 3]); stage_addr = sb("stage_addr", [P, CCOLS], I32)
        stage_dst = sb("stage_dst", [P, SEG * SUP], I32)
        below = sb("below", [P, P], F16)
        hilo = sb("hilo", [P, P], F16)
        ones16 = sb("ones16", [P, P], F16)
        pick = sb("pick", [P, 2 * P], F16)
        block_ids = sb("block_ids", [P, BLOCKS], F16)

        at, lay = layer(slots[:, :, :].rearrange("p t f -> p (t f)"), 3 * (TILES + 4))
        xT = lay(2, KB, CT, dt=F16)
        bucket = lay(COLS, dt=F16)
        onehot = lay(2, SORT_COLS, BLOCKS, dt=F16)
        pos = lay(CCOLS); posi = lay(CCOLS, dt=I32); posl = lay(CCOLS, dt=I32); post = lay(CCOLS, dt=I32)
        at[0] = 0
        runs = lay(2, HALF); firstT = lay(HALF, dt=I32); hi_i = lay(HALF, dt=I32)
        ARENA = 29952
        arena = sb("arena", [P, ARENA])
        at, lay = layer(arena, ARENA)
        wqkv_s = lay(2, KB, 3 * D, dt=F16); wg_s = lay(2, KB, D, dt=F16)
        WEIGHTS_END = at[0]
        xz = lay(NT, D); xn = lay(NT, D)
        hT = lay(2, KB, CT, dt=F16); qT = lay(2, 4, CT, dt=F16); kT = lay(2, 4, CT, dt=F16)
        v = lay(2, NT, HEADS, VW, dt=F16)
        kp = lay(2, 2, NT, 2 * NF, dt=F16)
        tmp = lay(MMB, CT)
        hb = lay(2 * NT, D, dt=F16).rearrange("p (t h) n -> p t h n", h=2)
        picked = lay(SORT_COLS, BLOCKS)
        first = lay(2 * SORT_COLS * BLOCKS, dt=F16)
        at[0] = WEIGHTS_END
        raw = lay(JB * D + KB * HID + KB * D)
        bv_raw = lay(D); bv_h = lay(D, dt=F16)
        srci = lay(COLS, dt=I32); ewf = lay(COLS); lanei = lay(COLS, dt=I32)
        ohb = lay(OHB, COLS, dt=F16)
        count = lay(HALF); firstf = lay(HALF)
        lo_i = lay(HALF, dt=I32); hl = lay(2, HALF, dt=F16)
        samehalf = lay(P); otherhalf = lay(P); upto = lay(P)
        sup_i = lay(SUPERS, dt=I32); sup_f = lay(SUPERS); passed = lay(SUPERS, dt=F16)
        blk_f = lay(SUPERS)
        lane_i = lay(P, dt=I32); blkid_i = lay(BLOCKS, dt=I32); blkid_f = lay(BLOCKS); row_f = lay(2)
        tot = lay(2); toti = lay(2, dt=I32); supn = lay(2); ends = lay(2)
        at[0] = 0
        qTb = lay(2, 4, CT, dt=F16); xnb = lay(NT, D)
        qp = lay(2, 2 * NF); qpT = lay(2, 4, P)
        att = lay(2, D); attT = lay(2, 2, KB, P, dt=F16)
        x1 = lay(NT, D); z2 = lay(NT, D)
        h2T = lay(2, KB, CT, dt=F16); gT = lay(2, JB, CT, dt=F16); tmp_b = lay(MMB, CT)
        oh = lay(2 * SUP, 2, P, dt=F16)
        acc = lay(AR, D); y3 = lay(D)
        ring = lay(GS, GT, 2 * D, dt=F16)
        at[0] = 0
        xb = lay(2, NT, D); yb = lay(2, NT, D); aggb = lay(2, NT, D)
        outb = lay(2, NT, D); z3 = lay(NT, D)
        z3T = lay(2, KB, CT, dt=F16); fT = lay(4, KB, CT, dt=F16); tmp_c = lay(MMB, CT)
        fT = fT.rearrange("p (b h) k n -> p b h k n", b=2)
        f1_s = wproj_s
        f2_s = w1_s[:, :, :, :].rearrange("p h k n -> p (h k n)")[:, 0:2 * KB * D]\
            .rearrange("p (h k n) -> p h k n", h=2, k=KB)

        ps = ctx.enter_context(nc.psum_tensor("ps", [P, 8, 512], F32))
        mm_bank = lambda u: ps[:, u % MMB, :]
        TR0, KV_BANK, RANK_BANK, ATT_BANK, SEG0 = 4, 6, 7, 5, 6
        F2_BANKS, Z3_BANKS = (6, 7, 0, 1), (4, 5, 2, 3)
        att_out = ps[:, ATT_BANK, 0:2 * VW].rearrange("p (h e) -> p h e", e=VW)

        names = """loaded_edges loaded_w loaded_w2 consts_made zeroed slots_cleared recs_loaded lanes_made recs_made scaled weights_high weights_low first_low
            counted onehot_made pe_setup dve_setup dve_done first_split first_stored setup_left
            x_loaded xn_made xn_stored z_ready z_made first_loaded q_stored h_stored mm_full tr_full hi_made lo_made
            tmp_made max_made exp_made kv_full kv_free rank_full rank_free addr_made staged scattered phase_done
            slots_loaded idle qb_loaded xnb_loaded xb_made qpT_made att_full att_made x1_made z2_made y_made y_stored y3_stored
            brow_loaded dst_staged oh_made seg_full acc_made acc_saved agg_stored ffn_loaded tril_made ffn_high
            ffn_low x2_made x2b_made yx_made z3_made out_made out_stored out_free""".split()
        S = {n: sem(n) for n in names}
        (loaded_edges, loaded_w, loaded_w2, consts_made, zeroed, slots_cleared, recs_loaded, lanes_made, recs_made, scaled, weights_high, weights_low, first_low,
         counted, onehot_made, pe_setup, dve_setup, dve_done, first_split, first_stored, setup_left,
         x_loaded, xn_made, xn_stored, z_ready, z_made, first_loaded, q_stored, h_stored, mm_full, tr_full, hi_made, lo_made,
         tmp_made, max_made, exp_made, kv_full, kv_free, rank_full, rank_free, addr_made, staged, scattered, phase_done,
         slots_loaded, idle, qb_loaded, xnb_loaded, xb_made, qpT_made, att_full, att_made, x1_made, z2_made, y_made,
         y_stored, y3_stored, brow_loaded, dst_staged, oh_made, seg_full, acc_made, acc_saved, agg_stored, ffn_loaded, tril_made,
         ffn_high, ffn_low, x2_made, x2b_made, yx_made, z3_made, out_made, out_stored, out_free) = S.values()
        gathered = [sem(f"gathered{s}") for s in range(GS)]
        yx_loaded = [sem(f"yx_loaded{s}") for s in range(2)]
        agg_loaded = [sem(f"agg_loaded{s}") for s in range(2)]

        SEG_CREDIT = GS * GSUP
        ACC_CREDIT = 2
        SAVED_CREDIT = AR
        OUT_CREDIT = NT
        LOADS_W = 4 + 8

        def hold(eng, s, value):
            eng.wait_ge(s, value)
            eng.sem_inc(idle, 1)

        def a_val(table, i, key, last=False):
            return i * HL_A + (HL_A0 + (A_LAST if last else A_BODY)[table][key] + 1)

        def zx_low(i, key, table=2):
            if isinstance(i, int) and i == 0:
                return order_of(some("z") + some("x"))[key] + 1
            return i * HL_A + (HL_A0 - HL_A + A_BODY[table][key] + 1)

        def b_val(i, key):
            return i * HL_B + (HL_B0 + HL_BT[key] + 1)

        def c_val(i, key):
            return i * len(HL_CT) + (HL_C0 + HL_CT[key] + 1)

        def mm_a(i, key):
            return i * len(MM_A) + (MM_A[key] + 1)

        def mm_b(i, key):
            first = isinstance(i, int) and i == 0
            return MM_B0 + MM_B1[key] + 1 if first else i * len(MM_B) + (MM_BB + MM_B[key] + 1)

        def mm_down(i, t):
            if isinstance(i, int) and i == CHUNKS - 1:
                return MM_D0 + t + 1
            return (i + 1) * len(MM_B) + (MM_BB + MM_B["down", t] + 1)

        def mm_f1(i, j):
            if isinstance(i, int) and i == 0:
                return MM_C0 + j + 1
            return i * len(MM_C) + (MM_C0 - NT + j + 1)

        def mm_f2(i, t):
            last = isinstance(i, int) and i == CHUNKS - 1
            return i * len(MM_C) + (MM_C0 + (KB if last else 2 * KB) + t + 1)

        def bank_b(i, key):
            first = isinstance(i, int) and i == 0
            return mm_bank((MM_B1 if first else MM_B)[key])

        class Chain:
            def __init__(self):
                self.base, self.n, self.i, self.per, self.first = 0, 0, None, 0, 0

            def enter(self, i, per, first=0):
                self.base += self.n
                self.i, self.per, self.first, self.n = i, per, first, 0

            def leave(self, times):
                assert self.n == self.per, (self.n, self.per)
                self.base += times * self.per
                self.i, self.n = None, 0

            def step(self, ins):
                ins.then_inc(dve_done, 1)
                self.n += 1
                return ins

            def value(self):
                if self.i is None:
                    return self.base + self.n
                return (self.i - self.first) * self.per + (self.base + self.n)

        block = ctx.enter_context(nc.Block())

        @block.sync
        def _(sp):
            cols = lambda a: a.rearrange("(p c) -> p c", p=P)
            wide = lambda w: w.rearrange("(k p) n -> p k n", p=P)

            def raw_at(start, k, n):
                return raw[:, start:start + k * n].rearrange("p (k n) -> p k n", n=n)
            sp.sem_inc(acc_saved, SAVED_CREDIT)
            sp.dma_start(srci, cols(src)).then_inc(loaded_edges, 16)
            sp.dma_start(raw_at(0, KB, 3 * D), wide(wqkv)).then_inc(loaded_w, 16)
            sp.wait_ge(slots_cleared, 1)
            sp.dma_start(slots_d.rearrange("(p t) f -> p t f", p=P), slots[:, 0:TILES, :]).then_inc(zeroed, 16)
            sp.dma_start(ewf, cols(ew)).then_inc(recs_loaded, 16)
            sp.dma_start(dsti, cols(dst)).then_inc(recs_loaded, 16)
            sp.dma_start(raw_at(KB * 3 * D, KB, D), wide(wgT)).then_inc(loaded_w, 16)
            p0 = KB * 4 * D
            sp.wait_ge(consts_made, PBD_CLEARED)
            sp.dma_start(raw[0:DH, p0:p0 + NF], pmat).then_inc(loaded_w, 16)
            sp.dma_start(raw[DH:P, p0 + NF:p0 + 2 * NF], pmat).then_inc(loaded_w, 16)
            for to, of in ((bq, bqkv_c[:, 0:4]), (bk, bqkv_c[:, 4:8]), (g1c, g1), (be1c, be1), (g2c, g2), (be2c, be2),
                           (b1c, b1), (fb1c, fb1)):
                sp.dma_start(to[:, :], of).then_inc(loaded_w, 16)
            sp.dma_start(bv_raw[0:2, :], bqkv[2 * D:3 * D].partition_broadcast(2)).then_inc(loaded_w2, 16)
            sp.dma_start(brow[:, 0, :], bproj.partition_broadcast(P)).then_inc(brow_loaded, 16)
            sp.dma_start(brow[:, 1, :], b2.partition_broadcast(P)).then_inc(brow_loaded, 16)
            sp.wait_ge(weights_high, 3)
            sp.wait_ge(first_low, 3)
            sp.dma_start(raw_at(0, KB, HID), wide(w1)).then_inc(loaded_w2, 16)
            sp.dma_start(raw_at(KB * HID, JB, D), wide(w2)).then_inc(loaded_w2, 16)
            sp.dma_start(raw_at(KB * HID + JB * D, KB, D), wide(wproj)).then_inc(loaded_w2, 16)
            sp.wait_ge(first_split, 1)
            for part in range(2):
                for h in range(2):
                    sp.dma_start(first_d[part, :].rearrange("(h k p b) -> h p k b", h=2, p=P, b=BLOCKS)[h],
                                 hl[:, part, :].rearrange("p (k h b) -> p k h b", h=2, b=BLOCKS)[:, :, h, :])\
                        .then_inc(first_stored, 16)
            sp.wait_ge(first_stored, 64)
            sp.wait_ge(setup_left, 2)
            sp.dma_start(xz, x_v[:, 0, :, :]).then_inc(x_loaded, 16)

            def load_first(i):
                for g in range(4):
                    w = 2 * SORT_COLS * BLOCKS
                    sp.dma_start(first[32 * g:32 * g + 2, :], first_d[:, bass.ds(i * (CCOLS * BLOCKS) + g * w, w)])\
                        .then_inc(first_loaded, 16)
            load_first(0)
            sp.wait_ge(xn_made, 1)
            sp.dma_start(xn_v[:, 0, :, :], xn).then_inc(xn_stored, 16)
            sp.wait_ge(tr_full, KB)
            sp.dma_start(xz, x_v[:, 1, :, :]).then_inc(x_loaded, 16)

            def a_chunk(i, load=True, last=False):
                if not last:
                    sp.wait_ge(xn_made, i + 2)
                    sp.dma_start(xn_v[:, i + 1, :, :], xn).then_inc(xn_stored, 16)
                sp.wait_ge(lo_made, a_val(2, i, ("q", 3), last))
                sp.dma_start(qT_v[:, i, :], qT.rearrange("p h k n -> p (h k n)")).then_inc(q_stored, 16)
                if load:
                    sp.wait_ge(tr_full, (i + 1) * TR_A + KB)
                    sp.dma_start(xz, x_v[:, i + 2, :, :]).then_inc(x_loaded, 16)
                sp.wait_ge(lo_made, a_val(2, i, ("g", 3), last))
                sp.dma_start(h_v[:, i, :, :], hb.rearrange("p t h n -> p t (h n)")).then_inc(h_stored, 16)
                if not last:
                    sp.wait_ge(rank_full, i * SORT_STEPS + SORT_STEPS)
                    load_first(i + 1)
            with sp.Fori(0, CHUNKS - 2) as i:
                a_chunk(i)
            a_chunk(CHUNKS - 2, load=False)
            a_chunk(CHUNKS - 1, load=False, last=True)
            for s in (q_stored, xn_stored, h_stored):
                sp.wait_ge(s, 16 * CHUNKS)
            sp.sem_inc(phase_done, 1)
            sp.wait_ge(phase_done, 4)
            sp.dma_start(qTb.rearrange("p h k n -> p (h k n)"), qT_v[:, 0, :]).then_inc(qb_loaded, 16)
            sp.dma_start(xnb, xn_v[:, 0, :, :]).then_inc(xnb_loaded, 16)

            def load_q(i):
                sp.wait_ge(exp_made, (i + 1) * MS + CHUNKS * MS)
                sp.dma_start(qTb.rearrange("p h k n -> p (h k n)"), qT_v[:, (i + 1) % CHUNKS, :]).then_inc(qb_loaded, 16)

            def load_xn(i):
                sp.wait_ge(x1_made, i * NT + NT)
                sp.dma_start(xnb, xn_v[:, (i + 1) % CHUNKS, :, :]).then_inc(xnb_loaded, 16)

            def store_y(i):
                sp.wait_ge(y_made, i * NT + (NT - 1))
                sp.dma_start(y_v[:, i, 0:NT - 1, :], x1[:, 0:NT - 1, :]).then_inc(y_stored, 16)

            def store_y3(i):
                sp.wait_ge(y_made, i * NT + NT)
                sp.dma_start(y_v[:, i, NT - 1, :], y3).then_inc(y3_stored, 16)
            load_q(0)
            load_xn(0)
            sp.wait_ge(scattered, 16 * COLS)
            sp.dma_start(slots[:, 0:TILES, :], slots_d.rearrange("(p t) f -> p t f", p=P)).then_inc(slots_loaded, 16)
            sp.dma_start(f1_raw, wide(f1T)).then_inc(ffn_loaded, 16)
            sp.dma_start(f2_raw, wide(f2T)).then_inc(ffn_loaded, 16)

            def flush(i, start, stop):
                if start == stop:
                    return
                with sp.Fori(start // AR, stop // AR) as r:
                    for a in range(AR):
                        s = (i - B1) * SEG + (r * AR + a)
                        hold(sp, acc_made, s + (ACC_CREDIT + 1))
                        here = sp.value_load(block_of[0:1, bass.ds(s, 1)], min_val=0, max_val=BLOCKS - 1)
                        nxt = sp.value_load(block_of[0:1, bass.ds(s + 1, 1)], min_val=0, max_val=BLOCKS)
                        with sp.If(here < nxt):
                            sp.dma_start(agg_d[bass.ds(here * P, P), :], acc[:, a, :]).then_inc(agg_stored, 16)
                            hold(sp, agg_stored, (here + 1) * 16)
                        sp.sem_inc(acc_saved, 1)

            def b_chunk(i, count):
                f1, f2, f3 = (sum(seg_plan(count)[0:n]) // AR * AR for n in (NT, MS, B_STEPS))
                flush(i, 0, f1)
                store_y(i - 1)
                flush(i, f1, f2)
                load_q(i)
                flush(i, f2, f3)
                load_xn(i)
                store_y3(i - 1)
                flush(i, f3, count)
            with sp.Fori(B1, CHUNKS - 1) as i:
                b_chunk(i, SEG)
            b_chunk(CHUNKS - 1, SEG_LAST)

            def yx_load(i, b):
                sp.dma_start(xb[:, b, :, :], x_v[:, i, :, :]).then_inc(yx_loaded[b], 16)
                sp.dma_start(yb[:, b, :, :], y_v[:, i, :, :]).then_inc(yx_loaded[b], 16)
            sp.wait_ge(qb_loaded, 16 * (CHUNKS + 1))
            sp.wait_ge(xnb_loaded, 16 * (CHUNKS + 1))
            sp.wait_ge(z2_made, CHUNKS * NT)
            sp.wait_ge(y_stored, 16 * (CHUNKS - 1))
            sp.wait_ge(y3_stored, 16 * (CHUNKS - 1))
            for b in range(2):
                yx_load(b, b)
            store_y(CHUNKS - 1)
            store_y3(CHUNKS - 1)
            sp.wait_ge(y_stored, 16 * CHUNKS)
            sp.wait_ge(y3_stored, 16 * CHUNKS)
            sp.wait_ge(agg_stored, 16 * BLOCKS)
            sp.sem_inc(phase_done, 1)
            sp.wait_ge(phase_done, 9)
            sp.dma_start(brow[:, 0, :], fb2.partition_broadcast(P)).then_inc(brow_loaded, 16)

            def agg_load(i, b):
                sp.dma_start(aggb[:, b, :, :], agg_v[:, i, :, :]).then_inc(agg_loaded[b], 16)

            def c_load(i, b):
                yx_load(i, b)
                agg_load(i, b)

            def c_store(i, b):
                sp.wait_ge(out_made, i * NT + (OUT_CREDIT + NT))
                sp.dma_start(out_v[:, i, :, :], outb[:, b, :, :]).then_inc(out_stored, 16)
                sp.wait_ge(out_stored, i * 16 + 16)
                sp.sem_inc(out_free, 1)
            agg_load(0, 0)
            agg_load(1, 1)
            for b in range(2):
                sp.wait_ge(z3_made, b + 1)
                sp.wait_ge(x2b_made, b + 1)
                c_load(b + 2, b)
            with sp.Fori(0, CHUNKS // 2 - 2) as r:
                for b in range(2):
                    i = 2 * r + b
                    c_store(i, b)
                    sp.wait_ge(z3_made, i + 3)
                    sp.wait_ge(x2b_made, i + 3)
                    c_load(i + 4, b)
            for i in range(CHUNKS - 4, CHUNKS):
                c_store(i, i % 2)
            sp.wait_ge(out_stored, 16 * CHUNKS)

        @block.gpsimd
        def _(pool):
            g = nc.gpsimd
            made = [0]

            def const(ins):
                ins.then_inc(consts_made, 1)
                made[0] += 1
            const(g.memset(raw[:, KB * 4 * D:KB * 4 * D + 2 * NF], 0.0))
            assert made[0] == PBD_CLEARED
            const(g.memset(pick[:, :], 0.0))
            const(g.memset(ident[:, :], 0.0))
            const(g.memset(samehalf, 0.0))
            const(g.memset(otherhalf, 0.0))
            const(g.memset(upto[0:BLOCKS, :], 1.0))
            const(g.memset(below[:, :], 1.0))
            const(g.memset(ones16[:, :], 1.0))
            const(g.memset(hilo[:, :], 1.0))
            const(g.memset(minus[:, :], -1.0))
            const(g.iota(lane_i, pattern=[[1, P]], base=0, channel_multiplier=0))
            const(g.iota(blkid_i, pattern=[[1, BLOCKS]], base=0, channel_multiplier=0))
            const(g.iota(sup_i, pattern=[[1, SUPERS]], base=0, channel_multiplier=0))
            const(g.iota(toti[:, 0:1], pattern=[[1, 1]], base=0, channel_multiplier=1))
            pool.wait_ge(consts_made, made[0])
            const(g.memset(pick[:, P:P + 1], 1.0))
            assert made[0] == EARLY_CONSTS

            def diag(m, base):
                const(g.affine_select(out=m, in_=m, compare_op=ALU.not_equal, fill=1.0, base=base,
                                      pattern=[[-1, P]], channel_multiplier=1))
            diag(ident[:, :], 0)
            diag(samehalf, 0)
            diag(otherhalf, BLOCKS)
            for q in range(4):
                pool.wait_ge(consts_made, made[0])
                const(g.memset(hilo[32 * q:32 * q + 1, :], float(P)))
            pool.wait_ge(consts_made, made[0])
            const(g.affine_select(out=below[:, :], in_=below[:, :], compare_op=ALU.is_gt, fill=0.0, base=0,
                                  pattern=[[1, P]], channel_multiplier=-1))
            halves = upto[0:BLOCKS, :].rearrange("p (a b) -> p a b", a=2)
            const(g.affine_select(out=halves, in_=halves, compare_op=ALU.is_ge, fill=0.0, base=0,
                                  pattern=[[0, 2], [1, BLOCKS]], channel_multiplier=-1))
            pool.wait_ge(consts_made, made[0])
            diag(samehalf, BLOCKS)
            pool.wait_ge(consts_made, made[0])
            diag(samehalf, -BLOCKS)
            assert made[0] == ALL_CONSTS
            pool.wait_ge(recs_loaded, 32)
            g.tensor_copy(rec16[:, :, 2], ewf).then_inc(recs_made, 1)
            g.tensor_copy(rec[:, :, 2].bitcast(I32), dsti).then_inc(recs_made, 1)
            hold(pool, recs_made, 2)
            g.tensor_tensor(rec16[:, :, 3], ewf, rec16[:, :, 2], ALU.subtract).then_inc(recs_made, 1)
            pool.wait_ge(recs_made, 3)
            pool.wait_ge(lanes_made, 1)

            flat = lambda w: w.rearrange("p k n -> p (k n)")
            c0, c1, c2 = KB * 3 * D, KB * 4 * D, KB * HID + JB * D
            pool.wait_ge(weights_high, 3)
            for to, of, high in (
                    (flat(wqkv_s[:, 1]), raw[:, 0:c0], flat(wqkv_s[:, 0])),
                    (flat(wg_s[:, 1]), raw[:, c0:c1], flat(wg_s[:, 0])),
                    (pbd[:, 1, :], raw[:, c1:c1 + 2 * NF], pbd[:, 0, :])):
                g.tensor_tensor(to, of, high, ALU.subtract).then_inc(first_low, 1)
            pool.wait_ge(weights_high, 6)
            g.tensor_tensor(flat(wproj_s[:, 1]), raw[:, c2:c2 + KB * D], flat(wproj_s[:, 0]), ALU.subtract)\
                .then_inc(first_low, 1)
            pool.wait_ge(first_low, 4)
            pool.sem_inc(setup_left, 1)
            with pool.Fori(0, CHUNKS) as i:
                hold(pool, addr_made, i + 1)
                g.tensor_copy(stage_rec[:, :, :], rec[:, bass.ds(i * CCOLS, CCOLS), :]).then_inc(staged, 1)
                g.tensor_copy(stage_addr[:, :], addr[:, bass.ds(i * CCOLS, CCOLS)]).then_inc(staged, 1)
                hold(pool, staged, 2 * i + 2)
                for c in range(CCOLS):
                    pool.indirect_dma_start(
                        out=slots_d, out_offset=bass.IndirectOffsetOnAxis(ap=stage_addr[:, c:c + 1], axis=0),
                        in_=stage_rec[:, c, :], in_offset=None).then_inc(scattered, 16)
                hold(pool, scattered, (i + 1) * (16 * CCOLS))
            pool.wait_ge(phase_done, 4)
            pool.wait_ge(slots_loaded, 16)

            def gather(i, count):
                g.tensor_copy(stage_dst[:, 0:count * SUP],
                              slots[:, bass.ds(i * (SEG * SUP), count * SUP), 2].bitcast(I32)).then_inc(dst_staged, 1)
                hold(pool, dst_staged, i + 1)
                for gr in range(count * SUP // GT):
                    hold(pool, seg_full, i * SEG + (GSUP * gr + GSUP))
                    for t in range(GT):
                        c = gr * GT + t
                        pool.indirect_dma_start(
                            out=ring[:, gr % GS, t, :], out_offset=None, in_=h_d,
                            in_offset=bass.IndirectOffsetOnAxis(ap=stage_dst[:, c:c + 1], axis=0))\
                            .then_inc(gathered[gr % GS], 16)
                if count == SEG:
                    for s in range(GS):
                        hold(pool, gathered[s], (i + 1) * (16 * GT * GROUPS // GS))
            with pool.Fori(0, CHUNKS - B1 - 1) as i:
                gather(i, SEG)
            gather(CHUNKS - B1 - 1, SEG_LAST)
            pool.wait_ge(ffn_loaded, 32)
            for m in (f1_raw, f2_raw):
                for k in range(KB):
                    tri = m[:, k, k * P:(k + 1) * P]
                    g.affine_select(out=tri, in_=tri, compare_op=ALU.is_ge, fill=0.0, base=0, pattern=[[1, P]],
                                    channel_multiplier=-1).then_inc(tril_made, 1)
            def add_x(i, b, r):
                hold(pool, yx_loaded[b], r * 32 + 32)
                g.tensor_tensor(yb[:, b, :, :], yb[:, b, :, :], xb[:, b, :, :], ALU.add).then_inc(yx_made, 1)

            for b in range(2):
                add_x(b, b, 0)
            pool.sem_inc(phase_done, 1)
            pool.wait_ge(phase_done, 9)
            pool.wait_ge(brow_loaded, 48)

            def add_bias(i, b):
                hold(pool, x2_made, i * NT + NT)
                if not (isinstance(i, int) and i < 2):
                    hold(pool, out_free, i - 1)
                g.tensor_tensor(outb[:, b, :, :], yb[:, b, :, :], brow[:, 0, :].unsqueeze(1).broadcast_to([P, NT, D]), ALU.add)\
                    .then_inc(x2b_made, 1)
            for i in range(2):
                add_bias(i, i)
            add_x(2, 0, 1)
            with pool.Fori(1, CHUNKS // 2 - 1) as r:
                for b in range(2):
                    i = 2 * r + b
                    add_x(i + 1, 1 - b, r + b)
                    add_bias(i, b)
            add_x(CHUNKS - 1, 1, CHUNKS // 2 - 1)
            add_bias(CHUNKS - 2, 0)
            add_bias(CHUNKS - 1, 1)

        @block.scalar
        def _(act):
            a = nc.scalar

            def weights(to, of, s, scale=WS):
                a.activation(to, of, ACT.Copy, scale=scale).then_inc(s, 1)
            act.wait_ge(loaded_w, 16 * LOADS_W)
            c0, c1 = KB * 3 * D, KB * 4 * D
            flat = lambda w: w.rearrange("p k n -> p (k n)")
            a.activation(raw[:, 0:c1], raw[:, 0:c1], ACT.Copy, scale=WS).then_inc(scaled, 1)
            act.wait_ge(scaled, 1)
            weights(flat(wqkv_s[:, 0]), raw[:, 0:c0], weights_high, 1.0)
            weights(flat(wg_s[:, 0]), raw[:, c0:c1], weights_high, 1.0)
            weights(pbd[:, 0, :], raw[:, c1:c1 + 2 * NF], weights_high, 1.0)
            act.wait_ge(loaded_w2, 64)
            c0, c1 = KB * HID, KB * HID + JB * D
            wproj_raw = raw[:, c1:c1 + KB * D]
            a.activation(wproj_raw, wproj_raw, ACT.Copy, scale=WS).then_inc(scaled, 1)
            weights(flat(w1_s[:, 0]), raw[:, 0:c0], weights_high)
            weights(flat(w2_s[:, 0]), raw[:, c0:c1], weights_high)
            act.wait_ge(scaled, 2)
            weights(flat(wproj_s[:, 0]), wproj_raw, weights_high, 1.0)
            act.wait_ge(setup_left, 2)

            def both(t_slot, high, of, func, **kw):
                a.activation(t_slot, of, func, **kw).then_inc(tmp_made, 1)
                a.activation(high, of, func, **kw).then_inc(hi_made, 1)

            def z_high(i, k):
                act.wait_ge(tr_full, i * TR_A + (k + 1))
                both(tmp[:, k, :], hT[:, 0, k, :], ps[:, TR0 + k % 2, :], ACT.Identity, bias=be1c[:, k:k + 1],
                     scale=g1c[:, k:k + 1])

            def x_high(i, k):
                act.wait_ge(tr_full, i * TR_A + (KB + k + 1))
                a.activation(xT[:, 0, k, :], ps[:, TR0 + k % 2, :], ACT.Copy).then_inc(hi_made, 1)

            def make_z(i):
                hold(act, z_ready, i + 1)
                for t in range(NT):
                    a.activation(xz[:, t, :], xn[:, t, :], ACT.Identity, bias=shift[:, t:t + 1],
                                 scale=rstd[:, t:t + 1]).then_inc(z_made, 1)
            make_z(0)
            for k in range(KB):
                z_high(0, k)
            for k in range(KB):
                x_high(0, k)

            def a_chunk(i, last=False):
                mm, hi, lo, tm = A_LAST if last else A_BODY
                tmps = list(tm)

                def slot(key):
                    u = tm[key]
                    if u >= MMB:
                        hold(act, lo_made, a_val(2, i, tmps[u - MMB], last))
                    elif isinstance(i, int) and i == 0:
                        act.wait_ge(lo_made, u + 1)
                    else:
                        hold(act, lo_made, a_val(2, i - 1, ("e", MS - MMB + u)))
                    return tmp[:, u % MMB, :]
                later = not (isinstance(i, int) and i == 0)
                if later:
                    hold(act, q_stored, i * 16)
                for part, to, bias in (("q", qT, bq), ("k", kT, bk)):
                    for j in range(4):
                        s = slot((part, j))
                        act.wait_ge(mm_full, mm_a(i, (part, j)))
                        both(s, to[:, 0, j, :], mm_bank(MM_A[part, j]), ACT.Identity, bias=bias[:, j:j + 1],
                             scale=1.0 / WS)
                if not last:
                    make_z(i + 1)
                for t in range(NT):
                    act.wait_ge(mm_full, mm_a(i, ("v", t)))
                    a.activation(v[:, 0, t, :, 0:DH], mm_bank(MM_A["v", t]).rearrange("p (h e) -> p h e", e=DH),
                                 ACT.Copy, scale=1.0 / WS).then_inc(hi_made, 1)
                if not last:
                    for k in range(KB):
                        act.wait_ge(tr_full, (i + 1) * TR_A + (k + 1))
                        s = slot(("z", k))
                        both(s, hT[:, 0, k, :], ps[:, TR0 + k % 2, :], ACT.Identity, bias=be1c[:, k:k + 1],
                             scale=g1c[:, k:k + 1])

                def e_high(m):
                    act.wait_ge(exp_made, i * MS + (m + 1))
                    a.activation(kp[:, m // NT % 2, 0, m % NT, :], tmp[:, tm["e", m] % MMB, :], ACT.Copy, scale=FS)\
                        .then_inc(hi_made, 1)
                for h in range(PAIRS):
                    for t in range(NT):
                        m = NT * h + t
                        s = slot(("e", m))
                        hold(act, max_made, i * MS + (m + 1))
                        for e in range(2):
                            ins = a.activation(s[:, e * NF:(e + 1) * NF],
                                               mm_bank(MM_A["e", m])[:, e * NF:(e + 1) * NF], ACT.Exp,
                                               bias=nmax[:, m, e:e + 1])
                        ins.then_inc(exp_made, 1)
                        if m:
                            e_high(m - 1)
                    if h == 0 and later:
                        hold(act, h_stored, i * 16)
                    act.wait_ge(mm_full, mm_a(i, ("g", h)))
                    a.activation(hb[:, h, 0, :], mm_bank(MM_A["g", h]), ACT.Copy, scale=1.0 / WS).then_inc(hi_made, 1)
                e_high(MS - 1)
                if not last:
                    for k in range(KB):
                        x_high(i + 1, k)
            a_chunk(0)
            with act.Fori(1, CHUNKS - 1) as i:
                a_chunk(i)
            a_chunk(CHUNKS - 1, last=True)
            act.sem_inc(phase_done, 1)
            act.wait_ge(phase_done, 4)

            def b_chunk(i):
                first = isinstance(i, int) and i == 0
                for n in range(B_STEPS):
                    if n < MS:
                        act.wait_ge(max_made, i * MS + (CHUNKS * MS + n + 1))
                        for e in range(2):
                            ins = a.activation(qp[:, n % 2, e * NF:(e + 1) * NF],
                                               bank_b(i, ("e", n))[:, e * NF:(e + 1) * NF], ACT.Exp,
                                               bias=nmax[:, n, e:e + 1])
                        ins.then_inc(exp_made, 1)
                    if 1 <= n <= MS:
                        m = n - 1
                        if m >= 2:
                            hold(act, att_full, i * MS + (m - 1))
                        act.wait_ge(tr_full, i * len(TR_B) + (TR_B0 + TR_B["q", m] + 1))
                        a.activation(qpT[:, m % 2, :, :], ps[:, TR0, :], ACT.Copy).then_inc(qpT_made, 1)
                    if ("att", (n - 6) // 4) in TR_B and (n - 6) % 4 == 0:
                        t = (n - 6) // 4
                        if t >= 2:
                            hold(act, mm_full, mm_b(i, ("proj", t - 2)))
                        act.wait_ge(tr_full, i * len(TR_B) + (TR_B0 + TR_B["att", t] + 1))
                        a.activation(attT[:, t % 2, 0, :, :], ps[:, TR0, :], ACT.Copy).then_inc(hi_made, 1)

                def slot(u):
                    if u >= MMB:
                        key = ("h", u - MMB) if u < 2 * MMB else ("up", u - 2 * MMB)
                        hold(act, lo_made, b_val(i, key))
                    elif not first:
                        hold(act, lo_made, b_val(i - 1, ("up", JB - MMB + u)))
                    return tmp_b[:, u % MMB, :]
                for k in range(KB):
                    s = slot(k)
                    act.wait_ge(tr_full, i * len(TR_B) + (TR_B0 + TR_B["h", k] + 1))
                    both(s, h2T[:, 0, k, :], ps[:, TR0 + k % 2, :], ACT.Identity, bias=be2c[:, k:k + 1], scale=g2c[:, k:k + 1])
                for j in range(JB):
                    s = slot(KB + j)
                    act.wait_ge(mm_full, mm_b(i, ("up", j)))
                    both(s, gT[:, 0, j, :], bank_b(i, ("up", j)), ACT.Gelu, bias=b1c[:, j:j + 1], scale=1.0 / WS)
            b_chunk(0)
            with act.Fori(1, CHUNKS) as i:
                b_chunk(i)
            act.wait_ge(tril_made, 2 * KB)
            act.wait_ge(mm_full, MM_D0)
            weights(flat(f1_s[:, 0]), flat(f1_raw), ffn_high)
            weights(flat(f2_s[:, 0]), flat(f2_raw), ffn_high)
            act.sem_inc(phase_done, 1)
            act.wait_ge(phase_done, 9)

            def c_chunk(i, b):
                first = isinstance(i, int) and i == 0
                for k in range(KB):
                    act.wait_ge(tr_full, i * KB + (TR_C0 + k + 1))
                    a.activation(z3T[:, 0, k, :], ps[:, Z3_BANKS[k], :], ACT.Copy).then_inc(hi_made, 1)
                for j in range(KB):
                    if not first:
                        hold(act, lo_made, c_val(i - 1, ("f", j)))
                    act.wait_ge(mm_full, mm_f1(i, j))
                    both(tmp_c[:, j, :], fT[:, b, 0, j, :], mm_bank(j), ACT.Gelu, bias=fb1c[:, j:j + 1],
                         scale=1.0 / WS)
            c_chunk(0, 0)
            with act.Fori(0, CHUNKS // 2 - 1) as r:
                c_chunk(2 * r + 1, 1)
                c_chunk(2 * r + 2, 0)
            c_chunk(CHUNKS - 1, 1)

        @block.vector
        def _(dve):
            vec = nc.vector
            ch = Chain()

            def link(ins):
                ch.step(ins)
                hold(dve, dve_done, ch.value())

            def settle():
                hold(dve, dve_done, ch.value())

            norm_at = {}
            ROOT = 3 + 3 * 3
            dve.sem_inc(kv_free, 1)
            dve.sem_inc(rank_free, 1)
            dve.sem_inc(acc_made, ACC_CREDIT)
            dve.sem_inc(out_made, OUT_CREDIT)
            link(vec.memset(slots[:, :, :], 0.0))
            dve.sem_inc(slots_cleared, 1)
            vec.memset(kv[:, :, :, :], 0.0)
            vec.memset(keep[:, 0:1], 0.0)
            vec.memset(block_of[0:1, SUPERS:SUPERS + 1], BLOCKS)
            dve.wait_ge(consts_made, EARLY_CONSTS)
            vec.tensor_copy(lane_ids[:, :], lane_i)
            vec.tensor_copy(block_ids[:, :], blkid_i)
            vec.tensor_copy(blkid_f, blkid_i)
            vec.tensor_copy(row_f[:, 0:1], toti[:, 0:1])
            vec.tensor_copy(sup_f, sup_i)
            dve.wait_ge(loaded_edges, 16)
            link(vec.tensor_scalar(lanei, srci, P - 1, None, ALU.bitwise_and))
            link(vec.tensor_scalar(srci, srci, 7, None, ALU.logical_shift_right))
            dve.wait_ge(zeroed, 16)
            link(vec.tensor_copy(bucket, srci))
            vec.tensor_copy(rec[:, :, 0], lanei).then_inc(lanes_made, 1)

            def one_block(k, b):
                return vec.tensor_scalar(ohb[:, b, :], bucket, blkid_f[:, bass.ds(k, 1)], None, ALU.is_equal)\
                    .then_inc(onehot_made, 1)
            for b in range(OHB):
                one_block(b, b)
            with dve.Fori(1, BLOCKS // OHB) as r:
                for b in range(OHB):
                    if b % 2 == 0:
                        hold(dve, counted, r * OHB + (b + 2 - OHB))
                    one_block(OHB * r + b, b)

            def low(to, of, high, s, scale=WS):
                vec.scalar_tensor_tensor(to, of, scale, high, ALU.mult, ALU.subtract).then_inc(s, 1)
            flat = lambda w: w.rearrange("p k n -> p (k n)")
            c0, c1 = KB * 3 * D, KB * 4 * D
            dve.wait_ge(counted, BLOCKS + 1)
            vec.memset(runs[:, 0, 0:1], 0.0)
            vec.tensor_copy(runs[:, 0, 1:HALF], ps[:, RANK_BANK, 0:HALF - 1])
            link(vec.tensor_copy(count, ps[:, RANK_BANK, :]))
            k, d = 0, 1
            while d < HALF:
                vec.tensor_copy(runs[:, 1 - k, 0:d], runs[:, k, 0:d])
                link(vec.tensor_tensor(runs[:, 1 - k, d:HALF], runs[:, k, d:HALF], runs[:, k, 0:HALF - d], ALU.add))
                k, d = 1 - k, 2 * d
            vec.tensor_tensor(tot[:, 0:1], runs[:, k, HALF - 1:HALF], count[:, HALF - 1:HALF], ALU.add)\
                .then_inc(dve_setup, 1)
            dve.wait_ge(pe_setup, 1)
            vec.tensor_copy(tot[:, 1:2], ps[:, 5, 0:1])
            link(vec.tensor_scalar(toti[:, 0:1], ps[:, 6, 0:1], float(SUP_EDGES - 1), None, ALU.add))
            link(vec.tensor_scalar(toti[:, 1:2], toti[:, 0:1], 8, None, ALU.logical_shift_right))
            vec.tensor_scalar(supn[:, 0:1], toti[:, 1:2], 1.0, None, ALU.max).then_inc(dve_setup, 1)
            dve.wait_ge(pe_setup, 2)
            link(vec.tensor_copy(ends[:, 0:1], ps[:, 4, 0:1]))
            link(vec.tensor_tensor(ends[:, 1:2], ends[:, 0:1], supn[:, 0:1], ALU.subtract))
            link(vec.scalar_tensor_tensor(ends[:, 1:2], ends[:, 1:2], float(SUP_EDGES), tot[:, 1:2],
                                          ALU.mult, ALU.add))
            vec.tensor_scalar(passed[0:BLOCKS, :], sup_f[0:BLOCKS, :], ends[0:BLOCKS, 0:1], None, ALU.is_ge)
            vec.tensor_scalar(firstf, runs[:, k, :], ends[:, 1:2], None, ALU.add).then_inc(dve_setup, 1)
            dve.wait_ge(pe_setup, 3)
            half = SUPERS // 2
            for h in range(2):
                vec.tensor_scalar(blk_f[:, h * half:(h + 1) * half], ps[:, 2 + h, 0:half], float(BLOCKS - 1), None,
                                  ALU.min)
            link(vec.tensor_copy(firstT, ps[:, 0, :]))
            vec.tensor_tensor(keep[:, 1:SUPERS], blk_f[:, 1:SUPERS], blk_f[:, 0:SUPERS - 1], ALU.is_equal)
            vec.tensor_copy(block_of[0:1, 0:SUPERS], blk_f[0:1, :])
            vec.tensor_scalar(hi_i, firstT, 7, None, ALU.logical_shift_right)
            link(vec.tensor_scalar(lo_i, firstT, P - 1, None, ALU.bitwise_and))
            vec.tensor_copy(hl[:, 0, :], hi_i)
            vec.tensor_copy(hl[:, 1, :], lo_i).then_inc(first_split, 1)
            dve.wait_ge(loaded_w2, 64)
            link(vec.tensor_scalar(bv_raw[0:2, :], bv_raw[0:2, :], WS, None, ALU.mult))
            link(vec.tensor_copy(bv_h[0:2, :], bv_raw[0:2, :]))
            link(vec.scalar_tensor_tensor(bv2[:, :], bv_h[0:2, :], row_f[0:2, 0:1], bv_raw[0:2, :],
                                          ALU.mult, ALU.subtract))
            dve.wait_ge(weights_high, 6)
            c0, c1 = KB * HID, KB * HID + JB * D
            low(flat(w1_s[:, 1]), raw[:, 0:c0], flat(w1_s[:, 0]), weights_low)
            low(flat(w2_s[:, 1]), raw[:, c0:c1], flat(w2_s[:, 0]), weights_low)
            dve.wait_ge(weights_low, 2)
            dve.wait_ge(first_stored, 64)
            dve.sem_inc(setup_left, 1)
            dve.wait_ge(setup_left, 2)
            vec.memset(v[:, 0, :, :, DH:VW], 1.0)
            link(vec.memset(v[:, 1, :, :, DH:VW], 0.0))

            def root_part(p):
                if p:
                    hold(dve, dve_done, norm_at["root"])
                if p == 0:
                    ins = vec.tensor_scalar(vpe[:, :], mv[:, :, 1], EPS, None, ALU.add)
                elif p == 1:
                    ins = vec.tensor_scalar(guess[:, :], vpe[:, :].bitcast(I32), 1, None, ALU.logical_shift_right)
                elif p == 2:
                    ins = vec.tensor_scalar(rstd[:, :].bitcast(I32), guess[:, :], -1.0, float(0x5F3759DF),
                                            ALU.mult, ALU.add)
                elif p % 3 == 0:
                    ins = vec.scalar_tensor_tensor(half_vy[:, :], rstd[:, :], -0.5, rstd[:, :], ALU.mult, ALU.mult)
                elif p % 3 == 1:
                    ins = vec.tensor_tensor(half_vy[:, :], half_vy[:, :], vpe[:, :], ALU.mult)
                else:
                    ins = vec.scalar_tensor_tensor(rstd[:, :], half_vy[:, :], 1.5, rstd[:, :], ALU.add, ALU.mult)
                ch.step(ins)
                norm_at["root"] = ch.value()

            def statistics(of):
                for t in range(NT):
                    last = vec.bn_stats(stats[:, t, :], of[:, t, :])
                link(last)
                for t in range(NT):
                    last = vec.bn_aggr(mv[:, t, :], stats[:, t, :])
                link(last)

            def apply(to, of):
                hold(dve, dve_done, norm_at["root"])
                for t in range(NT):
                    last = vec.tensor_scalar(to[:, t, :], of[:, t, :], mv[:, t, 0:1], rstd[:, t:t + 1],
                                             ALU.subtract, ALU.mult)
                return last

            def normalise(to, of):
                statistics(of)
                for p in range(ROOT):
                    root_part(p)
                return apply(to, of)

            def norm_x(i):
                hold(dve, x_loaded, (i + 1) * 16)
                if not (isinstance(i, int) and i == 0):
                    hold(dve, xn_stored, i * 16)
                    hold(dve, tr_full, i * TR_A)
                    hold(dve, z_made, i * NT)
                normalise(xn, xz).then_inc(xn_made, 1)
                hold(dve, xn_made, i + 1)

            def norm_z(i):
                statistics(xn)
                for p in range(ROOT):
                    root_part(p)
                hold(dve, dve_done, norm_at["root"])
                vec.scalar_tensor_tensor(shift[:, :], mv[:, :, 0], -1.0, rstd[:, :], ALU.mult, ALU.mult)\
                    .then_inc(z_ready, 1)

            def rank_onehot(i, r):
                vec.tensor_tensor(
                    onehot[:, r % 2, :, :],
                    bucket[:, bass.ds(i * CCOLS + r * SORT_COLS, SORT_COLS)].unsqueeze(2)
                    .broadcast_to([P, SORT_COLS, BLOCKS]),
                    block_ids[:, :].unsqueeze(1).broadcast_to([P, SORT_COLS, BLOCKS]), ALU.is_equal)\
                    .then_inc(onehot_made, 1)

            def rank(i, r):
                hold(dve, rank_full, i * SORT_STEPS + (r + 1))
                settle()
                vec.tensor_tensor(picked, ps[:, RANK_BANK, :].rearrange("p (c b) -> p c b", b=BLOCKS),
                                  onehot[:, r % 2, :, :], ALU.mult).then_inc(rank_free, 1)
                hold(dve, rank_free, i * SORT_STEPS + (r + 2))
                ch.step(vec.tensor_reduce(pos[:, r * SORT_COLS:(r + 1) * SORT_COLS], picked, X, ALU.add))
                if r + 2 < SORT_STEPS:
                    rank_onehot(i, r + 2)

            def z_low(i, k, slot, value):
                hold(dve, hi_made, value)
                vec.tensor_tensor(hT[:, 1, k, :], tmp[:, slot, :], hT[:, 0, k, :], ALU.subtract).then_inc(lo_made, 1)

            def x_low(i, k, value):
                hold(dve, hi_made, value)
                vec.tensor_tensor(xT[:, 1, k, :], ps[:, TR0 + k % 2, :], xT[:, 0, k, :], ALU.subtract)\
                    .then_inc(lo_made, 1)
            norm_x(0)
            norm_z(0)
            dve.wait_ge(z_made, NT)
            for k in range(KB):
                z_low(0, k, k, k + 1)
            for k in range(KB):
                x_low(0, k, KB + k + 1)

            def kv_add(i, h):
                hold(dve, kv_full, i * PAIRS + (h + 1))
                to = kv[:, 2 * h:2 * h + 2, :, :].rearrange("p h c e -> p (h c e)")
                vec.scalar_tensor_tensor(to, ps[:, KV_BANK, 0:4 * VW], 1.0 / (FS * float(NF) ** 0.5), to,
                                         ALU.mult, ALU.add).then_inc(kv_free, 1)

            def a_chunk(i, last=False):
                mm, hi, lo, tm = A_LAST if last else A_BODY
                high = lambda key: a_val(1, i, key, last)
                settle()
                rank_onehot(i, 0)
                rank_onehot(i, 1)
                if not last:
                    norm_x(i + 1)

                def qk_low(part, to, j):
                    hold(dve, hi_made, high((part, j)))
                    vec.tensor_tensor(to[:, 1, j, :], tmp[:, tm[part, j] % MMB, :], to[:, 0, j, :], ALU.subtract)\
                        .then_inc(lo_made, 1)
                for j in range(4):
                    qk_low("q", qT, j)
                    if j == 1:
                        rank(i, RANK_Q)
                if not last:
                    norm_z(i + 1)
                for j in range(4):
                    qk_low("k", kT, j)
                    if j == 3:
                        rank(i, RANK_K)
                for t in range(NT):
                    hold(dve, hi_made, high(("v", t)))
                    vec.scalar_tensor_tensor(v[:, 1, t, :, 0:DH],
                                             mm_bank(MM_A["v", t]).rearrange("p (h e) -> p h e", e=DH), 1.0 / WS,
                                             v[:, 0, t, :, 0:DH], ALU.mult, ALU.subtract).then_inc(lo_made, 1)
                    if t < len(RANK_V):
                        rank(i, RANK_V[t])
                if not last:
                    for k in range(KB):
                        z_low(i + 1, k, tm["z", k] % MMB, high(("z", k)))

                def e_low(m):
                    hold(dve, hi_made, high(("e", m)))
                    vec.scalar_tensor_tensor(kp[:, m // NT % 2, 1, m % NT, :], tmp[:, tm["e", m] % MMB, :], FS,
                                             kp[:, m // NT % 2, 0, m % NT, :], ALU.mult, ALU.subtract)\
                        .then_inc(lo_made, 1)

                def g_low(h):
                    hold(dve, hi_made, high(("g", h)))
                    vec.scalar_tensor_tensor(hb[:, h, 1, :], mm_bank(MM_A["g", h]), 1.0 / WS, hb[:, h, 0, :],
                                             ALU.mult, ALU.subtract).then_inc(lo_made, 1)
                for h in range(PAIRS):
                    for t in range(NT):
                        m = NT * h + t
                        hold(dve, mm_full, mm_a(i, ("e", m)))
                        vec.tensor_reduce(nmax[:, m, :], mm_bank(MM_A["e", m]).rearrange("p (e f) -> p e f", e=2),
                                          X, ALU.max, negate=True).then_inc(max_made, 1)
                        if m >= 2:
                            e_low(m - 2)
                        if t == 0 and h:
                            g_low(h - 1)
                        if t == 0 and h >= 2:
                            kv_add(i, h - 2)
                        if t == 1 and h:
                            rank(i, RANK_E[h - 1])
                g_low(PAIRS - 1)
                e_low(MS - 2)
                e_low(MS - 1)
                if not last:
                    for k in range(2):
                        x_low(i + 1, k, high(("x", k)))
                kv_add(i, PAIRS - 2)
                if not last:
                    for k in range(2, KB):
                        x_low(i + 1, k, high(("x", k)))
                settle()
                link(vec.tensor_copy(posi, pos))
                vec.tensor_scalar(posl, posi, P - 1, None, ALU.bitwise_and)
                link(vec.tensor_scalar(post, posi, 7, None, ALU.logical_shift_right))
                vec.scalar_tensor_tensor(addr[:, bass.ds(i * CCOLS, CCOLS)], posl, float(TILES), post,
                                         ALU.mult, ALU.add).then_inc(addr_made, 1)
                hold(dve, addr_made, i + 1)
                kv_add(i, PAIRS - 1)
                hold(dve, kv_free, i * PAIRS + (PAIRS + 1))

            A_LINKS = 2 * (2 + ROOT) + SORT_STEPS + 2
            ch.enter(0, A_LINKS)
            a_chunk(0)
            ch.leave(1)
            with dve.Fori(1, CHUNKS - 1) as i:
                ch.enter(i, A_LINKS, 1)
                a_chunk(i)
            ch.leave(CHUNKS - 2)
            a_chunk(CHUNKS - 1, last=True)
            link(vec.tensor_scalar(kv[:, :, :, DH:VW], kv[:, :, :, DH:VW], KSUM_EPS, None, ALU.add))
            dve.sem_inc(phase_done, 1)
            dve.wait_ge(phase_done, 4)
            link(vec.memset(acc[:, AR - 1, :], 0.0))
            dve.wait_ge(brow_loaded, 32)

            def make_oh(s, b):
                for t in range(SUP):
                    c = s * SUP + t
                    w = slots16[:, bass.ds(c, 1), 2:4].rearrange("p a h -> p (a h)")
                    last = vec.scalar_tensor_tensor(
                        oh[:, b * SUP + t, :, :], lane_ids[:, :].unsqueeze(1).broadcast_to([P, 2, P]),
                        slots[:, bass.ds(c, 1), 0], w.unsqueeze(2).broadcast_to([P, 2, P]), ALU.is_equal, ALU.mult)
                last.then_inc(oh_made, 1)

            def seg_sum(i, k):
                s = (i - B1) * SEG + k
                hold(dve, seg_full, s + (SEG_CREDIT + 1))
                hold(dve, acc_saved, s + 1)
                hold(dve, acc_made, s + ACC_CREDIT)
                vec.scalar_tensor_tensor(acc[:, k % AR, :], acc[:, (k - 1) % AR, :], keep[:, bass.ds(s, 1)],
                                         ps[:, SEG0 + k % 2, :], ALU.mult, ALU.add).then_inc(acc_made, 1)

            def seg_oh(i, k):
                make_oh((i - B1) * SEG + (k + 2), k % 2)

            def seg(i, k):
                seg_sum(i, k)
                seg_oh(i, k)

            def norm_part(i, t, p):
                y, c = rstd[:, t:t + 1], slice(t, t + 1)
                if p:
                    hold(dve, dve_done, norm_at[t])
                if p == 0:
                    ins = vec.bn_stats(stats[:, t, :], x1[:, t, :])
                elif p == 1:
                    ins = vec.bn_aggr(mv[:, t, :], stats[:, t, :])
                elif p == 2:
                    ins = vec.tensor_scalar(vpe[:, c], mv[:, c, 1], EPS, None, ALU.add)
                elif p == 3:
                    vec.tensor_scalar(half_vy[:, c], vpe[:, c], -0.5, None, ALU.mult)
                    ins = vec.tensor_scalar(guess[:, c], vpe[:, c].bitcast(I32), 1, None, ALU.logical_shift_right)
                elif p == 4:
                    ins = vec.tensor_scalar(y.bitcast(I32), guess[:, c], -1.0, float(0x5F3759DF), ALU.mult, ALU.add)
                elif p == 11:
                    vec.tensor_scalar(z2[:, t, :], x1[:, t, :], mv[:, t, 0:1], y, ALU.subtract, ALU.mult)\
                        .then_inc(z2_made, 1)
                    return
                elif p % 2:
                    ins = vec.scalar_tensor_tensor(vpe[:, c], y, y, half_vy[:, c], ALU.mult, ALU.mult)
                else:
                    ins = vec.scalar_tensor_tensor(y, vpe[:, c], 1.5, y, ALU.add, ALU.mult)
                ch.step(ins)
                norm_at[t] = ch.value()

            def take_down(i, t):
                dve.wait_ge(mm_full, mm_down(i, t))
                bank = mm_bank(t) if isinstance(i, int) and i == CHUNKS - 1 else mm_bank(MM_B["down", t])
                y = x1[:, t, :] if t < NT - 1 else y3
                vec.scalar_tensor_tensor(y, bank, 1.0 / WS, y, ALU.mult, ALU.add)\
                    .then_inc(y_made, 1)

            def add_b2(i, a, b):
                hold(dve, z2_made, i * NT + b)
                to = x1[:, a:b, :]
                if b == NT:
                    to = y3.rearrange("p (t n) -> p t n", t=1)
                    if not (isinstance(i, int) and i == 0):
                        hold(dve, y3_stored, i * 16)
                link(vec.tensor_tensor(to, x1[:, a:b, :],
                                       brow[:, 1, :].unsqueeze(1).broadcast_to([P, b - a, D]), ALU.add))

            def b_chunk(i, count):
                first = isinstance(i, int) and i == 0
                todo = seg_plan(count)
                done = [0]

                def fill(n):
                    for _ in range(n):
                        seg(i, done[0])
                        done[0] += 1
                for n in range(B_STEPS):
                    t_norm, at_norm = divmod(n - 8, 4)

                    def part(k):
                        if 0 <= t_norm < NT - 1:
                            norm_part(i, t_norm, 3 * at_norm + k)
                    if at_norm:
                        part(0)
                    if 3 <= n < MS + 3:
                        m = n - 3
                        t, h = m // PAIRS, m % PAIRS
                        hold(dve, att_full, i * MS + (m + 1))
                        ch.step(vec.reciprocal(rden[:, m, :], att_out[:, :, DH]))
                        made = ch.value()
                        if at_norm:
                            part(1)
                        hold(dve, dve_done, made)
                        vec.tensor_tensor(att[:, t % 2, h * P:(h + 1) * P].rearrange("p (h e) -> p h e", e=DH),
                                          att_out[:, :, 0:DH], rden[:, m, :].unsqueeze(2).broadcast_to([P, 2, DH]),
                                          ALU.mult).then_inc(att_made, 1)
                    elif at_norm:
                        part(1)
                    if n < MS:
                        dve.wait_ge(mm_full, mm_b(i, ("e", n)))
                        vec.tensor_reduce(nmax[:, n, :], bank_b(i, ("e", n)).rearrange("p (e f) -> p e f", e=2),
                                          X, ALU.max, negate=True).then_inc(max_made, 1)
                    if not first and 2 <= n <= NT:
                        take_down(i - 1, n - 2)
                    if n == 6:
                        hold(dve, xnb_loaded, i * 16 + 16)
                        vec.tensor_tensor(xnb, xnb, brow[:, 0, :].unsqueeze(1).broadcast_to([P, NT, D]), ALU.add)\
                            .then_inc(xb_made, 1)
                    if n >= 8 and n % 4 == 0:
                        t = n // 4 - 2
                        u = ("proj", t)
                        if t == 0:
                            hold(dve, xb_made, i + 1)
                            if not first:
                                hold(dve, y_stored, i * 16)
                        dve.wait_ge(mm_full, mm_b(i, u))
                        vec.scalar_tensor_tensor(x1[:, t, :], bank_b(i, u), 1.0 / WS, xnb[:, t, :],
                                                 ALU.mult, ALU.add).then_inc(x1_made, 1)
                        hold(dve, x1_made, i * NT + (t + 1))
                        if t < NT - 1:
                            part(0)
                            fill(min(1, todo[n]))
                            part(1)
                            fill(max(0, todo[n] - 1))
                        else:
                            for p in range(5):
                                norm_part(i, t, p)
                            for k in range(2):
                                if count:
                                    seg_sum(i, done[0])
                                norm_part(i, t, 5 + 2 * k)
                                if count:
                                    seg_oh(i, done[0])
                                    done[0] += 1
                                norm_part(i, t, 6 + 2 * k)
                            assert todo[n] == (2 if count else 0)
                            for p in range(9, 12):
                                norm_part(i, t, p)
                            if not first:
                                take_down(i - 1, NT - 1)
                    else:
                        fill(todo[n])
                    part(2)
                    if n >= 6 and (n - 6) % 4 == 0 and (n - 6) // 4 < NT:
                        t = (n - 6) // 4
                        hold(dve, hi_made, b_val(i, ("att", t)))
                        vec.tensor_tensor(attT[:, t % 2, 1, :, :].rearrange("p k n -> p (k n)"), ps[:, TR0, :],
                                          attT[:, t % 2, 0, :, :].rearrange("p k n -> p (k n)"), ALU.subtract)\
                            .then_inc(lo_made, 1)
                for part, to, count_, u0 in (("h", h2T, KB, 0), ("up", gT, JB, KB)):
                    if part == "up":
                        add_b2(i, 0, NT - 1)
                        add_b2(i, NT - 1, NT)
                    for k in range(count_):
                        hold(dve, hi_made, b_val(i, (part, k)))
                        vec.tensor_tensor(to[:, 1, k, :], tmp_b[:, (u0 + k) % MMB, :], to[:, 0, k, :], ALU.subtract)\
                            .then_inc(lo_made, 1)
                        fill(todo[B_STEPS + u0 + k])

            B_LINKS = MS + 11 * NT + 2
            ch.enter(0, B_LINKS)
            b_chunk(0, 0)
            ch.leave(1)
            dve.wait_ge(slots_loaded, 16)
            link(vec.memset(slots[:, TILES:TILES + 4, :], 0.0))
            make_oh(0, 0)
            make_oh(1, 1)
            with dve.Fori(B1, CHUNKS - 1) as i:
                ch.enter(i, B_LINKS, B1)
                b_chunk(i, SEG)
            ch.leave(CHUNKS - B1 - 1)
            b_chunk(CHUNKS - 1, SEG_LAST)
            dve.wait_ge(ffn_high, 2)
            low(flat(f1_s[:, 1]), flat(f1_raw), flat(f1_s[:, 0]), ffn_low)
            low(flat(f2_s[:, 1]), flat(f2_raw), flat(f2_s[:, 0]), ffn_low)
            for t in range(NT):
                take_down(CHUNKS - 1, t)
            dve.wait_ge(ffn_low, 2)
            dve.wait_ge(oh_made, SUPERS + 2)
            dve.sem_inc(phase_done, 1)
            dve.wait_ge(phase_done, 9)

            def take_sum(i, b, r):
                hold(dve, yx_made, i + 1)
                hold(dve, agg_loaded[b], r * 16 + 16)
                for t in range(NT):
                    vec.tensor_tensor(yb[:, b, t, :], aggb[:, b, t, :], yb[:, b, t, :], ALU.add).then_inc(x2_made, 1)
                hold(dve, x2_made, i * NT + NT)
                statistics(yb[:, b, :, :])

            def put_z3(i, b, first=False):
                if not first:
                    hold(dve, tr_full, i * KB + TR_C0)
                apply(z3, yb[:, b, :, :]).then_inc(z3_made, 1)
                hold(dve, z3_made, i + 1)

            def z3_low(i):
                for k in range(KB):
                    hold(dve, hi_made, c_val(i, ("z", k)))
                    vec.tensor_tensor(z3T[:, 1, k, :], ps[:, Z3_BANKS[k], :], z3T[:, 0, k, :], ALU.subtract)\
                        .then_inc(lo_made, 1)

            def f_low(i, b, j):
                hold(dve, hi_made, c_val(i, ("f", j)))
                vec.tensor_tensor(fT[:, b, 1, j, :], tmp_c[:, j, :], fT[:, b, 0, j, :], ALU.subtract)\
                    .then_inc(lo_made, 1)

            def put_out(i, b, t):
                if t == 0:
                    hold(dve, x2b_made, i + 1)
                hold(dve, mm_full, mm_f2(i, t))
                vec.scalar_tensor_tensor(outb[:, b, t, :], ps[:, F2_BANKS[t], :], 1.0 / WS,
                                         outb[:, b, t, :], ALU.mult, ALU.add).then_inc(out_made, 1)

            def c_chunk(i, b, r):
                z3_low(i + 1)
                take_sum(i + 2, b, r + 1)
                for p in range(ROOT):
                    root_part(p)
                    if p % 3 == 1:
                        f_low(i + 1, 1 - b, p // 3)
                    if p == ROOT - 3:
                        put_out(i, b, 0)
                put_z3(i + 2, b)
                for t in range(1, NT):
                    put_out(i, b, t)

            def alone(i, b, first=False):
                take_sum(i, b, 0)
                for p in range(ROOT):
                    root_part(p)
                put_z3(i, b, first)

            C_LINKS = 2 + ROOT
            alone(0, 0, first=True)
            z3_low(0)
            alone(1, 1)
            for j in range(KB):
                f_low(0, 0, j)
            with dve.Fori(0, CHUNKS // 2 - 1) as r:
                ch.enter(r, 2 * C_LINKS)
                c_chunk(2 * r, 0, r)
                c_chunk(2 * r + 1, 1, r)
            ch.leave(CHUNKS // 2 - 1)
            z3_low(CHUNKS - 1)
            for j in range(KB):
                f_low(CHUNKS - 1, 1, j)
            for i in range(CHUNKS - 2, CHUNKS):
                for t in range(NT):
                    put_out(i, i % 2, t)

        @block.tensor
        def _(pe):
            mm, tr = nc.tensor.matmul, nc.tensor.transpose

            def mm3(bank, pairs, start=True):
                n = len(pairs) * len(PARTS)
                c = 0
                for lhs, rhs in pairs:
                    for p, q in PARTS:
                        ins = mm(bank, lhs[p], rhs[q], start=start and c == 0, stop=c == n - 1)
                        c += 1
                return ins

            pe.wait_ge(consts_made, EARLY_CONSTS)
            pe.wait_ge(onehot_made, 2)
            mm(ps[:, RANK_BANK, :], pick[:, 0:P], ohb[:, 0, 0:HALF], start=True, stop=False)
            with pe.Fori(0, BLOCKS // OHB) as r:
                for b in range(OHB):
                    if b % 2 == 0:
                        hold(pe, onehot_made, OHB * r + (b + 2))
                    for h in range(2):
                        last = mm(ps[:, RANK_BANK, :], pick[:, bass.ds((P - h * BLOCKS - b) - OHB * r, P)],
                                  ohb[:, b, h * HALF:(h + 1) * HALF], start=False, stop=False)
                    last.then_inc(counted, 1)
            mm(ps[:, RANK_BANK, :], pick[:, 0:P], ohb[:, 0, 0:HALF], start=False, stop=True).then_inc(counted, 1)
            pe.wait_ge(consts_made, ALL_CONSTS)
            pe.wait_ge(dve_setup, 1)
            mm(ps[:, 6, 0:1], samehalf, tot[:, 0:1], start=True, stop=True)
            mm(ps[:, 5, 0:1], otherhalf, tot[:, 0:1], start=True, stop=True).then_inc(pe_setup, 1)
            pe.wait_ge(dve_setup, 2)
            mm(ps[:, 4, 0:1], upto[0:BLOCKS, :], supn[0:BLOCKS, 0:1], start=True, stop=True).then_inc(pe_setup, 1)
            pe.wait_ge(dve_setup, 3)
            half = SUPERS // 2
            for h in range(2):
                mm(ps[:, 2 + h, 0:half], ones16[0:BLOCKS, :], passed[0:BLOCKS, h * half:(h + 1) * half],
                   start=True, stop=True)
            for k in range(KB):
                last = tr(ps[:, 0, k * P:(k + 1) * P], firstf[:, k * P:(k + 1) * P], ident[:, :])
            last.then_inc(pe_setup, 1)
            pe.wait_ge(setup_left, 2)
            pe.sem_inc(seg_full, SEG_CREDIT)

            def transposes(bank, of, k):
                for t in range(NT):
                    last = tr(bank[:, t * P:(t + 1) * P], of[:, t, k * P:(k + 1) * P], ident[:, :])
                last.then_inc(tr_full, 1)

            def z_transposes(i, first=False):
                pe.wait_ge(z_made, i * NT + NT)
                for k in range(KB):
                    if k < 2 and not first:
                        pe.wait_ge(lo_made, zx_low(i - 1, ("x", k + 2)))
                    elif k >= 2:
                        pe.wait_ge(hi_made, zx_low(i, ("z", k - 2), 1))
                    transposes(ps[:, TR0 + k % 2, :], xz, k)

            def x_transposes(i, blocks):
                for k in blocks:
                    if k < 2:
                        pe.wait_ge(hi_made, zx_low(i, ("z", k + 2), 1))
                    else:
                        pe.wait_ge(lo_made, zx_low(i, ("x", k - 2)))
                    transposes(ps[:, TR0 + k % 2, :], xn, k)

            def rank(i, r):
                pe.wait_ge(onehot_made, i * SORT_STEPS + (BLOCKS + r + 1))
                pe.wait_ge(rank_free, i * SORT_STEPS + (r + 1))
                if r == 0:
                    pe.wait_ge(first_loaded, i * 64 + 64)
                g, w = 32 * (r // 2), SORT_COLS * BLOCKS
                mm(ps[:, RANK_BANK, :], below[:, :], onehot[:, r % 2, :, :].rearrange("p c b -> p (c b)"),
                   start=True, stop=False)
                mm(ps[:, RANK_BANK, :], hilo[g:g + 2, :], first[g:g + 2, r % 2 * w:(r % 2 + 1) * w],
                   start=False, stop=True).then_inc(rank_full, 1)

            def kv_product(i, h, last):
                pe.wait_ge(lo_made, a_val(2, i, ("e", h * NT + NT - 1), last))
                pe.wait_ge(kv_free, i * PAIRS + (h + 1))
                for r in range(4):
                    e = r // 2
                    ins = mm3(ps[:, KV_BANK, r * VW:(r + 1) * VW],
                              [([kp[:, h % 2, p, t, r * P:(r + 1) * P] for p in range(2)],
                                [v[:, p, t, 2 * h + e, :] for p in range(2)]) for t in range(NT)])
                ins.then_inc(kv_full, 1)

            def a_bank(key, i, last):
                u = MM_A[key]
                j = i
                if u < MMB:
                    if isinstance(i, int) and i == 0:
                        return mm_bank(u)
                    j = i - 1
                name, k = list(MM_A)[(u - MMB) % len(MM_A)]
                late = last and u >= MMB
                if name in ("q", "k"):
                    pe.wait_ge(hi_made, a_val(1, j, (name, k), late))
                elif name in ("v", "g"):
                    pe.wait_ge(lo_made, a_val(2, j, (name, k), late))
                else:
                    pe.wait_ge(exp_made, j * MS + (k + 1))
                return mm_bank(u)

            def a_chunk(i, last=False):
                pe.wait_ge(lo_made, zx_low(i, ("z", KB - 1)))
                both = lambda w, *rest: [w[(slice(None), p) + rest] for p in range(2)]
                al = slice(None)
                for part, off in (("q", 0), ("k", D)):
                    for j in range(4):
                        bank = a_bank((part, j), i, last)
                        mm3(bank, [(both(wqkv_s, k, slice(off + j * P, off + (j + 1) * P)), both(hT, k, al))
                                   for k in range(KB)]).then_inc(mm_full, 1)
                        if part == "q" and j == 1:
                            rank(i, RANK_Q)
                        if part == "k" and j == 3:
                            rank(i, RANK_K)
                for t in range(NT):
                    bank = a_bank(("v", t), i, last)
                    mm(bank, minus[:, :], bv2[:, :], start=True, stop=False)
                    mm3(bank, [(both(hT, k, slice(t * P, (t + 1) * P)), both(wqkv_s, k, slice(2 * D, 3 * D)))
                               for k in range(KB)], start=False).then_inc(mm_full, 1)
                    if t < len(RANK_V):
                        rank(i, RANK_V[t])
                if not last:
                    z_transposes(i + 1)
                pe.wait_ge(lo_made, a_val(2, i, ("k", 3), last))
                for h in range(PAIRS):
                    for t in range(NT):
                        bank = a_bank(("e", NT * h + t), i, last)
                        mm3(bank, [(both(kT, h, slice(t * P, (t + 1) * P)), both(pbd, al))]).then_inc(mm_full, 1)
                    if h == 0:
                        pe.wait_ge(lo_made, zx_low(i, ("x", KB - 1)))
                    bank = a_bank(("g", h), i, last)
                    mm3(bank, [(both(xT, k, slice(h * P, (h + 1) * P)), both(wg_s, k, al)) for k in range(KB)])\
                        .then_inc(mm_full, 1)
                    if h < len(RANK_E):
                        rank(i, RANK_E[h])
                    if 1 <= h < PAIRS - 1:
                        kv_product(i, h - 1, last)
                if not last:
                    x_transposes(i + 1, range(0, 2))
                kv_product(i, PAIRS - 2, last)
                if not last:
                    x_transposes(i + 1, range(2, KB))
                kv_product(i, PAIRS - 1, last)

            z_transposes(0, first=True)
            x_transposes(0, range(KB))
            a_chunk(0)
            with pe.Fori(1, CHUNKS - 1) as i:
                a_chunk(i)
            a_chunk(CHUNKS - 1, last=True)
            pe.sem_inc(phase_done, 1)
            pe.wait_ge(phase_done, 4)

            both = lambda w, *rest: [w[(slice(None), p) + rest] for p in range(2)]
            al = slice(None)

            def seg(i, k):
                s = (i - B1) * SEG + k
                gr = k // GSUP
                if k % GSUP == 0:
                    pe.wait_ge(gathered[gr % GS], (i - B1) * (16 * GT * GROUPS // GS) + (gr // GS + 1) * 16 * GT)
                pe.wait_ge(oh_made, s + 1)
                pe.wait_ge(acc_made, s + 1)
                mm3(ps[:, SEG0 + k % 2, :],
                    [([oh[:, k % 2 * SUP + t, p, :] for p in range(2)],
                      [ring[:, gr % GS, k % GSUP * SUP + t, p * D:(p + 1) * D] for p in range(2)])
                     for t in range(SUP)]).then_inc(seg_full, 1)

            def down(i, t, bank):
                mm3(bank, [(both(gT, j, slice(t * P, (t + 1) * P)), both(w2_s, j, al)) for j in range(JB)])\
                    .then_inc(mm_full, 1)

            def b_chunk(i, count):
                first = isinstance(i, int) and i == 0
                table = MM_B1 if first else MM_B
                todo = seg_plan(count)
                done = [0]

                def fill(n):
                    for _ in range(n):
                        seg(i, done[0])
                        done[0] += 1

                def take(key):
                    u = table[key]
                    if u < MMB:
                        if not first:
                            pe.wait_ge(hi_made, b_val(i - 1, ("up", JB - MMB + u)))
                        return mm_bank(u)
                    name, k = list(table)[u - MMB]
                    if name == "e":
                        pe.wait_ge(exp_made, i * MS + (CHUNKS * MS + k + 1))
                    elif name == "down":
                        pe.wait_ge(y_made, i * NT + (k + 1 - NT))
                    elif name == "proj":
                        pe.wait_ge(x1_made, i * NT + (k + 1))
                    else:
                        pe.wait_ge(hi_made, b_val(i, ("up", k)))
                    return mm_bank(u)

                def take_tr(key):
                    name, k = key
                    if name == "h" and k >= 2:
                        pe.wait_ge(hi_made, b_val(i, ("h", k - 2)))
                    if name == "h":
                        if k == 0:
                            pe.wait_ge(lo_made, b_val(i, ("att", NT - 1)))
                        return ps[:, TR0 + k % 2, :]
                    if TR_B[key] == 0:
                        if not first:
                            pe.wait_ge(hi_made, b_val(i - 1, ("h", 2)))
                    else:
                        name, k = list(TR_B)[TR_B[key] - 1]
                        if name == "q":
                            pe.wait_ge(qpT_made, i * MS + (k + 1))
                        else:
                            pe.wait_ge(lo_made, b_val(i, ("att", k)))
                    return ps[:, TR0, :]
                pe.wait_ge(qb_loaded, i * 16 + 16)
                for n in range(B_STEPS):
                    if n < MS:
                        t, h = n // PAIRS, n % PAIRS
                        bank = take(("e", n))
                        mm3(bank, [(both(qTb, h, slice(t * P, (t + 1) * P)), both(pbd, al))]).then_inc(mm_full, 1)
                    if not first and n in DOWN_AT[:-1]:
                        if n == DOWN_AT[0]:
                            pe.wait_ge(lo_made, b_val(i - 1, ("up", JB - 1)))
                        down(i - 1, DOWN_AT.index(n), take(("down", DOWN_AT.index(n))))
                    fill(min(1, todo[n]))
                    if 1 <= n <= MS:
                        m = n - 1
                        pe.wait_ge(exp_made, i * MS + (CHUNKS * MS + m + 1))
                        bank = take_tr(("q", m))
                        for r in range(4):
                            ins = tr(bank[:, r * P:(r + 1) * P], qp[:, m % 2, r * P:(r + 1) * P], ident[:, :])
                        ins.then_inc(tr_full, 1)
                    fill(max(0, todo[n] - 1))
                    if not first and n == DOWN_AT[-1]:
                        down(i - 1, NT - 1, take(("down", NT - 1)))
                    if 2 <= n < MS + 2:
                        m = n - 2
                        pe.wait_ge(qpT_made, i * MS + (m + 1))
                        if m >= 1:
                            pe.wait_ge(att_made, i * MS + m)
                        h = m % PAIRS
                        for e in range(2):
                            for c in range(2):
                                ins = mm(att_out[:, e, :], qpT[:, m % 2, e * 2 + c, :], kv[:, 2 * h + e, c, :],
                                         start=(c == 0), stop=(c == 1))
                        ins.then_inc(att_full, 1)
                    if n >= 6 and (n - 6) % 4 == 0 and (n - 6) // 4 < NT:
                        t = (n - 6) // 4
                        pe.wait_ge(att_made, i * MS + (t * PAIRS + PAIRS))
                        bank = take_tr(("att", t))
                        for k in range(KB):
                            ins = tr(bank[:, k * P:(k + 1) * P], att[:, t % 2, k * P:(k + 1) * P], ident[:, :])
                        ins.then_inc(tr_full, 1)
                    if n >= 7 and (n - 7) % 4 == 0 and (n - 7) // 4 < NT:
                        t = (n - 7) // 4
                        pe.wait_ge(lo_made, b_val(i, ("att", t)))
                        mm3(take(("proj", t)),
                            [([attT[:, t % 2, p, k, :] for p in range(2)], both(wproj_s, k, al)) for k in range(KB)])\
                            .then_inc(mm_full, 1)
                pe.wait_ge(z2_made, i * NT + NT)
                for k in range(KB):
                    transposes(take_tr(("h", k)), z2, k)
                    fill(todo[B_STEPS + k])
                pe.wait_ge(lo_made, b_val(i, ("h", KB - 1)))
                for j in range(JB):
                    mm3(take(("up", j)), [(both(w1_s, k, slice(j * P, (j + 1) * P)), both(h2T, k, al))
                                          for k in range(KB)]).then_inc(mm_full, 1)
                    fill(todo[B_STEPS + KB + j])

            b_chunk(0, 0)
            with pe.Fori(B1, CHUNKS - 1) as i:
                b_chunk(i, SEG)
            b_chunk(CHUNKS - 1, SEG_LAST)
            pe.wait_ge(lo_made, b_val(CHUNKS - 1, ("up", JB - 1)))
            for t in range(NT):
                down(CHUNKS - 1, t, mm_bank(t))
            pe.sem_inc(phase_done, 1)
            pe.wait_ge(phase_done, 9)

            def first_product(i, first=False):
                pe.wait_ge(z3_made, i + 1)
                for k in range(KB):
                    if not first:
                        pe.wait_ge(hi_made, c_val(i - 1, ("f", k)))
                        pe.wait_ge(lo_made, c_val(i - 1, ("z", k)))
                    transposes(ps[:, Z3_BANKS[k], :], z3, k)
                for j in range(KB):
                    pe.wait_ge(lo_made, c_val(i, ("z", j)))
                    if not first:
                        pe.wait_ge(hi_made, c_val(i - 1, ("f", j)))
                        if j < 2:
                            pe.wait_ge(out_made, i * NT + (OUT_CREDIT - NT + j - 1))
                    mm3(mm_bank(j), [(both(f1_s, k, slice(j * P, (j + 1) * P)), both(z3T, k, al))
                                     for k in range(j + 1)]).then_inc(mm_full, 1)

            def second_product(i, b):
                pe.wait_ge(lo_made, c_val(i, ("f", KB - 1)))
                for t in range(NT):
                    if t < 2 or isinstance(i, int) and i == CHUNKS - 1:
                        pe.wait_ge(out_made, i * NT + (OUT_CREDIT - NT + t + 1))
                    else:
                        pe.wait_ge(hi_made, c_val(i + 1, ("f", t - 2)))
                    bank = ps[:, F2_BANKS[t], :]
                    for k in range(KB):
                        for c, (p, q) in enumerate(PARTS):
                            ins = mm(bank[:, k * P:D], fT[:, b, p, k, t * P:(t + 1) * P], f2_s[:, q, k, k * P:D],
                                     start=(k == 0 and c == 0), stop=(k == KB - 1 and c == len(PARTS) - 1))
                    ins.then_inc(mm_full, 1)

            first_product(0, first=True)
            with pe.Fori(0, CHUNKS // 2 - 1) as r:
                for b in range(2):
                    first_product(2 * r + b + 1)
                    second_product(2 * r + b, b)
            first_product(CHUNKS - 1)
            second_product(CHUNKS - 2, 0)
            second_product(CHUNKS - 1, 1)


def kernel(x, src, dst, edge_weight, L0_gnn_weight, L0_mix_Wqkv, L0_mix_bqkv, L0_mix_Pmat, L0_mix_Wproj, L0_mix_bproj,
           L0_mix_W1, L0_mix_b1, L0_mix_W2, L0_mix_b2, L0_mix_g1, L0_mix_be1, L0_mix_g2, L0_mix_be2,
           L0_ffn_W1, L0_ffn_b1, L0_ffn_W2, L0_ffn_b2):
    import numpy as np
    import concourse.bacc as bacc
    from concourse.bass_utils import run_bass_kernel_spmd

    def cols(a):
        return np.asarray(a).reshape(-1, P).T
    given = {"x": x, "src": src, "dst": dst, "ew": edge_weight, "wgT": np.asarray(L0_gnn_weight).T,
             "wqkv": L0_mix_Wqkv, "bqkv": L0_mix_bqkv, "pmat": L0_mix_Pmat, "wproj": L0_mix_Wproj,
             "bproj": L0_mix_bproj, "w1": L0_mix_W1, "b1": cols(L0_mix_b1), "w2": L0_mix_W2, "b2": L0_mix_b2,
             "g1": cols(L0_mix_g1), "be1": cols(L0_mix_be1), "g2": cols(L0_mix_g2), "be2": cols(L0_mix_be2),
             "f1T": np.asarray(L0_ffn_W1).T, "fb1": cols(L0_ffn_b1), "f2T": np.asarray(L0_ffn_W2).T, "fb2": L0_ffn_b2,
             "bqkv_c": cols(L0_mix_bqkv)}
    nc = bacc.Bacc("TRN2", target_bir_lowering=False, num_devices=1)
    arrays, aps = {}, {}
    for name, a in given.items():
        a = np.ascontiguousarray(a)
        arrays["in_" + name] = a
        aps[name] = nc.dram_tensor("in_" + name, a.shape, mybir.dt.from_np(a.dtype), kind="ExternalInput").ap()
    out = nc.dram_tensor("out", (N, D), F32, kind="ExternalOutput").ap()
    build(nc, *aps.values(), out)
    r = run_bass_kernel_spmd(nc, [arrays], core_ids=[0])
    return r.results[0]["out"]
```
